# Optimizing a Trainium2 kernel written in Bass

```python
import numpy as np
import jax
import jax.numpy as jnp

def _softmax(x, axis=-1):
    return jax.nn.softmax(x, axis=axis)

def _gelu(x):
    return jax.nn.gelu(x, approximate=True)

def _silu(x):
    return jax.nn.silu(x)

def _sigmoid(x):
    return jax.nn.sigmoid(x)

def _layernorm(x, axis=-1, eps=1e-05):
    m = jnp.mean(x, axis=axis, keepdims=True)
    v = jnp.var(x, axis=axis, keepdims=True)
    return (x - m) / jnp.sqrt(v + eps)

def _scatter_add(tgt, idx, src, axis=0):
    return tgt.at[idx].add(src)

def _segment_sum(src, seg, n):
    return jax.ops.segment_sum(src, seg, n)
kernel_name = 'mk_gnn_ffn_d1_gnn_r8_0e7ee8'

def setup_inputs(seed: int=0):
    np.random.seed(seed)
    _w = jnp.asarray

    def _rec_inputs():
        import jax
        import jax.numpy as jnp
        _gk = jax.random.key(seed)
        x = -0.0003713 + 1 * jax.random.normal(jax.random.fold_in(_gk, 1), (6250, 256), jnp.float32)
        src = jax.random.randint(jax.random.fold_in(_gk, 2), (100000,), 0, 6250, jnp.int32)
        dst = jax.random.randint(jax.random.fold_in(_gk, 3), (100000,), 0, 6250, jnp.int32)
        _o = jnp.argsort(dst, stable=True)
        src = src[_o]
        dst = dst[_o]
        return (x, src, dst)
    x, src, dst = _rec_inputs()

    def _L0_gnn_setup():
        import jax, jax.numpy as jnp
        import numpy as np
        N_NODES = 6250
        N_EDGES = 100000
        IN_DIM = 256
        HEADS = 4
        HEAD_DIM = 64
        NEG_SLOPE = 0.2
        key = jax.random.key(seed)
        k1, k2, k3, k4, k5 = jax.random.split(key, 5)
        x = jax.random.normal(k1, (N_NODES, IN_DIM), dtype=jnp.float32)
        edge_index = jax.random.randint(k2, (2, N_EDGES), 0, N_NODES, dtype=jnp.int64)
        W = jax.random.normal(k3, (IN_DIM, HEADS * HEAD_DIM), dtype=jnp.float32) * (1.0 / np.sqrt(IN_DIM))
        att_src = jax.random.normal(k4, (HEADS, HEAD_DIM), dtype=jnp.float32) * (1.0 / np.sqrt(HEAD_DIM))
        att_dst = jax.random.normal(k5, (HEADS, HEAD_DIM), dtype=jnp.float32) * (1.0 / np.sqrt(HEAD_DIM))
        bias = jnp.zeros((HEADS * HEAD_DIM,), dtype=jnp.float32)
        return {'x': x, 'edge_index': edge_index, 'W': W, 'att_src': att_src, 'att_dst': att_dst, 'bias': bias}
    _L0_gnn_all = _L0_gnn_setup()
    _L0_gnn_in = {k: v for k, v in _L0_gnn_all.items() if k in ('W', 'att_src', 'att_dst', 'bias')}
    del _L0_gnn_all

    def _L0_ffn_setup():
        import jax, jax.numpy as jnp
        import numpy as np
        TOP_K = 2
        LN_EPS = 1e-05
        key = jax.random.key(seed)
        ks = jax.random.split(key, 8)
        B, S, D, E, H = (16, 1024, 256, 8, 1024)
        x = jax.random.normal(ks[0], (B, S, D), dtype=jnp.float32)
        Wr = jax.random.normal(ks[1], (D, E), dtype=jnp.float32) * 0.1
        br = jnp.zeros((E,), dtype=jnp.float32)
        ln_g = jnp.ones((E, D), dtype=jnp.float32)
        ln_b = jnp.zeros((E, D), dtype=jnp.float32)
        W1 = jax.random.normal(ks[2], (E, D, H), dtype=jnp.float32) * (1.0 / np.sqrt(D))
        b1 = jnp.zeros((E, H), dtype=jnp.float32)
        W2 = jax.random.normal(ks[3], (E, H, D), dtype=jnp.float32) * (1.0 / np.sqrt(H))
        b2 = jnp.zeros((E, D), dtype=jnp.float32)
        return {'x': x, 'Wr': Wr, 'br': br, 'ln_g': ln_g, 'ln_b': ln_b, 'W1': W1, 'b1': b1, 'W2': W2, 'b2': b2}
    _L0_ffn_all = _L0_ffn_setup()
    _L0_ffn_in = {k: v for k, v in _L0_ffn_all.items() if k in ('Wr', 'br', 'ln_g', 'ln_b', 'W1', 'b1', 'W2', 'b2')}
    del _L0_ffn_all
    return {'x': x, 'src': src, 'dst': dst, 'L0_gnn_W': _L0_gnn_in['W'], 'L0_gnn_att_src': _L0_gnn_in['att_src'], 'L0_gnn_att_dst': _L0_gnn_in['att_dst'], 'L0_gnn_bias': _L0_gnn_in['bias'], 'L0_ffn_Wr': _L0_ffn_in['Wr'], 'L0_ffn_br': _L0_ffn_in['br'], 'L0_ffn_ln_g': _L0_ffn_in['ln_g'], 'L0_ffn_ln_b': _L0_ffn_in['ln_b'], 'L0_ffn_W1': _L0_ffn_in['W1'], 'L0_ffn_b1': _L0_ffn_in['b1'], 'L0_ffn_W2': _L0_ffn_in['W2'], 'L0_ffn_b2': _L0_ffn_in['b2']}

def reference(x, src, dst, L0_gnn_W, L0_gnn_att_src, L0_gnn_att_dst, L0_gnn_bias, L0_ffn_Wr, L0_ffn_br, L0_ffn_ln_g, L0_ffn_ln_b, L0_ffn_W1, L0_ffn_b1, L0_ffn_W2, L0_ffn_b2):
    import jax
    import jax.numpy as jnp

    def _L0_gnn_ref(x, edge_index, W, att_src, att_dst, bias):
        import jax, jax.numpy as jnp
        import numpy as np
        N_NODES = 6250
        N_EDGES = 100000
        IN_DIM = 256
        HEADS = 4
        HEAD_DIM = 64
        NEG_SLOPE = 0.2
        N = x.shape[0]
        loops = jnp.arange(N, dtype=edge_index.dtype)
        src = jnp.concatenate([edge_index[0], loops])
        dst = jnp.concatenate([edge_index[1], loops])
        h = (x @ W).reshape(N, HEADS, HEAD_DIM)
        a_src = jnp.einsum('nhd,hd->nh', h, att_src)
        a_dst = jnp.einsum('nhd,hd->nh', h, att_dst)
        e = a_src[src] + a_dst[dst]
        e = jax.nn.leaky_relu(e, NEG_SLOPE)
        m = jax.ops.segment_max(e, dst, num_segments=N)
        e = jnp.exp(e - m[dst])
        denom = jax.ops.segment_sum(e, dst, num_segments=N)
        alpha = e / denom[dst]
        msg = alpha[:, :, None] * h[src]
        out = jax.ops.segment_sum(msg, dst, num_segments=N)
        return out.reshape(N, HEADS * HEAD_DIM) + bias

    def _L0_ffn_ref(x, Wr, br, ln_g, ln_b, W1, b1, W2, b2):
        import jax, jax.numpy as jnp
        import numpy as np
        TOP_K = 2
        LN_EPS = 1e-05
        B, S, D = x.shape
        N = B * S
        xt = x.reshape(N, D)
        logits = xt @ Wr + br
        probs = jax.nn.softmax(logits, axis=-1)
        top_p, top_idx = jax.lax.top_k(probs, TOP_K)
        weights = top_p / top_p.sum(axis=-1, keepdims=True)
        mu = xt.mean(axis=-1, keepdims=True)
        var = ((xt - mu) ** 2).mean(axis=-1, keepdims=True)
        xn = (xt - mu) * jax.lax.rsqrt(var + LN_EPS)
        xe = xn[None, :, :] * ln_g[:, None, :] + ln_b[:, None, :]
        h = jax.nn.gelu(jnp.einsum('end,edh->enh', xe, W1) + b1[:, None, :], approximate=False)
        y = jnp.einsum('enh,ehd->end', h, W2) + b2[:, None, :]
        y_tok = jnp.transpose(y, (1, 0, 2))
        sel = jnp.take_along_axis(y_tok, top_idx[:, :, None], axis=1)
        out = (weights[:, :, None] * sel).sum(axis=1)
        return out.reshape(B, S, D)
    edge_index = jnp.stack([src, dst])
    x = x + _L0_gnn_ref(_layernorm(x, axis=-1), edge_index, L0_gnn_W, L0_gnn_att_src, L0_gnn_att_dst, L0_gnn_bias)
    x = x + _L0_ffn_ref(_layernorm(x, axis=-1)[None], L0_ffn_Wr, L0_ffn_br, L0_ffn_ln_g, L0_ffn_ln_b, L0_ffn_W1, L0_ffn_b1, L0_ffn_W2, L0_ffn_b2)[0]
    return x

_drawn_inputs = setup_inputs


def setup_inputs(seed=0):
    import zlib

    import numpy as np

    out = dict(_drawn_inputs(seed))
    spreads = {'L0_gnn_bias': (0.0, 0.1),
     'L0_ffn_br': (0.0, 0.1),
     'L0_ffn_ln_g': (1.0, 0.2),
     'L0_ffn_ln_b': (0.0, 0.1),
     'L0_ffn_b1': (0.0, 0.1),
     'L0_ffn_b2': (0.0, 0.1)}
    factors = {}
    for name, (base, spread) in spreads.items():
        noise = np.random.default_rng([zlib.crc32(name.encode()), seed]).standard_normal(out[name].shape)
        drawn = base * np.exp(spread * noise) if base else spread * noise
        out[name] = jnp.asarray(drawn.astype(out[name].dtype))
    for name, factor in factors.items():
        out[name] = (out[name] * factor).astype(out[name].dtype)
    return out
```

```python
from contextlib import ExitStack

import concourse.bass as bass
from concourse import mybir

F32 = mybir.dt.float32
I32 = mybir.dt.int32
U32 = mybir.dt.uint32
BF16 = mybir.dt.bfloat16
ALU = mybir.AluOpType
ACT = mybir.ActivationFunctionType
X = mybir.AxisListType.X

P = 128
EPS = 1e-5
SLOPE = 0.2
BIG = 1e30
T = 4
STEP = T * P
HS = 4
RING = 3
TOK = 256


def gat_moe(nc, x, src, dst, gW, att_src, att_dst, gbias, Wr, br, ln_g, ln_b, W1, b1, W2, b2, out):
    N, D = x.shape
    E = src.shape[0]
    H, HD = att_src.shape
    NE = Wr.shape[1]
    FH = W1.shape[2]
    KD = D // P
    FC = FH // P
    NW = -(-N // P)
    LAST = N - (NW - 1) * P
    ROW = H * (HD + 1)
    steps_bound = (E + NW * (STEP - 1)) // STEP
    NH = -(-steps_bound // (HS * RING)) * RING
    NS = NH * HS
    PAIRS = 2 * N
    SLOTS = (PAIRS + NE * (TOK - 1)) // TOK
    PLACES = SLOTS * TOK
    NCNT = NW + 1
    GW = 6
    NG = (NW - 1) // GW
    assert NG * GW == NW - 1
    EP, EC = 125, E // 125
    assert EP * EC == E and D == KD * P and NS <= 2 * P and SLOTS % 2 == 0 and NW % 2 == 1

    dst_pad = nc.dram_tensor("dst_pad", [1 + E + 2 * STEP], I32, kind="Internal").ap()
    src_pad = nc.dram_tensor("src_pad", [E + 2 * STEP], I32, kind="Internal").ap()
    table = nc.dram_tensor("table", [N, ROW], F32, kind="Internal").ap()
    x1_dram = nc.dram_tensor("x1_dram", [N, D], F32, kind="Internal").ap()
    xs = nc.dram_tensor("xs", [PLACES, D], F32, kind="Internal").ap()
    ys = nc.dram_tensor("ys", [PLACES, D], F32, kind="Internal").ap()
    prm = nc.dram_tensor("prm", [NE, P, FC + 2 * KD], F32, kind="Internal").ap()

    ctx = ExitStack()
    with ctx:
        def allot(stack):
            def sb(name, shape, dt=F32):
                return stack.enter_context(nc.sbuf_tensor(name, shape, dt))

            def ps(name, shape, dt=F32):
                return stack.enter_context(nc.psum_tensor(name, shape, dt))

            def sem(name):
                return stack.enter_context(nc.semaphore(name))

            return sb, ps, sem

        sb, _, _ = allot(ctx)
        ident = sb("ident", [P, P])
        ident16 = sb("ident16", [P, P], BF16)
        ones = sb("ones", [P, P])
        iota_row = sb("iota_row", [P, P])
        iota_col = sb("iota_col", [P, 1])
        before = sb("before", [P, P])
        wbase = sb("wbase", [P, 2 * P])
        win_i = sb("win_i", [1, 2 * P], I32)
        off_i = sb("off_i", [1, 2 * P], I32)
        edge_cnt = sb("edge_cnt", [P, NCNT])
        big = sb("big", [P, NW * D])
        acc = sb("acc", [P, NW + 1, ROW])
        dm = sb("dm", [P, NW + 1, 2 * H])
        slot_e = sb("slot_e", [1, SLOTS], I32)
        pos = [sb(f"pos{k}", [P, NW], U32) for k in range(2)]
        wt = [sb(f"wt{k}", [P, NW]) for k in range(2)]
        eps_col = sb("eps_col", [P, 1])
        tick = sb("tick", [P, 1])

        node_rows = big[:, :].rearrange("p (w d) -> p w d", d=D)

        def chain(eng, s, base=0):
            count = [0]

            def link(ins):
                count[0] += 1
                ins.then_inc(s, 1)
                eng.wait_ge(s, base + count[0])

            link.count = count
            return link

        def moments(link, mean, var, stats, tmp):
            nc.vector.tensor_tensor(mean, stats[:, :, 1], stats[:, :, 4], ALU.add)
            nc.vector.tensor_tensor(tmp[:, 0, :], stats[:, :, 1], stats[:, :, 4], ALU.subtract)
            link(nc.vector.tensor_tensor(var, stats[:, :, 2], stats[:, :, 5], ALU.add))
            link(nc.vector.tensor_scalar(mean, mean, 0.5, None, ALU.mult))
            link(nc.vector.scalar_tensor_tensor(tmp[:, 1, :], tmp[:, 0, :], 0.25, tmp[:, 0, :], ALU.mult, ALU.mult))
            return nc.vector.scalar_tensor_tensor(var, var, 1.0 / D, tmp[:, 1, :], ALU.mult, ALU.add)

        def copied(out_ap, in_ap):
            return nc.vector.tensor_scalar(out_ap, in_ap, 1.0, None, ALU.mult)

        def load_nodes(sp, loaded):
            for g in range(NG):
                sp.dma_start(node_rows[:, g * GW:(g + 1) * GW, :],
                             x[g * GW * P:(g + 1) * GW * P, :].rearrange("(w p) d -> p w d", p=P)).then_inc(loaded[g], 16)
            sp.dma_start(node_rows[0:LAST, NW - 1, :], x[(NW - 1) * P:N, :]).then_inc(loaded[NG], 16)

        with ExitStack() as st:
            sb, ps, sem = allot(st)
            pad = sb("pad", [1, 2 * STEP], I32)
            zpad = sb("zpad", [1, 2 * STEP], I32)
            dst_i = sb("dst_i", [P, EC], I32)
            dst_f = sb("dst_f", [P, EC])
            junk = sb("junk", [P, EC])
            bound = sb("bound", [P, NCNT])
            zeros = sb("zeros", [P, 2048])
            pt = sb("pt", [P, NE, FC + 2 * KD])
            consts_made = sem("consts_made")
            tiles_set = sem("tiles_set")
            dst_set = sem("dst_set")
            dst_loaded = sem("dst_loaded")
            ident_made = sem("ident_made")
            counted = sem("counted")
            prm_loaded = sem("prm_loaded")
            stores = sem("stores")
            loads = sem("loads")
            ZR = PLACES // P

            block = st.enter_context(nc.Block())

            @block.gpsimd
            def _(pool):
                nc.gpsimd.iota(iota_row[:, :], [[1, P]], base=0, channel_multiplier=0,
                               allow_small_or_imprecise_dtypes=True)
                nc.gpsimd.iota(iota_col[:, :], [[0, 1]], base=0, channel_multiplier=1,
                               allow_small_or_imprecise_dtypes=True)
                nc.gpsimd.iota(bound[:, :], [[P, NCNT]], base=0, channel_multiplier=0,
                               allow_small_or_imprecise_dtypes=True)
                nc.gpsimd.memset(ident[:, :], 0.0)
                nc.gpsimd.memset(ones[:, :], 1.0).then_inc(consts_made, 1)
                pool.wait_ge(consts_made, 1)
                nc.gpsimd.affine_select(out=ident[:, :], in_=ident[:, :], compare_op=ALU.not_equal, fill=1.0,
                                        base=0, pattern=[[-1, P]], channel_multiplier=1).then_inc(ident_made, 1)
                nc.gpsimd.affine_select(out=before[:, :], in_=ones[:, :], compare_op=ALU.is_gt, fill=0.0,
                                        base=0, pattern=[[1, P]], channel_multiplier=-1).then_inc(ident_made, 1)

            @block.vector
            def _(dve):
                link = chain(dve, counted)
                nc.vector.memset(dst_i[:, :], N + P)
                nc.vector.memset(pad[:, :], 2 * N).then_inc(dst_set, 1)
                nc.vector.memset(zpad[:, :], 0)
                nc.vector.memset(zeros[:, :], 0.0)
                nc.vector.memset(eps_col[:, :], EPS)
                nc.vector.memset(edge_cnt[:, :], 0.0).then_inc(tiles_set, 1)
                dve.wait_ge(ident_made, 1)
                nc.vector.tensor_copy(ident16[:, :], ident[:, :])
                dve.wait_ge(dst_loaded, 16)
                link(nc.vector.tensor_copy(dst_f[:, :], dst_i[:, :]))
                with dve.Fori(1, NCNT) as w:
                    nc.vector.tensor_scalar(junk[:, :], dst_f[:, :], bound[:, bass.ds(w, 1)], 0.0, ALU.is_lt, ALU.add,
                                            accum_out=edge_cnt[:, bass.ds(w, 1)]).then_inc(counted, 1)
                    dve.wait_ge(counted, w + 1)

            @block.sync
            def _(sp):
                sp.wait_ge(dst_set, 1)
                sp.dma_start(dst_i[0:EP, :], dst.rearrange("(p c) -> p c", p=EP)).then_inc(dst_loaded, 16)
                sp.dma_start(dst_pad[1:1 + E].rearrange("(a b) -> a b", a=EP), dst.rearrange("(a b) -> a b", a=EP)).then_inc(stores, 16)
                sp.dma_start(src_pad[0:E].rearrange("(a b) -> a b", a=EP), src.rearrange("(a b) -> a b", a=EP)).then_inc(stores, 16)
                sp.wait_ge(tiles_set, 1)
                sp.dma_start(dst_pad[0:1].rearrange("(a b) -> a b", a=1), pad[:, 0:1]).then_inc(stores, 16)
                sp.dma_start(dst_pad[1 + E:].rearrange("(a b) -> a b", a=1), pad[:, :]).then_inc(stores, 16)
                sp.dma_start(src_pad[E:].rearrange("(a b) -> a b", a=1), zpad[:, :]).then_inc(stores, 16)
                n = 5
                flat = xs.rearrange("(p r) d -> p (r d)", p=P)
                for c in range(0, ZR * D, 2048):
                    k = min(2048, ZR * D - c)
                    sp.dma_start(flat[:, c:c + k], zeros[:, 0:k]).then_inc(stores, 16)
                    n += 1
                sp.wait_ge(stores, 16 * n)

            @block.scalar
            def _(act):
                for e in range(NE):
                    act.dma_start(pt[:, e, 0:FC], b1[e].rearrange("(c p) -> p c", p=P),
                                  allow_slow_non_contiguous=True).then_inc(prm_loaded, 16)
                    act.dma_start(pt[:, e, FC:FC + KD], ln_g[e].rearrange("(k p) -> p k", p=P),
                                  allow_slow_non_contiguous=True).then_inc(prm_loaded, 16)
                    act.dma_start(pt[:, e, FC + KD:], ln_b[e].rearrange("(k p) -> p k", p=P),
                                  allow_slow_non_contiguous=True).then_inc(prm_loaded, 16)
                act.wait_ge(prm_loaded, 16 * 3 * NE)
                act.dma_start(prm.rearrange("e p c -> p e c"), pt[:, :, :]).then_inc(loads, 16)
                act.wait_ge(loads, 16)

        with ExitStack() as st:
            sb, ps, sem = allot(st)
            start_ps = ps("start_ps", [P, NCNT])
            row_ps = ps("row_ps", [P, 4, P])
            start = sb("start", [P, NCNT])
            first = sb("first", [P, NCNT])
            cnt = sb("cnt", [P, NW])
            cnt_i = sb("cnt_i", [P, NW], I32)
            zero = sb("zero", [P, NW])
            q = sb("q", [P, NCNT])
            dq = sb("dq", [P, NCNT])
            passed = sb("passed", [P, 2, NCNT])
            part = sb("part", [P, 2, NCNT])
            stepno = sb("stepno", [P, 2])
            val = sb("val", [P, 4])
            spread = sb("spread", [P, 4, P])
            summed = sem("summed")
            spread_done = sem("spread_done")
            rows_done = sem("rows_done")
            dve_seq = sem("sched_seq")
            block = st.enter_context(nc.Block())

            @block.tensor
            def _(pe):
                nc.tensor.matmul(start_ps[:, :], ones[:, :], edge_cnt[:, :], start=True, stop=True).then_inc(summed, 1)
                pe.wait_ge(spread_done, 1)
                for v in range(4):
                    last = nc.tensor.matmul(row_ps[:, v, :], spread[:, v, :], ident[:, :], start=True, stop=True)
                last.then_inc(rows_done, 1)

            @block.vector
            def _(dve):
                link = chain(dve, dve_seq)
                nc.vector.memset(zero[:, :], 0.0)
                nc.vector.memset(first[:, :], 0.0)
                nc.vector.memset(dq[:, :], 0.0)
                nc.vector.tensor_copy(stepno[:, 0:1], iota_col[:, :])
                link(nc.vector.tensor_scalar(stepno[:, 1:2], iota_col[:, :], float(P), None, ALU.add))
                dve.wait_ge(summed, 1)
                link(nc.vector.tensor_copy(start[:, :], start_ps[:, :]))
                link(nc.vector.tensor_tensor(cnt[:, :], start[:, 1:], start[:, 0:NW], ALU.subtract))
                link(nc.vector.tensor_scalar(cnt_i[:, :], cnt[:, :], float(STEP - 1), None, ALU.add))
                link(nc.vector.tensor_scalar(cnt_i[:, :], cnt_i[:, :], STEP.bit_length() - 1, None, ALU.arith_shift_right))
                link(nc.vector.tensor_copy(cnt[:, :], cnt_i[:, :]))
                link(nc.vector.tensor_tensor_scan(first[:, 1:], cnt[:, :], zero[:, :], 0.0, ALU.add, ALU.add))
                link(nc.vector.scalar_tensor_tensor(q[:, :], first[:, :], -float(STEP), start[:, :], ALU.mult, ALU.add))
                link(nc.vector.tensor_tensor(dq[:, 1:], q[:, 1:], q[:, 0:NW], ALU.subtract))
                for j in range(2):
                    last = nc.vector.tensor_scalar(passed[:, j, :], first[:, :], stepno[:, j:j + 1], None, ALU.is_le)
                link(last)
                for j in range(2):
                    last = nc.vector.tensor_tensor(part[:, j, :], passed[:, j, :], dq[:, :], ALU.mult)
                link(last)
                nc.vector.tensor_reduce(val[:, 0:2], passed[:, :, :], X, ALU.add)
                link(nc.vector.tensor_reduce(val[:, 2:4], part[:, :, :], X, ALU.add))
                link(nc.vector.scalar_tensor_tensor(val[:, 2:4], stepno[:, :], float(STEP), val[:, 2:4], ALU.mult, ALU.add))
                nc.vector.tensor_scalar(val[:, 0:2], val[:, 0:2], -1.0, None, ALU.add)
                link(nc.vector.tensor_scalar(val[:, 2:4], val[:, 2:4], float(E), None, ALU.min))
                for v in range(4):
                    last = nc.vector.tensor_scalar(spread[:, v, :], ones[:, :], val[:, v:v + 1], None, ALU.mult)
                last.then_inc(spread_done, 1)
                dve.wait_ge(rows_done, 1)
                nc.vector.tensor_scalar(wbase[:, :], row_ps[:, 0:2, :].rearrange("p a b -> p (a b)"), float(P), None, ALU.mult)
                nc.vector.tensor_copy(win_i[:, :], row_ps[0:1, 0:2, :].rearrange("p a b -> p (a b)"))
                nc.vector.tensor_copy(off_i[:, :], row_ps[0:1, 2:4, :].rearrange("p a b -> p (a b)"))

        with ExitStack() as st:
            sb, ps, sem = allot(st)
            WX = ROW + H
            wx = sb("wx", [P, KD, WX])
            w_sb = sb("w_sb", [P, KD, D])
            attb = sb("attb", [P, 2, D])
            prod = sb("prod", [P, 2, KD, D])
            attw = sb("attw", [P, 2, KD, H])
            stat = sb("stat", [P, NW, 6])
            mv = sb("mv", [P, NW, 2])
            rstd = sb("rstd", [P, NW])
            mtmp = sb("mtmp", [P, 2, NW])
            xn_st = sb("xn_st", [P, 2, D])
            xT = sb("xT", [P, 2, D])
            hx = sb("hx", [P, 2, WX])
            xT_ps = ps("xT_ps", [P, 2, 512])
            h_ps = ps("h_ps", [P, 2, 512])
            w_loaded = sem("w_loaded")
            x_loaded = [sem(f"x_loaded{g}") for g in range(NG + 1)]
            pad_zeroed = sem("pad_zeroed")
            acc_one = sem("acc_one")
            wx_ready = sem("wx_ready")
            var_ready = sem("var_ready")
            std_ready = sem("std_ready")
            dve_seq = sem("proj_seq")
            xn_ready = sem("xn_ready")
            xT_made = sem("xT_made")
            xT_copied = sem("xT_copied")
            h_made = sem("h_made")
            h_copied = sem("h_copied")
            dm_done = sem("dm_done")
            acc_set = sem("acc_set")
            table_stored = [sem(f"table_stored{b}") for b in range(2)]
            block = st.enter_context(nc.Block())

            @block.sync
            def _(sp):
                sp.dma_start(w_sb[:, :, :], gW.rearrange("(k p) n -> p k n", p=P)).then_inc(w_loaded, 16)
                sp.dma_start(attb[:, 0, :], att_src.rearrange("h c -> (h c)").partition_broadcast(P)).then_inc(w_loaded, 16)
                sp.dma_start(attb[:, 1, :], att_dst.rearrange("h c -> (h c)").partition_broadcast(P)).then_inc(w_loaded, 16)
                sp.wait_ge(pad_zeroed, 1)
                load_nodes(sp, x_loaded)

                def store_rows(w, b, rows=P):
                    sp.wait_ge(h_copied, w + 1)
                    sp.dma_start(table[bass.ds(w * P, rows), :], hx[0:rows, b, 0:ROW]).then_inc(table_stored[b], 16)

                with sp.Fori(0, NW // 2) as i:
                    for b in range(2):
                        store_rows(2 * i + b, b)
                store_rows(NW - 1, 0, LAST)
                sp.wait_ge(table_stored[0], 16 * (NW // 2 + 1))
                sp.wait_ge(table_stored[1], 16 * (NW // 2))

            @block.gpsimd
            def _(pool):
                nc.gpsimd.memset(acc[:, :, :], 1.0).then_inc(acc_one, 1)
                pool.wait_ge(acc_one, 1)

                def start_acc(w, b):
                    pool.wait_ge(h_copied, w + 1)
                    nc.gpsimd.tensor_copy(acc[:, bass.ds(w, 1), :].rearrange("p o (h c) -> p (o h) c", h=H)[:, :, 0:HD],
                                          hx[:, b, 0:ROW].rearrange("p (h c) -> p h c", h=H)[:, :, 0:HD]).then_inc(acc_set, 1)

                with pool.Fori(0, NW // 2) as i:
                    for b in range(2):
                        start_acc(2 * i + b, b)
                start_acc(NW - 1, 0)

            @block.scalar
            def _(act):
                act.wait_ge(var_ready, 1)
                nc.scalar.activation(rstd[:, :], mv[:, :, 1], ACT.Sqrt, bias=eps_col[:, 0:1]).then_inc(std_ready, 1)

                def copy_xT(w, b):
                    act.wait_ge(xT_made, w + 1)
                    nc.scalar.activation(xT[:, b, :], xT_ps[:, b, 0:D], ACT.Copy).then_inc(xT_copied, 1)

                with act.Fori(0, NW // 2) as i:
                    for b in range(2):
                        copy_xT(2 * i + b, b)
                copy_xT(NW - 1, 0)

            @block.tensor
            def _(pe):
                def transpose(w, b):
                    pe.wait_ge(xn_ready, w + 1)
                    for k in range(KD):
                        last = nc.tensor.transpose(xT_ps[:, b, k * P:(k + 1) * P], xn_st[:, b, k * P:(k + 1) * P], ident[:, :])
                    last.then_inc(xT_made, 1)

                def product(w, b, reused=True):
                    pe.wait_ge(xT_copied, w + 1)
                    if reused:
                        pe.wait_ge(h_copied, w - 1)
                    for k in range(KD):
                        last = nc.tensor.matmul(h_ps[:, b, 0:WX], xT[:, b, k * P:(k + 1) * P], wx[:, k, :],
                                                start=(k == 0), stop=(k == KD - 1))
                    last.then_inc(h_made, 1)

                pe.wait_ge(wx_ready, 1)
                transpose(0, 0)
                transpose(1, 1)
                product(0, 0, reused=False)
                transpose(2, 0)
                product(1, 1, reused=False)
                with pe.Fori(1, NW // 2) as i:
                    for b in range(2):
                        transpose(2 * i + b + 1, 1 - b)
                        product(2 * i + b, b)
                product(NW - 1, 0)

            @block.vector
            def _(dve):
                link = chain(dve, dve_seq)
                nc.vector.memset(node_rows[:, NW - 1, :], 0.0)
                nc.vector.memset(dm[:, :, :], 0.0).then_inc(pad_zeroed, 1)
                dve.wait_ge(w_loaded, 48)
                for v in range(2):
                    for k in range(KD):
                        last = nc.vector.tensor_tensor(prod[:, v, k, :], w_sb[:, k, :], attb[:, v, :], ALU.mult)
                link(last)
                for v in range(2):
                    last = nc.vector.tensor_reduce(attw[:, v, :, :].rearrange("p k h -> p (k h)"),
                                                   prod[:, v, :, :].rearrange("p k (h c) -> p (k h) c", h=H), X, ALU.add)
                link(last)
                for k in range(KD):
                    rows = wx[:, k, 0:ROW].rearrange("p (h c) -> p h c", h=H)
                    nc.vector.tensor_copy(rows[:, :, 0:HD], w_sb[:, k, :].rearrange("p (h c) -> p h c", h=H))
                    nc.vector.tensor_copy(rows[:, :, HD], attw[:, 0, k, :])
                    last = nc.vector.tensor_copy(wx[:, k, ROW:], attw[:, 1, k, :])
                last.then_inc(wx_ready, 1)

                for g in range(NG + 1):
                    dve.wait_ge(x_loaded[g], 16)
                    with dve.Fori(g * GW, min((g + 1) * GW, NW)) as w:
                        nc.vector.bn_stats(stat[:, bass.ds(w, 1), :].rearrange("p o c -> p (o c)"),
                                           node_rows[:, bass.ds(w, 1), :].rearrange("p o c -> p (o c)"))
                link(nc.vector.memset(tick[:, :], 0.0))
                moments(link, mv[:, :, 0], mv[:, :, 1], stat, mtmp).then_inc(var_ready, 1)
                dve.wait_ge(std_ready, 1)
                link(nc.vector.reciprocal(rstd[:, :], rstd[:, :]))

                def normalise(w, b, reused=True):
                    if reused:
                        dve.wait_ge(xT_made, w - 1)
                    nc.vector.tensor_scalar(xn_st[:, b, :], node_rows[:, bass.ds(w, 1), :].rearrange("p o c -> p (o c)"),
                                            mv[:, bass.ds(w, 1), 0], rstd[:, bass.ds(w, 1)],
                                            ALU.subtract, ALU.mult).then_inc(xn_ready, 1)

                def take_h(w, b, use=None):
                    dve.wait_ge(h_made, w + 1)
                    if use is not None:
                        dve.wait_ge(table_stored[b], 16 * use)
                        dve.wait_ge(acc_set, w - 1)
                    nc.vector.tensor_copy(hx[:, b, :], h_ps[:, b, 0:WX]).then_inc(h_copied, 1)
                    dve.wait_ge(h_copied, w + 1)
                    d_row = dm[:, bass.ds(w, 1), :].rearrange("p o c -> p (o c)")
                    copied(d_row[:, 0:H], hx[:, b, ROW:])
                    nc.vector.tensor_tensor(d_row[:, H:], hx[:, b, ROW:],
                                            hx[:, b, 0:ROW].rearrange("p (h c) -> p h c", h=H)[:, :, HD], ALU.add)

                normalise(0, 0, reused=False)
                normalise(1, 1, reused=False)
                normalise(2, 0)
                take_h(0, 0)
                normalise(3, 1)
                take_h(1, 1)
                with dve.Fori(1, NW // 2 - 1) as i:
                    for b in range(2):
                        normalise(2 * i + b + 2, b)
                        take_h(2 * i + b, b, use=i)
                w = NW - 3
                normalise(w + 2, 0)
                take_h(w, 0, use=w // 2)
                take_h(w + 1, 1, use=w // 2)
                take_h(w + 2, 0, use=w // 2 + 1)
                link(nc.vector.memset(tick[:, :], 0.0))
                link(nc.vector.scalar_tensor_tensor(dm[:, :, H:], dm[:, :, H:], SLOPE, dm[:, :, H:], ALU.mult, ALU.max))

        with ExitStack() as st:
            sb, ps, sem = allot(st)
            HB = HS * H
            HT = HS * T
            D8 = 2 * H
            LINKS = 17
            NB = NH // RING
            gat = big[:, 0:RING * HT * ROW].rearrange("p (r j t h c) -> p r j t h c", r=RING, j=HS, t=T, h=H)
            gat_rows = big[:, 0:RING * HT * ROW].rearrange("p (n c) -> p n c", c=ROW)
            src_t = sb("src_t", [P, RING, HS, T], I32)
            dst_t = sb("dst_t", [P, 3, RING, HS, T], I32)
            dloc = sb("dloc", [P, RING, HS, T])
            begins = sb("begins", [P, HS, T])
            ends = sb("ends", [P, RING, HS, T])
            last_edge = sb("last_edge", [P, HS, T])
            last_col = sb("last_col", [P, 1])
            resets = sb("resets", [P, T, HS, H])
            onehot = sb("onehot", [P, RING, HS, T, P])
            onehot16 = sb("onehot16", [P, HS, T, P], BF16)
            iota16 = sb("iota16", [P, P], BF16)
            onehotT = sb("onehotT", [P, HS, T * P], BF16)
            a_s = sb("a_s", [P, RING, T, HS, H])
            resT = sb("resT", [HB, T * P])
            runmax = sb("runmax", [HB, T * P])
            seg = sb("seg", [P, HS, T, H])
            seg_r = sb("seg_r", [P, HS, T, H])
            seg16 = sb("seg16", [P, HS, T, 3, H + 1], BF16)
            absent = sb("absent", [P, HS])
            cand = sb("cand", [P, HS, H])
            cand2 = sb("cand2", [P, HS, H])
            known = sb("known", [P, HS, D8])
            cur = sb("cur", [P, HS, D8])
            best = sb("best", [P, H, HS])
            highest = sb("highest", [P, H, HS])
            old = sb("old", [P, H, HS])
            wreset = sb("wreset", [P, NS])
            reset_j = sb("reset_j", [P, H, HS])
            cur_r = sb("cur_r", [P, HS, D8])
            cur16 = sb("cur16", [P, HS, 3, D8], BF16)
            shrink_x = sb("shrink_x", [P, H, HS])
            shrink = sb("shrink", [P, RING, HS, H])
            score = sb("score", [P, HS, T, H])
            score2 = sb("score2", [P, HS, T, H])
            wgt = sb("wgt", [P, RING, HS, T, H])
            wrow = sb("wrow", [P, HS, T, H, HD + 1])
            asT_ps = ps("asT_ps", [HB, 512])
            resT_ps = ps("resT_ps", [HB, 512])
            seg_ps = ps("seg_ps", [P, 512])
            ohT_ps = ps("ohT_ps", [P, 2, 1024], BF16)
            edge_ps = ps("edge_ps", [P, 512])
            sum_ps = ps("sum_ps", [P, 2, 512])
            back_ps = seg_ps[:, 0:T * HB]
            win_ps = seg_ps[:, 128:128 + HS * (H + 1)].rearrange("p (j c) -> p j c", j=HS)

            edges_loaded = [sem(f"edges_loaded{r}") for r in range(RING)]
            rows_gathered = [sem(f"rows_gathered{r}") for r in range(RING)]
            seq = sem("attend_seq")
            marks_set = sem("marks_set")
            onehot_made = sem("onehot_made")
            a_s_staged = sem("a_s_staged")
            asT_made = sem("asT_made")
            resT_copied = sem("resT_copied")
            resets_made = sem("resets_made")
            resT_made = sem("resT_made")
            onehot_copied = sem("onehot_copied")
            ohT_made = sem("ohT_made")
            onehotT_copied = sem("onehotT_copied")
            scanned = sem("scanned")
            back_made = sem("back_made")
            seg_made = sem("seg_made")
            win_made = sem("win_made")
            cur_made = sem("cur_made")
            shrink_in = sem("shrink_in")
            shrink_made = sem("shrink_made")
            edge_made = sem("edge_made")
            score_made = sem("score_made")
            weights_made = sem("weights_made")
            rows_weighted = sem("rows_weighted")
            slot_free = sem("slot_free")
            summed = sem("step_summed")
            merged = sem("merged")
            block = st.enter_context(nc.Block())

            @block.sync
            def _(sp):
                def load_half(n, r, reused=True):
                    k = RING * n + r
                    if reused:
                        sp.wait_ge(score_made, k - RING + 1)
                    for j in range(HS):
                        off = sp.value_load(off_i[0:1, bass.ds(HS * k + j, 1)], min_val=0, max_val=E)
                        sp.dma_start(src_t[:, r, j, :], src_pad[bass.ds(off, STEP)].rearrange("(p t) -> p t", t=T)
                                     ).then_inc(edges_loaded[r], 16)
                        for v in range(3):
                            sp.dma_start(dst_t[:, v, r, j, :], dst_pad[bass.ds(off + v, STEP)].rearrange("(p t) -> p t", t=T)
                                         ).then_inc(edges_loaded[r], 16)

                for r in range(RING):
                    load_half(0, r, reused=False)
                with sp.Fori(1, NB) as n:
                    for r in range(RING):
                        load_half(n, r)

            @block.gpsimd
            def _(pool):
                def gather_half(n, r, reused=True):
                    pool.wait_ge(edges_loaded[r], 256 * (n + 1))
                    for j in range(HS):
                        if reused:
                            pool.wait_ge(rows_weighted, HS * (RING * n + r - RING) + j + 1)
                            pool.sem_inc(slot_free, 1)
                        for t in range(T):
                            pool.indirect_dma_start(
                                gat_rows[:, (r * HS + j) * T + t, :], None, table,
                                bass.IndirectOffsetOnAxis(ap=src_t[:, r, j, t:t + 1].bitcast(U32), axis=0),
                            ).then_inc(rows_gathered[r], 16)

                for r in range(RING):
                    gather_half(0, r, reused=False)
                with pool.Fori(1, NB) as n:
                    for r in range(RING):
                        gather_half(n, r)


            def turns(eng, half):
                for r in range(RING):
                    half(r, 0, r)
                with eng.Fori(1, NB - 1) as n:
                    for r in range(RING):
                        half(RING * n + r, n, r)
                for r in range(RING):
                    half(RING * (NB - 1) + r, NB - 1, r)

            @block.scalar
            def _(act):
                def half(k, n, r):
                    started = not (isinstance(k, int) and k == 0)
                    act.wait_ge(resT_made, k + 1)
                    if started:
                        act.wait_ge(scanned, k)
                    nc.scalar.activation(resT[:, :], resT_ps[:, :], ACT.Copy).then_inc(resT_copied, 1)
                    if started:
                        act.wait_ge(edge_made, k)
                    for g in range(2):
                        act.wait_ge(ohT_made, 2 * k + g + 1)
                        nc.scalar.activation(onehotT[:, 2 * g:2 * g + 2, :].rearrange("p j c -> p (j c)"), ohT_ps[:, g, :],
                                             ACT.Copy).then_inc(onehotT_copied, 1)
                    if not isinstance(k, int) or k >= RING:
                        act.wait_ge(summed, HS * (k - RING + 1))
                    nc.scalar.activation(onehot[:, r, :, :, :].rearrange("p j t c -> p (j t c)"),
                                         onehot16[:, :, :, :].rearrange("p j t c -> p (j t c)"),
                                         ACT.Copy).then_inc(onehot_copied, 1)
                    act.wait_ge(shrink_in, k + 1)
                    nc.scalar.activation(shrink[:, r, :, :].rearrange("p j h -> p h j"), shrink_x[:, :, :], ACT.Exp).then_inc(shrink_made, 1)
                    act.wait_ge(score_made, k + 1)
                    nc.scalar.activation(wgt[:, r, :, :, :], score[:, :, :, :], ACT.Exp).then_inc(weights_made, 1)

                turns(act, half)

            @block.tensor
            def _(pe):
                def add_rows(s, j, rr):
                    pe.wait_ge(rows_weighted, s + 1)
                    if not isinstance(s, int) or s >= 2:
                        pe.wait_ge(merged, s - 1)
                    for t in range(T):
                        last = nc.tensor.matmul(sum_ps[:, j % 2, 0:ROW], onehot[:, rr, j, t, :],
                                                wrow[:, j, t, :, :].rearrange("p h c -> p (h c)"),
                                                start=(t == 0), stop=(t == T - 1))
                    last.then_inc(summed, 1)

                def transpose_maxima(k, r):
                    pe.wait_ge(a_s_staged, k + 1)
                    for t in range(T):
                        last = nc.tensor.transpose(asT_ps[:, t:T * P:T], a_s[:, r, t, :, :].rearrange("p j h -> p (j h)"), ident[:, :])
                    last.then_inc(asT_made, 1)
                    pe.wait_ge(resets_made, k + 1)
                    if not (isinstance(k, int) and k == 0):
                        pe.wait_ge(resT_copied, k)
                    for t in range(T):
                        last = nc.tensor.transpose(resT_ps[:, t:T * P:T], resets[:, t, :, :].rearrange("p j h -> p (j h)"),
                                                   ident[:, :])
                    last.then_inc(resT_made, 1)

                def half(k, n, r):
                    prev = not (isinstance(k, int) and k == 0)
                    rr = (r - 1) % RING
                    s = HS * k - HS
                    pe.wait_ge(onehot_made, k + 1)
                    for g in range(2):
                        for j in (2 * g, 2 * g + 1):
                            for t in range(T):
                                c = (j % 2) * T * P + t * P
                                last = nc.tensor.transpose(ohT_ps[:, g, c:c + P], onehot16[:, j, t, :], ident16[:, :])
                        last.then_inc(ohT_made, 1)
                    pe.wait_ge(asT_made, 1)
                    pe.wait_ge(scanned, k + 1)
                    for t in range(T):
                        last = nc.tensor.transpose(back_ps[:, t * HB:(t + 1) * HB], runmax[:, t:T * P:T], ident[0:HB, 0:HB])
                    last.then_inc(back_made, 1)
                    if prev:
                        pe.wait_ge(onehot_copied, k)
                        add_rows(s, 0, rr)
                    pe.wait_ge(seg_made, k + 1)
                    for j in range(HS):
                        for t in range(T):
                            for v in range(3):
                                last = nc.tensor.matmul(win_ps[:, j, :], onehot16[:, j, t, :], seg16[:, j, t, v, :],
                                                        start=(t == 0 and v == 0), stop=(t == T - 1 and v == 2))
                    last.then_inc(win_made, 1)
                    if prev:
                        add_rows(s + 1, 1, rr)
                    pe.wait_ge(cur_made, k + 1)
                    pe.wait_ge(onehotT_copied, 2 * k + 2)
                    for j in range(HS):
                        for t in range(T):
                            c = (j * T + t) * D8
                            for v in range(3):
                                last = nc.tensor.matmul(edge_ps[:, c:c + D8], onehotT[:, j, t * P:(t + 1) * P],
                                                        cur16[:, j, v, :], start=(v == 0), stop=(v == 2))
                    last.then_inc(edge_made, 1)
                    if prev:
                        add_rows(s + 2, 2, rr)
                    if not (isinstance(k, int) and k == NH - 1):
                        transpose_maxima(k + 1, (r + 1) % RING)
                    if prev:
                        add_rows(s + 3, 3, rr)

                transpose_maxima(0, 0)
                turns(pe, half)
                pe.wait_ge(onehot_copied, NH)
                for j in range(HS):
                    add_rows(HS * (NH - 1) + j, j, (NH - 1) % RING)

            @block.vector
            def _(dve):
                link = chain(dve, marks_set)
                nc.vector.memset(seg16[:, :, :, :, H], 0.0)
                nc.vector.memset(old[:, :, 0], -BIG)
                nc.vector.memset(wreset[:, 0:1], 0.0)
                nc.vector.tensor_copy(iota16[:, :], iota_row[:, :])
                link(nc.vector.tensor_scalar(last_col[:, :], iota_col[:, :], float(P - 1), None, ALU.is_equal))
                link(nc.vector.memset(last_edge[:, :, :], 0.0))
                nc.vector.tensor_copy(last_edge[:, :, T - 1], last_col[:, 0:1].to_broadcast([P, HS]))
                link(nc.vector.tensor_tensor(wreset[:, 1:], wbase[:, 1:NS], wbase[:, 0:NS - 1], ALU.not_equal))
                link(nc.vector.tensor_scalar(wreset[:, :], wreset[:, :], -BIG, None, ALU.mult))
                link(nc.vector.memset(wreset[:, 0:NS:HS], -BIG))

                def edge_marks(k, n, r, link):
                    dve.wait_ge(edges_loaded[r], 256 * (n + 1))
                    base = wbase[:, bass.ds(HS * k, HS)].unsqueeze(2).to_broadcast([P, HS, T])
                    nc.vector.tensor_tensor(dloc[:, r, :, :], dst_t[:, 1, r, :, :], base, ALU.subtract)
                    nc.vector.tensor_tensor(ends[:, r, :, :], dst_t[:, 1, r, :, :], dst_t[:, 2, r, :, :], ALU.not_equal)
                    link(nc.vector.tensor_tensor(begins[:, :, :], dst_t[:, 1, r, :, :], dst_t[:, 0, r, :, :], ALU.not_equal))
                    nc.vector.tensor_scalar(resets[:, :, :, :],
                                            begins[:, :, :].rearrange("p j t -> p t j").unsqueeze(3).to_broadcast([P, T, HS, H]),
                                            -BIG, None, ALU.mult).then_inc(resets_made, 1)
                    nc.vector.tensor_tensor(ends[:, r, :, :], ends[:, r, :, :], last_edge[:, :, :], ALU.max)
                    copied(reset_j[:, :, :], wreset[:, bass.ds(HS * k, HS)].unsqueeze(1).to_broadcast([P, H, HS]))
                    if not (isinstance(k, int) and k == 0):
                        dve.wait_ge(onehot_copied, k)
                    for j in range(HS):
                        for t in range(T):
                            last = nc.vector.tensor_scalar(onehot16[:, j, t, :], iota16[:, :], dloc[:, r, j, t:t + 1],
                                                           None, ALU.is_equal)
                    last.then_inc(onehot_made, 1)

                def stage_and_mark(k, n, r, link):
                    dve.wait_ge(rows_gathered[r], 256 * (n + 1))
                    nc.vector.tensor_copy(a_s[:, r, :, :, :].rearrange("p t j h -> p j t h"),
                                          gat[:, r, :, :, :, HD]).then_inc(a_s_staged, 1)
                    edge_marks(k, n, r, link)

                def weight_rows(s, j, rr):
                    if not isinstance(s, int) or s >= HS:
                        dve.wait_ge(summed, s - HS + 1)
                    w_e = wgt[:, rr, j, :, :]
                    nc.vector.scalar_tensor_tensor(wrow[:, j, :, :, 0:HD], w_e.unsqueeze(3).to_broadcast([P, T, H, HD]), 1.0,
                                                   gat[:, rr, j, :, :, 0:HD], ALU.min, ALU.mult)
                    nc.vector.tensor_scalar(wrow[:, j, :, :, HD], w_e, 1.0, None, ALU.min).then_inc(rows_weighted, 1)

                def merge(s, j, rr, w):
                    dve.wait_ge(summed, s + 1)
                    if not isinstance(s, int) or s >= 1:
                        dve.wait_ge(merged, s)
                    for h in range(H):
                        cols = slice(h * (HD + 1), (h + 1) * (HD + 1))
                        a = acc[:, bass.ds(w, 1), cols].rearrange("p o c -> p (o c)")
                        last = nc.vector.scalar_tensor_tensor(a, a, shrink[:, rr, j, h:h + 1], sum_ps[:, j % 2, cols],
                                                              ALU.mult, ALU.add)
                    last.then_inc(merged, 1)

                win_regs = [[dve.alloc_register(f"win{r}_{j}") for j in range(HS)] for r in range(RING)]

                def windows(r):
                    return [dve.snap(reg, min_val=0, max_val=NW) for reg in win_regs[r]]

                def half(k, n, r, link):
                    prev = not (isinstance(k, int) and k == 0)
                    rr = (r - 1) % RING
                    s = HS * k - HS
                    by_head = "p j h -> p h j"
                    dve.wait_ge(asT_made, k + 1)
                    dve.wait_ge(resT_copied, k + 1)
                    nc.vector.tensor_tensor_scan(runmax[:, :], resT[:, :], asT_ps[:, :], -BIG, ALU.add, ALU.max
                                                 ).then_inc(scanned, 1)
                    if prev:
                        dve.wait_ge(weights_made, k)
                        weight_rows(s, 0, rr)
                    dve.wait_ge(back_made, k + 1)
                    nc.vector.tensor_copy(seg16[:, :, :, 0, H], ends[:, r, :, :])
                    link(nc.vector.tensor_tensor(seg[:, :, :, :], back_ps.rearrange("p (t j h) -> p j t h", t=T, j=HS),
                                                 ends[:, r, :, :].unsqueeze(3).to_broadcast([P, HS, T, H]), ALU.mult))
                    link(nc.vector.tensor_copy(seg16[:, :, :, 0, 0:H], seg[:, :, :, :]))
                    link(nc.vector.tensor_tensor(seg_r[:, :, :, :], seg[:, :, :, :], seg16[:, :, :, 0, 0:H], ALU.subtract))
                    link(nc.vector.tensor_copy(seg16[:, :, :, 1, 0:H], seg_r[:, :, :, :]))
                    nc.vector.tensor_tensor(seg16[:, :, :, 2, 0:H], seg_r[:, :, :, :], seg16[:, :, :, 1, 0:H],
                                            ALU.subtract).then_inc(seg_made, 1)
                    dve.load(win_regs[r], win_i[0:1, bass.ds(HS * k, HS)])
                    mine = windows(r)
                    wins = windows(rr)
                    if prev:
                        weight_rows(s + 1, 1, rr)
                    for j in range(HS):
                        last = copied(known[:, j, :], dm[:, bass.ds(mine[j], 1), :].rearrange("p o c -> p (o c)"))
                    link(last)
                    nc.vector.tensor_copy(cur[:, :, 0:H], known[:, :, 0:H])
                    if prev:
                        dve.wait_ge(shrink_made, k)
                        merge(s, 0, rr, wins[0])
                    dve.wait_ge(win_made, k + 1)
                    nc.vector.tensor_scalar(absent[:, :], win_ps[:, :, H], BIG, -BIG, ALU.mult, ALU.add)
                    link(nc.vector.tensor_tensor(cand[:, :, :], win_ps[:, :, 0:H], known[:, :, 0:H], ALU.add))
                    link(nc.vector.tensor_tensor(cand2[:, :, :], cand[:, :, :],
                                                 absent[:, :].unsqueeze(2).to_broadcast([P, HS, H]), ALU.add))
                    link(nc.vector.scalar_tensor_tensor(cand[:, :, :], cand2[:, :, :], SLOPE, cand2[:, :, :], ALU.mult, ALU.max))
                    link(nc.vector.tensor_tensor(best[:, :, :], cand[:, :, :].rearrange(by_head),
                                                 known[:, :, H:].rearrange(by_head), ALU.max))
                    link(nc.vector.tensor_tensor_scan(highest[:, :, :].rearrange("p h j -> p (h j)"),
                                                      reset_j[:, :, :].rearrange("p h j -> p (h j)"),
                                                      best[:, :, :].rearrange("p h j -> p (h j)"), -BIG, ALU.add, ALU.max))

                    def keep(j):
                        return copied(dm[:, bass.ds(mine[j], 1), H:].rearrange("p o c -> p (o c)"), highest[:, :, j])

                    nc.vector.tensor_copy(cur[:, :, H:].rearrange(by_head), highest[:, :, :])
                    keep(0)
                    link(nc.vector.tensor_tensor(old[:, :, 1:], highest[:, :, 0:HS - 1], reset_j[:, :, 1:], ALU.add))
                    nc.vector.tensor_copy(cur16[:, :, 0, :], cur[:, :, :])
                    keep(1)
                    link(nc.vector.tensor_tensor(best[:, :, :], old[:, :, :], known[:, :, H:].rearrange(by_head), ALU.max))
                    nc.vector.tensor_tensor(shrink_x[:, :, :], best[:, :, :], highest[:, :, :], ALU.subtract).then_inc(shrink_in, 1)
                    keep(2)
                    link(nc.vector.tensor_tensor(cur_r[:, :, :], cur[:, :, :], cur16[:, :, 0, :], ALU.subtract))
                    nc.vector.tensor_copy(cur16[:, :, 1, :], cur_r[:, :, :])
                    link(keep(3))
                    nc.vector.tensor_tensor(cur16[:, :, 2, :], cur_r[:, :, :], cur16[:, :, 1, :], ALU.subtract).then_inc(cur_made, 1)
                    if prev:
                        weight_rows(s + 2, 2, rr)
                        merge(s + 1, 1, rr, wins[1])
                        weight_rows(s + 3, 3, rr)
                    dve.wait_ge(edge_made, k + 1)
                    edge = edge_ps[:, 0:HT * D8].rearrange("p (j t c) -> p j t c", j=HS, t=T)
                    link(nc.vector.tensor_tensor(score[:, :, :, :], edge[:, :, :, 0:H],
                                                 a_s[:, r, :, :, :].rearrange("p t j h -> p j t h"), ALU.add))
                    flat = "p j t h -> p (j t h)"
                    link(nc.vector.scalar_tensor_tensor(score2[:, :, :, :].rearrange(flat), score[:, :, :, :].rearrange(flat), SLOPE,
                                                        score[:, :, :, :].rearrange(flat), ALU.mult, ALU.max))
                    nc.vector.tensor_tensor(score[:, :, :, :], score2[:, :, :, :], edge[:, :, :, H:], ALU.subtract).then_inc(score_made, 1)
                    if not (isinstance(k, int) and k == NH - 1):
                        stage_and_mark(k + 1, n + (r + 1) // RING, (r + 1) % RING, link)
                    if prev:
                        merge(s + 2, 2, rr, wins[2])
                        merge(s + 3, 3, rr, wins[3])

                before_loop = 1 + RING * LINKS
                link = chain(dve, seq)
                stage_and_mark(0, 0, 0, link)
                for r in range(RING):
                    half(r, 0, r, link)
                assert link.count[0] == before_loop, link.count
                with dve.Fori(1, NB - 1) as n:
                    link = chain(dve, seq, base=(n - 1) * (RING * LINKS) + before_loop)
                    for r in range(RING):
                        half(RING * n + r, n, r, link)
                link = chain(dve, seq, base=before_loop + (NB - 2) * RING * LINKS)
                for r in range(RING):
                    half(RING * (NB - 1) + r, NB - 1, r, link)
                wins = windows(RING - 1)
                s, rr = HS * (NH - 1), (NH - 1) % RING
                dve.wait_ge(weights_made, NH)
                dve.wait_ge(shrink_made, NH)
                weight_rows(s, 0, rr)
                weight_rows(s + 1, 1, rr)
                for j in range(HS):
                    merge(s + j, j, rr, wins[j])
                    if j + 2 < HS:
                        weight_rows(s + j + 2, j + 2, rr)

        with ExitStack() as st:
            sb, ps, sem = allot(st)
            xn = sb("xn", [P, NW, D])
            rden = sb("rden", [P, NW, H])
            gb = sb("gb", [P, D])
            brb = sb("brb", [P, NE])
            wr = sb("wr", [P, KD, NE])
            stat = sb("stat2", [P, NW, 6])
            mv = sb("mv2", [P, 2, NW, 2])
            mtmp = sb("mtmp2", [P, 2, NW])
            rstd = sb("rstd2", [P, 2, NW])
            xt_st = sb("xt_st", [P, 2, D])
            xT = sb("xtT", [P, 2, D])
            logit = sb("logit", [P, NW, NE])
            top = sb("top", [P, 2, NW])
            number = sb("number", [P, NE])
            equal = sb("equal", [P, NW, NE])
            rest = sb("rest", [P, NW, NE])
            chosen = sb("chosen", [P, NW])
            diff = sb("diff", [P, NW])
            gate = sb("gate", [P, NW])
            gate_d = sb("gate_d", [P, NW])
            pick = [sb(f"pick{k}", [P, NW, NE]) for k in range(2)]
            real = sb("real", [P, 1])
            both = sb("both", [P, NW, NE])
            total = sb("total", [P, NW, NE])
            upto = sb("upto", [P, NW, NE])
            place = sb("place", [P, NW, NE])
            placed = sb("placed", [P, NW, NE])
            posf = sb("posf", [P, NW])
            zero = sb("zero2", [P, NW])
            need = sb("need", [P, NE])
            need_i = sb("need_i", [P, NE], I32)
            need_c = sb("need_c", [P, NE])
            slot0 = sb("slot0", [P, NE])
            owner = sb("owner", [1, SLOTS, NE])
            owner_s = sb("owner_s", [1, SLOTS])
            xT_ps = ps("xtT_ps", [P, 2, 512])
            lg_ps = ps("lg_ps", [P, 2, 512])
            rank_ps = ps("rank_ps", [P, 512])
            total_ps = ps("total_ps", [P, 512])
            x_loaded = [sem(f"x_again{g}") for g in range(NG + 1)]
            small_loaded = sem("small_loaded")
            pad_zeroed = sem("pad_zeroed2")
            seq = sem("norm_seq")
            added = sem("added")
            biased = sem("biased")
            var_ready = [sem(f"var_ready{v}") for v in range(2)]
            std_ready = [sem(f"std_ready{v}") for v in range(2)]
            xt_ready = sem("xt_ready")
            xT_made = sem("xtT_made")
            xT_copied = sem("xtT_copied")
            lg_made = sem("lg_made")
            lg_taken = sem("lg_taken")
            gate_in = sem("gate_in")
            gate_made = sem("gate_made")
            both_made = sem("both_made")
            ranked = sem("ranked")
            xn_ready = sem("xn_ready2")
            pos_ready = sem("pos_ready")
            scattered = sem("scattered")
            block = st.enter_context(nc.Block())
            acc_rows = lambda w: acc[:, bass.ds(w, 1), :].rearrange("p o (h c) -> p (o h) c", h=H)[:, :, 0:HD]
            row = lambda a, w: a[:, bass.ds(w, 1), :].rearrange("p o c -> p (o c)")
            xt_row = lambda w: acc[:, bass.ds(w, 1), 0:D].rearrange("p o c -> p (o c)")

            @block.sync
            def _(sp):
                sp.dma_start(gb[:, :], gbias.partition_broadcast(P)).then_inc(small_loaded, 16)
                sp.dma_start(brb[:, :], br.partition_broadcast(P)).then_inc(small_loaded, 16)
                sp.dma_start(wr[:, :, :], Wr.rearrange("(k p) e -> p k e", p=P)).then_inc(small_loaded, 16)
                sp.wait_ge(pad_zeroed, 1)
                load_nodes(sp, x_loaded)

            @block.gpsimd
            def _(pool):
                pool.wait_ge(small_loaded, 48)
                with pool.Fori(0, NW) as w:
                    pool.wait_ge(added, w + 1)
                    nc.gpsimd.tensor_tensor(row(node_rows, w), row(node_rows, w), gb[:, :], ALU.add).then_inc(biased, 1)
                pool.wait_ge(xn_ready, 1)
                pool.wait_ge(pos_ready, 1)
                for w in range(NW):
                    n = LAST if w == NW - 1 else P
                    for k in range(2):
                        pool.indirect_dma_start(xs, bass.IndirectOffsetOnAxis(ap=pos[k][0:n, w:w + 1], axis=0),
                                                xn[0:n, w, :], None).then_inc(scattered, 16)
                pool.wait_ge(scattered, 16 * 2 * NW)

            @block.scalar
            def _(act):
                act.wait_ge(var_ready[0], 1)
                nc.scalar.activation(rstd[:, 0, :], mv[:, 0, :, 1], ACT.Sqrt, bias=eps_col[:, 0:1]).then_inc(std_ready[0], 1)

                def copy_xT(w, b):
                    act.wait_ge(xT_made, w + 1)
                    nc.scalar.activation(xT[:, b, :], xT_ps[:, b, 0:D], ACT.Copy).then_inc(xT_copied, 1)

                with act.Fori(0, NW // 2) as i:
                    for b in range(2):
                        copy_xT(2 * i + b, b)
                copy_xT(NW - 1, 0)
                act.wait_ge(var_ready[1], 1)
                nc.scalar.activation(rstd[:, 1, :], mv[:, 1, :, 1], ACT.Sqrt, bias=eps_col[:, 0:1]).then_inc(std_ready[1], 1)
                act.wait_ge(gate_in, 1)
                nc.scalar.activation(gate[:, :], diff[:, :], ACT.Exp).then_inc(gate_made, 1)

            @block.tensor
            def _(pe):
                def transpose(w, b):
                    pe.wait_ge(xt_ready, w + 1)
                    for k in range(KD):
                        last = nc.tensor.transpose(xT_ps[:, b, k * P:(k + 1) * P], xt_st[:, b, k * P:(k + 1) * P], ident[:, :])
                    last.then_inc(xT_made, 1)

                def product(w, b, reused=True):
                    pe.wait_ge(xT_copied, w + 1)
                    if reused:
                        pe.wait_ge(lg_taken, w - 1)
                    for k in range(KD):
                        last = nc.tensor.matmul(lg_ps[:, b, 0:NE], xT[:, b, k * P:(k + 1) * P], wr[:, k, :],
                                                start=(k == 0), stop=(k == KD - 1))
                    last.then_inc(lg_made, 1)

                pe.wait_ge(small_loaded, 48)
                transpose(0, 0)
                transpose(1, 1)
                product(0, 0, reused=False)
                transpose(2, 0)
                product(1, 1, reused=False)
                with pe.Fori(1, NW // 2) as i:
                    for b in range(2):
                        transpose(2 * i + b + 1, 1 - b)
                        product(2 * i + b, b)
                product(NW - 1, 0)
                pe.wait_ge(both_made, 1)
                flat = both[:, :, :].rearrange("p w e -> p (w e)")
                nc.tensor.matmul(rank_ps[:, 0:NW * NE], before[:, :], flat, start=True, stop=True)
                nc.tensor.matmul(total_ps[:, 0:NW * NE], ones[:, :], flat, start=True, stop=True).then_inc(ranked, 1)

            @block.vector
            def _(dve):
                link = chain(dve, seq)
                nc.vector.memset(node_rows[:, NW - 1, :], 0.0).then_inc(pad_zeroed, 1)
                nc.vector.memset(zero[:, :], 0.0)
                link(nc.vector.reciprocal(rden[:, :, :], acc[:, 0:NW, :].rearrange("p w (h c) -> p w h c", h=H)[:, :, :, HD]))
                with dve.Fori(0, NW) as w:
                    nc.vector.tensor_tensor(acc_rows(w), acc_rows(w), rden[:, bass.ds(w, 1), :].rearrange("p o h -> p (o h)").unsqueeze(2)
                                            .to_broadcast([P, H, HD]), ALU.mult)
                link(nc.vector.memset(tick[:, :], 0.0))
                for g in range(NG + 1):
                    dve.wait_ge(x_loaded[g], 16)
                    with dve.Fori(g * GW, min((g + 1) * GW, NW)) as w:
                        r4 = row(node_rows, w).rearrange("p (h c) -> p h c", h=H)
                        nc.vector.tensor_tensor(r4, r4, acc_rows(w), ALU.add).then_inc(added, 1)

                def statistics(src_of, v, wait=None):
                    with dve.Fori(0, NW) as w:
                        if wait is not None:
                            dve.wait_ge(wait, w + 1)
                        nc.vector.bn_stats(row(stat, w), src_of(w))
                    link(nc.vector.memset(tick[:, :], 0.0))
                    moments(link, mv[:, v, :, 0], mv[:, v, :, 1], stat, mtmp).then_inc(var_ready[v], 1)
                    dve.wait_ge(std_ready[v], 1)
                    link(nc.vector.reciprocal(rstd[:, v, :], rstd[:, v, :]))

                def scaled(out_ap, in_ap, v, w):
                    return nc.vector.tensor_scalar(out_ap, in_ap, mv[:, v, bass.ds(w, 1), 0], rstd[:, v, bass.ds(w, 1)],
                                                   ALU.subtract, ALU.mult)

                statistics(lambda w: row(node_rows, w), 0, biased)

                def take_xt(w, b, reused=True):
                    if reused:
                        dve.wait_ge(xT_made, w - 1)
                    scaled(xt_st[:, b, :], row(node_rows, w), 0, w).then_inc(xt_ready, 1)
                    scaled(xt_row(w), row(node_rows, w), 0, w)

                def take_logits(w, b):
                    dve.wait_ge(lg_made, w + 1)
                    nc.vector.tensor_tensor(row(logit, w), lg_ps[:, b, 0:NE], brb[:, :], ALU.add).then_inc(lg_taken, 1)

                dve.wait_ge(small_loaded, 48)
                take_xt(0, 0, reused=False)
                take_xt(1, 1, reused=False)
                with dve.Fori(1, NW // 2) as i:
                    for b in range(2):
                        take_xt(2 * i + b, b)
                        take_logits(2 * i + b - 2, b)
                take_xt(NW - 1, 0)
                take_logits(NW - 3, 0)
                take_logits(NW - 2, 1)
                take_logits(NW - 1, 0)
                link(nc.vector.memset(tick[:, :], 0.0))
                statistics(xt_row, 1)
                with dve.Fori(0, NW) as w:
                    scaled(row(xn, w), xt_row(w), 1, w)
                nc.vector.memset(tick[:, :], 0.0).then_inc(xn_ready, 1)

                of_rows = lambda a: a.unsqueeze(2).to_broadcast([P, NW, NE])
                dve.wait_ge(xn_ready, 1)
                nc.vector.tensor_scalar(real[:, :], iota_col[:, :], float(LAST), None, ALU.is_lt)
                link(nc.vector.tensor_scalar(number[:, :], iota_row[:, 0:NE], -float(NE), None, ALU.add))
                numbers = number[:, :].unsqueeze(1).to_broadcast([P, NW, NE])
                left = logit
                for k in range(2):
                    link(nc.vector.tensor_reduce(top[:, k, :], left[:, :, :], X, ALU.max))
                    link(nc.vector.tensor_tensor(equal[:, :, :], left[:, :, :], of_rows(top[:, k, :]), ALU.is_equal))
                    link(nc.vector.tensor_tensor(equal[:, :, :], equal[:, :, :], numbers, ALU.mult))
                    link(nc.vector.tensor_reduce(chosen[:, :], equal[:, :, :], X, ALU.min))
                    link(nc.vector.tensor_tensor(pick[k][:, :, :], numbers, of_rows(chosen[:, :]), ALU.is_equal))
                    if k == 0:
                        link(nc.vector.scalar_tensor_tensor(rest[:, :, :], pick[0][:, :, :], -BIG, logit[:, :, :], ALU.mult, ALU.add))
                        left = rest
                nc.vector.tensor_tensor(diff[:, :], top[:, 1, :], top[:, 0, :], ALU.subtract).then_inc(gate_in, 1)
                for k in range(2):
                    last = nc.vector.tensor_scalar(pick[k][:, NW - 1, :], pick[k][:, NW - 1, :], real[:, 0:1], None, ALU.mult)
                link(last)
                nc.vector.tensor_tensor(both[:, :, :], pick[0][:, :, :], pick[1][:, :, :], ALU.add).then_inc(both_made, 1)
                dve.wait_ge(gate_made, 1)
                link(nc.vector.tensor_scalar(gate_d[:, :], gate[:, :], 1.0, None, ALU.add))
                link(nc.vector.reciprocal(wt[0][:, :], gate_d[:, :]))
                nc.vector.tensor_tensor(wt[1][:, :], gate[:, :], wt[0][:, :], ALU.mult)
                dve.wait_ge(ranked, 1)
                link(nc.vector.tensor_copy(total[:, :, :].rearrange("p w e -> p (w e)"), total_ps[:, 0:NW * NE]))
                for e in range(NE):
                    last = nc.vector.tensor_tensor_scan(upto[:, :, e], total[:, :, e], zero[:, :], 0.0, ALU.add, ALU.add)
                link(last)
                link(nc.vector.tensor_scalar(need_i[:, :], upto[:, NW - 1, :], float(TOK - 1), None, ALU.add))
                link(nc.vector.tensor_scalar(need_i[:, :], need_i[:, :], TOK.bit_length() - 1, None, ALU.arith_shift_right))
                link(nc.vector.tensor_copy(need[:, :], need_i[:, :]))
                link(nc.vector.tensor_tensor_scan(need_c[:, :], need[:, :], zero[:, 0:NE], 0.0, ALU.add, ALU.add))
                link(nc.vector.tensor_tensor(slot0[:, :], need_c[:, :], need[:, :], ALU.subtract))
                link(nc.vector.tensor_tensor(owner[:, :, :], iota_row[0:1, 0:SLOTS].unsqueeze(2).to_broadcast([1, SLOTS, NE]),
                                             slot0[0:1, :].unsqueeze(1).to_broadcast([1, SLOTS, NE]), ALU.is_ge))
                link(nc.vector.tensor_reduce(owner_s[:, :], owner[:, :, :], X, ALU.add))
                nc.vector.tensor_scalar(slot_e[:, :], owner_s[:, :], -1.0, None, ALU.add)
                link(nc.vector.tensor_tensor(place[:, :, :], upto[:, :, :], total[:, :, :], ALU.subtract))
                link(nc.vector.tensor_tensor(place[:, :, :], place[:, :, :],
                                             rank_ps[:, 0:NW * NE].rearrange("p (w e) -> p w e", e=NE), ALU.add))
                link(nc.vector.tensor_scalar(slot0[:, :], slot0[:, :], float(TOK), None, ALU.mult))
                link(nc.vector.tensor_tensor(place[:, :, :], place[:, :, :],
                                             slot0[:, :].unsqueeze(1).to_broadcast([P, NW, NE]), ALU.add))
                for k in range(2):
                    link(nc.vector.tensor_tensor(placed[:, :, :], place[:, :, :], pick[k][:, :, :], ALU.mult))
                    link(nc.vector.tensor_reduce(posf[:, :], placed[:, :, :], X, ALU.add))
                    link(nc.vector.tensor_copy(pos[k][:, :], posf[:, :]))
                nc.vector.memset(tick[:, :], 0.0).then_inc(pos_ready, 1)

        with ExitStack() as st:
            sb, ps, sem = allot(st)
            NT = TOK // P
            NPRM = FC + 2 * KD
            w1_sb = sb("w1_sb", [P, 2, KD, FH])
            w2_sb = sb("w2_sb", [P, 2, FC, D])
            prm_sb = sb("prm_sb", [P, 2, NPRM])
            b2_sb = sb("b2_sb", [P, 2, D])
            xin = sb("xin", [P, 2, NT, D])
            xe = sb("xe", [P, 2, KD, TOK])
            hid = sb("hid", [P, 2, FC, TOK])
            yo = sb("yo", [P, 2, NT, D])
            xT_ps = ps("xeT_ps", [P, 2, 512])
            hid_ps = ps("hid_ps", [P, 4, 512])
            y_ps = ps("y_ps", [P, 2, 512])
            loaded = [sem(f"slot_loaded{b}") for b in range(2)]
            stored = [sem(f"y_stored{b}") for b in range(2)]
            xT_made = sem("xeT_made")
            xe_ready = sem("xe_ready")
            hid_made = sem("hid_made")
            gelu_done = sem("gelu_done")
            y_made = sem("y_made")
            y_taken = sem("y_taken")
            block = st.enter_context(nc.Block())
            LOADS = 5

            def slots(eng, slot):
                for b in range(2):
                    slot(b, 0, b, True)
                with eng.Fori(1, SLOTS // 2) as i:
                    for b in range(2):
                        slot(2 * i + b, i, b, False)

            @block.sync
            def _(sp):
                def slot(q, i, b, new):
                    if not new:
                        sp.wait_ge(y_taken, q - 1)
                    sp.dma_start(xin[:, b, :, :], xs[bass.ds(q * TOK, TOK), :].rearrange("(t p) d -> p t d", p=P)).then_inc(loaded[b], 16)
                    e = sp.value_load(slot_e[0:1, bass.ds(q, 1)], min_val=0, max_val=NE - 1)
                    if new:
                        load_expert(e, b)
                    else:
                        held = sp.value_load(slot_e[0:1, bass.ds(q - 2, 1)], min_val=0, max_val=NE - 1)
                        with sp.If(e != held):
                            load_expert(e, b)
                        with sp.If(e == held):
                            sp.sem_inc(loaded[b], 16 * (LOADS - 1))

                def load_expert(e, b):
                    one = lambda a: a[bass.ds(e, 1)]
                    sp.dma_start(prm_sb[:, b, :], one(prm).rearrange("o p c -> p (o c)")).then_inc(loaded[b], 16)
                    sp.dma_start(w1_sb[:, b, :, :], one(W1).rearrange("o (k p) f -> p (o k) f", p=P)).then_inc(loaded[b], 16)
                    sp.dma_start(w2_sb[:, b, :, :], one(W2).rearrange("o (c p) d -> p (o c) d", p=P)).then_inc(loaded[b], 16)
                    sp.dma_start(b2_sb[:, b, :], one(b2).rearrange("o d -> (o d)").partition_broadcast(P)).then_inc(loaded[b], 16)

                slots(sp, slot)

            @block.gpsimd
            def _(pool):
                def slot(q, i, b, new):
                    pool.wait_ge(y_taken, q + 1)
                    pool.dma_start(ys[bass.ds(q * TOK, TOK), :].rearrange("(t p) d -> p t d", p=P), yo[:, b, :, :]).then_inc(stored[b], 16)

                slots(pool, slot)
                for b in range(2):
                    pool.wait_ge(stored[b], 16 * (SLOTS // 2))

            @block.scalar
            def _(act):
                def slot(q, i, b, new):
                    for c in range(FC):
                        if c % 2 == 0:
                            act.wait_ge(hid_made, FC // 2 * q + c // 2 + 1)
                        nc.scalar.activation(hid[:, b, c, :], hid_ps[:, c // 2, (c % 2) * TOK:(c % 2 + 1) * TOK], ACT.Gelu,
                                             bias=prm_sb[:, b, c:c + 1]).then_inc(gelu_done, 1)

                slots(act, slot)

            @block.tensor
            def _(pe):
                def transpose(q, i, b):
                    pe.wait_ge(loaded[b], 16 * LOADS * (i + 1))
                    for t in range(NT):
                        for k in range(KD):
                            last = nc.tensor.transpose(xT_ps[:, b, k * TOK + t * P:k * TOK + (t + 1) * P],
                                                       xin[:, b, t, k * P:(k + 1) * P], ident[:, :])
                    last.then_inc(xT_made, 1)

                def slot(q, i, b, new, following=True):
                    pe.wait_ge(xe_ready, q + 1)
                    for c in range(FC):
                        if c % 2 == 0 and not (isinstance(q, int) and q == 0):
                            pe.wait_ge(gelu_done, FC * q - FC + c + 2)
                        for k in range(KD):
                            last = nc.tensor.matmul(hid_ps[:, c // 2, (c % 2) * TOK:(c % 2 + 1) * TOK],
                                                    w1_sb[:, b, k, c * P:(c + 1) * P], xe[:, b, k, :],
                                                    start=(k == 0), stop=(k == KD - 1))
                        if c % 2:
                            last.then_inc(hid_made, 1)
                    if following:
                        transpose(q + 1, i + b, 1 - b)
                    pe.wait_ge(gelu_done, FC * q + FC)
                    if not new:
                        pe.wait_ge(y_taken, q - 1)
                    for t in range(NT):
                        for c in range(FC):
                            last = nc.tensor.matmul(y_ps[:, b, t * D:(t + 1) * D], hid[:, b, c, t * P:(t + 1) * P],
                                                    w2_sb[:, b, c, :], start=(c == 0), stop=(c == FC - 1))
                    last.then_inc(y_made, 1)

                transpose(0, 0, 0)
                slot(0, 0, 0, True)
                slot(1, 0, 1, True)
                with pe.Fori(1, SLOTS // 2 - 1) as i:
                    for b in range(2):
                        slot(2 * i + b, i, b, False)
                i = SLOTS // 2 - 1
                slot(2 * i, i, 0, False)
                slot(2 * i + 1, i, 1, False, following=False)

            @block.vector
            def _(dve):
                def take_x(q, b):
                    dve.wait_ge(xT_made, q + 1)
                    for k in range(KD):
                        last = nc.vector.tensor_scalar(xe[:, b, k, :], xT_ps[:, b, k * TOK:(k + 1) * TOK],
                                                       prm_sb[:, b, FC + k:FC + k + 1], prm_sb[:, b, FC + KD + k:FC + KD + k + 1],
                                                       ALU.mult, ALU.add)
                    last.then_inc(xe_ready, 1)

                def take_y(q, i, b, new):
                    dve.wait_ge(y_made, q + 1)
                    if not new:
                        dve.wait_ge(stored[b], 16 * i)
                    nc.vector.tensor_tensor(yo[:, b, :, :], y_ps[:, b, :].rearrange("p (t d) -> p t d", t=NT),
                                            b2_sb[:, b, :].unsqueeze(1).to_broadcast([P, NT, D]), ALU.add).then_inc(y_taken, 1)

                take_x(0, 0)
                take_x(1, 1)
                take_y(0, 0, 0, True)
                take_x(2, 0)
                take_y(1, 0, 1, True)
                with dve.Fori(1, SLOTS // 2 - 1) as i:
                    for b in range(2):
                        take_x(2 * i + b + 1, 1 - b)
                        take_y(2 * i + b, i, b, False)
                i = SLOTS // 2 - 1
                take_x(2 * i + 1, 1)
                take_y(2 * i, i, 0, False)
                take_y(2 * i + 1, i, 1, False)

        with ExitStack() as st:
            sb, ps, sem = allot(st)
            CR = 4
            y_g = sb("y_g", [P, CR, 2, D])
            gathered = [sem(f"gathered{r}") for r in range(CR)]
            first_added = sem("first_added")
            done = sem("done")
            stored = sem("out_stored")
            block = st.enter_context(nc.Block())
            rows = lambda w: LAST if w == NW - 1 else P

            @block.gpsimd
            def _(pool):
                for w in range(NW):
                    if w >= CR:
                        pool.wait_ge(done, w - CR + 1)
                    for k in range(2):
                        pool.indirect_dma_start(y_g[0:rows(w), w % CR, k, :], None, ys,
                                                bass.IndirectOffsetOnAxis(ap=pos[k][0:rows(w), w:w + 1], axis=0)
                                                ).then_inc(gathered[w % CR], 16)

            @block.vector
            def _(dve):
                def add(w):
                    n = rows(w)
                    dve.wait_ge(gathered[w % CR], 32 * (w // CR + 1))
                    x1 = node_rows[0:n, w, :]
                    nc.vector.scalar_tensor_tensor(x1, y_g[0:n, w % CR, 0, :], wt[0][0:n, w:w + 1], x1,
                                                   ALU.mult, ALU.add).then_inc(first_added, 1)
                    dve.wait_ge(first_added, w + 1)
                    nc.vector.scalar_tensor_tensor(x1, y_g[0:n, w % CR, 1, :], wt[1][0:n, w:w + 1], x1,
                                                   ALU.mult, ALU.add).then_inc(done, 1)

                for w in range(NW):
                    add(w)

            @block.sync
            def _(sp):
                for g in range(NG):
                    sp.wait_ge(done, (g + 1) * GW)
                    sp.dma_start(out[g * GW * P:(g + 1) * GW * P, :].rearrange("(w p) d -> p w d", p=P),
                                 node_rows[:, g * GW:(g + 1) * GW, :]).then_inc(stored, 16)
                sp.wait_ge(done, NW)
                sp.dma_start(out[(NW - 1) * P:N, :], node_rows[0:LAST, NW - 1, :]).then_inc(stored, 16)
                sp.wait_ge(stored, 16 * (NG + 1))


_INS = ['x', 'src', 'dst', 'L0_gnn_W', 'L0_gnn_att_src', 'L0_gnn_att_dst', 'L0_gnn_bias', 'L0_ffn_Wr', 'L0_ffn_br',
        'L0_ffn_ln_g', 'L0_ffn_ln_b', 'L0_ffn_W1', 'L0_ffn_b1', 'L0_ffn_W2', 'L0_ffn_b2']


def kernel(**inputs):
    import numpy as _np
    import concourse.bacc as _bacc
    from concourse import mybir as _mybir
    from concourse.bass_utils import run_bass_kernel_spmd as _run

    nc = _bacc.Bacc("TRN2", target_bir_lowering=False, num_devices=1)
    arrays, args = {}, []
    for name in _INS:
        a = _np.ascontiguousarray(inputs[name])
        arrays[f"in_{name}"] = a
        args.append(nc.dram_tensor(f"in_{name}", a.shape, _mybir.dt.from_np(a.dtype), kind="ExternalInput").ap())
    out = nc.dram_tensor("out_x", inputs["x"].shape, _mybir.dt.float32, kind="ExternalOutput").ap()
    gat_moe(nc, *args, out)
    r = _run(nc, [arrays], core_ids=[0])
    return r.results[0]["out_x"]
```

```python
from contextlib import ExitStack

import concourse.bass as bass
from concourse import mybir

F32 = mybir.dt.float32
I32 = mybir.dt.int32
U32 = mybir.dt.uint32
BF16 = mybir.dt.bfloat16
ALU = mybir.AluOpType
ACT = mybir.ActivationFunctionType
X = mybir.AxisListType.X

P = 128
EPS = 1e-5
SLOPE = 0.2
BIG = 1e30
T = 4
STEP = T * P
HS = 4
RING = 3
TOK = 256


def gat_moe(nc, x, src, dst, gW, att_src, att_dst, gbias, Wr, br, ln_g, ln_b, W1, b1, W2, b2, out):
    N, D = x.shape
    E = src.shape[0]
    H, HD = att_src.shape
    NE = Wr.shape[1]
    FH = W1.shape[2]
    KD = D // P
    FC = FH // P
    NW = -(-N // P)
    LAST = N - (NW - 1) * P
    ROW = H * (HD + 1)
    steps_bound = (E + NW * (STEP - 1)) // STEP
    NH = -(-steps_bound // (HS * RING)) * RING
    NS = NH * HS
    PAIRS = 2 * N
    SLOTS = (PAIRS + NE * (TOK - 1)) // TOK
    PLACES = SLOTS * TOK
    NCNT = NW + 1
    GW = 6
    NG = (NW - 1) // GW
    assert NG * GW == NW - 1
    EP, EC = 125, E // 125
    assert EP * EC == E and D == KD * P and NS <= 2 * P and SLOTS % 2 == 0 and NW % 2 == 1

    dst_pad = nc.dram_tensor("dst_pad", [1 + E + 2 * STEP], I32, kind="Internal").ap()
    src_pad = nc.dram_tensor("src_pad", [E + 2 * STEP], I32, kind="Internal").ap()
    table = nc.dram_tensor("table", [N, ROW], F32, kind="Internal").ap()
    x1_dram = nc.dram_tensor("x1_dram", [N, D], F32, kind="Internal").ap()
    xs = nc.dram_tensor("xs", [PLACES, D], F32, kind="Internal").ap()
    ys = nc.dram_tensor("ys", [PLACES, D], F32, kind="Internal").ap()
    prm = nc.dram_tensor("prm", [NE, P, FC + 2 * KD], F32, kind="Internal").ap()

    ctx = ExitStack()
    with ctx:
        def allot(stack):
            def sb(name, shape, dt=F32):
                return stack.enter_context(nc.sbuf_tensor(name, shape, dt))

            def ps(name, shape, dt=F32):
                return stack.enter_context(nc.psum_tensor(name, shape, dt))

            def sem(name):
                return stack.enter_context(nc.semaphore(name))

            return sb, ps, sem

        sb, _, _ = allot(ctx)
        ident = sb("ident", [P, P])
        ident16 = sb("ident16", [P, P], BF16)
        ones = sb("ones", [P, P])
        iota_row = sb("iota_row", [P, P])
        iota_col = sb("iota_col", [P, 1])
        before = sb("before", [P, P])
        wbase = sb("wbase", [P, 2 * P])
        win_i = sb("win_i", [1, 2 * P], I32)
        off_i = sb("off_i", [1, 2 * P], I32)
        edge_cnt = sb("edge_cnt", [P, NCNT])
        big = sb("big", [P, NW * D])
        slot_e = sb("slot_e", [1, SLOTS], I32)
        pos = [sb(f"pos{k}", [P, NW], U32) for k in range(2)]
        wt = [sb(f"wt{k}", [P, NW]) for k in range(2)]
        eps_col = sb("eps_col", [P, 1])
        tick = sb("tick", [P, 1])

        _, _, lasting = allot(ctx)
        x_first = [lasting(f"x_first{g}") for g in range(NG + 1)]
        until_experts = ctx.enter_context(ExitStack())
        sb, _, _ = allot(until_experts)
        zeros = sb("zeros", [P, D])
        dm = sb("dm", [P, NW + 1, 2 * H])
        acc = sb("acc", [P, NW + 1, ROW])

        node_rows = big[:, :].rearrange("p (w d) -> p w d", d=D)

        def chain(eng, s, base=0):
            count = [0]

            def link(ins):
                count[0] += 1
                ins.then_inc(s, 1)
                eng.wait_ge(s, base + count[0])

            link.count = count
            return link

        def moments(link, mean, var, stats, tmp):
            nc.vector.tensor_tensor(mean, stats[:, :, 1], stats[:, :, 4], ALU.add)
            nc.vector.tensor_tensor(tmp[:, 0, :], stats[:, :, 1], stats[:, :, 4], ALU.subtract)
            link(nc.vector.tensor_tensor(var, stats[:, :, 2], stats[:, :, 5], ALU.add))
            link(nc.vector.tensor_scalar(mean, mean, 0.5, None, ALU.mult))
            link(nc.vector.scalar_tensor_tensor(tmp[:, 1, :], tmp[:, 0, :], 0.25, tmp[:, 0, :], ALU.mult, ALU.mult))
            return nc.vector.scalar_tensor_tensor(var, var, 1.0 / D, tmp[:, 1, :], ALU.mult, ALU.add)

        def copied(out_ap, in_ap):
            return nc.vector.tensor_scalar(out_ap, in_ap, 1.0, None, ALU.mult)

        def each_window(eng, body, start=0, count=NW):
            turn = next(u for u in (7, 3, 2, 1) if count % u == 0)
            if count == turn:
                for u in range(turn):
                    body(start + u)
                return
            with eng.Fori(0, count // turn) as i:
                for u in range(turn):
                    body(turn * i + u + start)

        def load_nodes(sp, loaded):
            for g in range(NG):
                sp.dma_start(node_rows[:, g * GW:(g + 1) * GW, :],
                             x[g * GW * P:(g + 1) * GW * P, :].rearrange("(w p) d -> p w d", p=P)).then_inc(loaded[g], 16)
            sp.dma_start(node_rows[0:LAST, NW - 1, :], x[(NW - 1) * P:N, :]).then_inc(loaded[NG], 16)

        with ExitStack() as st:
            sb, ps, sem = allot(st)
            pad = sb("pad", [1, 2 * STEP], I32)
            zpad = sb("zpad", [1, 2 * STEP], I32)
            dst_i = sb("dst_i", [P, EC], I32)
            win_of = sb("win_of", [P, EC], I32)
            win_f = sb("win_f", [P, EC], BF16)
            junk = sb("junk", [P, EC], BF16)
            bound = sb("bound", [P, NCNT])
            pt = sb("pt", [P, NE, FC + 2 * KD])
            consts_made = sem("consts_made")
            pad_zeroed = sem("pad_zeroed")
            tiles_set = sem("tiles_set")
            dst_set = sem("dst_set")
            dst_loaded = sem("dst_loaded")
            ident_made = sem("ident_made")
            counted = sem("counted")
            prm_loaded = sem("prm_loaded")
            stores = sem("stores")
            loads = sem("loads")
            block = st.enter_context(nc.Block())

            @block.gpsimd
            def _(pool):
                nc.gpsimd.iota(iota_row[:, :], [[1, P]], base=0, channel_multiplier=0,
                               allow_small_or_imprecise_dtypes=True)
                nc.gpsimd.iota(iota_col[:, :], [[0, 1]], base=0, channel_multiplier=1,
                               allow_small_or_imprecise_dtypes=True)
                nc.gpsimd.iota(bound[:, :], [[1, NCNT]], base=0, channel_multiplier=0,
                               allow_small_or_imprecise_dtypes=True)
                nc.gpsimd.memset(ident[:, :], 0.0)
                nc.gpsimd.memset(ones[:, :], 1.0).then_inc(consts_made, 1)
                pool.wait_ge(consts_made, 1)
                nc.gpsimd.affine_select(out=ident[:, :], in_=ident[:, :], compare_op=ALU.not_equal, fill=1.0,
                                        base=0, pattern=[[-1, P]], channel_multiplier=1).then_inc(ident_made, 1)
                nc.gpsimd.affine_select(out=before[:, :], in_=ones[:, :], compare_op=ALU.is_gt, fill=0.0,
                                        base=0, pattern=[[1, P]], channel_multiplier=-1).then_inc(ident_made, 1)

            @block.vector
            def _(dve):
                link = chain(dve, counted)
                nc.vector.memset(dst_i[:, :], N + P)
                nc.vector.memset(pad[:, :], 2 * N).then_inc(dst_set, 1)
                nc.vector.memset(zpad[:, :], 0)
                nc.vector.memset(node_rows[:, NW - 1, :], 0.0).then_inc(pad_zeroed, 1)
                nc.vector.memset(zeros[:, :], 0.0)
                nc.vector.memset(eps_col[:, :], EPS)
                nc.vector.memset(edge_cnt[:, :], 0.0).then_inc(tiles_set, 1)
                dve.wait_ge(ident_made, 1)
                nc.vector.tensor_copy(ident16[:, :], ident[:, :])
                dve.wait_ge(dst_loaded, 16)
                link(nc.vector.tensor_scalar(win_of[:, :], dst_i[:, :], P.bit_length() - 1, None, ALU.arith_shift_right))
                link(nc.vector.tensor_copy(win_f[:, :], win_of[:, :]))

                def count_before(w):
                    nc.vector.tensor_scalar(junk[:, :], win_f[:, :], bound[:, bass.ds(w, 1)], 0.0, ALU.is_lt, ALU.add,
                                            accum_out=edge_cnt[:, bass.ds(w, 1)]).then_inc(counted, 1)
                    dve.wait_ge(counted, w + 2)

                each_window(dve, count_before, 1, NW)

            @block.sync
            def _(sp):
                sp.wait_ge(dst_set, 1)
                sp.dma_start(dst_i[0:EP, :], dst.rearrange("(p c) -> p c", p=EP)).then_inc(dst_loaded, 16)
                sp.dma_start(dst_pad[1:1 + E].rearrange("(a b) -> a b", a=EP), dst.rearrange("(a b) -> a b", a=EP)).then_inc(stores, 16)
                sp.dma_start(src_pad[0:E].rearrange("(a b) -> a b", a=EP), src.rearrange("(a b) -> a b", a=EP)).then_inc(stores, 16)
                sp.wait_ge(tiles_set, 1)
                sp.dma_start(dst_pad[0:1].rearrange("(a b) -> a b", a=1), pad[:, 0:1]).then_inc(stores, 16)
                sp.dma_start(dst_pad[1 + E:].rearrange("(a b) -> a b", a=1), pad[:, :]).then_inc(stores, 16)
                sp.dma_start(src_pad[E:].rearrange("(a b) -> a b", a=1), zpad[:, :]).then_inc(stores, 16)
                sp.wait_ge(pad_zeroed, 1)
                load_nodes(sp, x_first)
                sp.wait_ge(stores, 16 * 5)

            @block.scalar
            def _(act):
                for e in range(NE):
                    act.dma_start(pt[:, e, 0:FC], b1[e].rearrange("(c p) -> p c", p=P),
                                  allow_slow_non_contiguous=True).then_inc(prm_loaded, 16)
                    act.dma_start(pt[:, e, FC:FC + KD], ln_g[e].rearrange("(k p) -> p k", p=P),
                                  allow_slow_non_contiguous=True).then_inc(prm_loaded, 16)
                    act.dma_start(pt[:, e, FC + KD:], ln_b[e].rearrange("(k p) -> p k", p=P),
                                  allow_slow_non_contiguous=True).then_inc(prm_loaded, 16)
                act.wait_ge(prm_loaded, 16 * 3 * NE)
                act.dma_start(prm.rearrange("e p c -> p e c"), pt[:, :, :]).then_inc(loads, 16)
                act.wait_ge(loads, 16)

        with ExitStack() as st:
            sb, ps, sem = allot(st)
            start_ps = ps("start_ps", [P, NCNT])
            row_ps = ps("row_ps", [P, 4, P])
            start = sb("start", [P, NCNT])
            first = sb("first", [P, NCNT])
            cnt = sb("cnt", [P, NW])
            cnt_i = sb("cnt_i", [P, NW], I32)
            zero = sb("zero", [P, NW])
            q = sb("q", [P, NCNT])
            dq = sb("dq", [P, NCNT])
            passed = sb("passed", [P, 2, NCNT])
            part = sb("part", [P, 2, NCNT])
            stepno = sb("stepno", [P, 2])
            val = sb("val", [P, 4])
            spread = sb("spread", [P, 4, P])
            summed = sem("summed")
            spread_done = sem("spread_done")
            rows_done = sem("rows_done")
            dve_seq = sem("sched_seq")
            block = st.enter_context(nc.Block())

            @block.tensor
            def _(pe):
                nc.tensor.matmul(start_ps[:, :], ones[:, :], edge_cnt[:, :], start=True, stop=True).then_inc(summed, 1)
                pe.wait_ge(spread_done, 1)
                for v in range(4):
                    last = nc.tensor.matmul(row_ps[:, v, :], spread[:, v, :], ident[:, :], start=True, stop=True)
                last.then_inc(rows_done, 1)

            @block.vector
            def _(dve):
                link = chain(dve, dve_seq)
                nc.vector.memset(zero[:, :], 0.0)
                nc.vector.memset(first[:, :], 0.0)
                nc.vector.memset(dq[:, :], 0.0)
                nc.vector.tensor_copy(stepno[:, 0:1], iota_col[:, :])
                link(nc.vector.tensor_scalar(stepno[:, 1:2], iota_col[:, :], float(P), None, ALU.add))
                dve.wait_ge(summed, 1)
                link(nc.vector.tensor_copy(start[:, :], start_ps[:, :]))
                link(nc.vector.tensor_tensor(cnt[:, :], start[:, 1:], start[:, 0:NW], ALU.subtract))
                link(nc.vector.tensor_scalar(cnt_i[:, :], cnt[:, :], float(STEP - 1), None, ALU.add))
                link(nc.vector.tensor_scalar(cnt_i[:, :], cnt_i[:, :], STEP.bit_length() - 1, None, ALU.arith_shift_right))
                link(nc.vector.tensor_copy(cnt[:, :], cnt_i[:, :]))
                link(nc.vector.tensor_tensor_scan(first[:, 1:], cnt[:, :], zero[:, :], 0.0, ALU.add, ALU.add))
                link(nc.vector.scalar_tensor_tensor(q[:, :], first[:, :], -float(STEP), start[:, :], ALU.mult, ALU.add))
                link(nc.vector.tensor_tensor(dq[:, 1:], q[:, 1:], q[:, 0:NW], ALU.subtract))
                for j in range(2):
                    last = nc.vector.tensor_scalar(passed[:, j, :], first[:, :], stepno[:, j:j + 1], None, ALU.is_le)
                link(last)
                for j in range(2):
                    last = nc.vector.tensor_tensor(part[:, j, :], passed[:, j, :], dq[:, :], ALU.mult)
                link(last)
                nc.vector.tensor_reduce(val[:, 0:2], passed[:, :, :], X, ALU.add)
                link(nc.vector.tensor_reduce(val[:, 2:4], part[:, :, :], X, ALU.add))
                link(nc.vector.scalar_tensor_tensor(val[:, 2:4], stepno[:, :], float(STEP), val[:, 2:4], ALU.mult, ALU.add))
                nc.vector.tensor_scalar(val[:, 0:2], val[:, 0:2], -1.0, None, ALU.add)
                link(nc.vector.tensor_scalar(val[:, 2:4], val[:, 2:4], float(E), None, ALU.min))
                for v in range(4):
                    last = nc.vector.tensor_scalar(spread[:, v, :], ones[:, :], val[:, v:v + 1], None, ALU.mult)
                last.then_inc(spread_done, 1)
                dve.wait_ge(rows_done, 1)
                nc.vector.tensor_scalar(wbase[:, :], row_ps[:, 0:2, :].rearrange("p a b -> p (a b)"), float(P), None, ALU.mult)
                nc.vector.tensor_copy(win_i[:, :], row_ps[0:1, 0:2, :].rearrange("p a b -> p (a b)"))
                nc.vector.tensor_copy(off_i[:, :], row_ps[0:1, 2:4, :].rearrange("p a b -> p (a b)"))

        with ExitStack() as st:
            sb, ps, sem = allot(st)
            WX = ROW + H
            wx = sb("wx", [P, KD, WX])
            w_sb = sb("w_sb", [P, KD, D])
            attb = sb("attb", [P, 2, D])
            prod = sb("prod", [P, 2, KD, D])
            attw = sb("attw", [P, 2, KD, H])
            stat = sb("stat", [P, NW, 6])
            mv = sb("mv", [P, NW, 2])
            rstd = sb("rstd", [P, NW])
            mtmp = sb("mtmp", [P, 2, NW])
            xn_st = sb("xn_st", [P, 2, D])
            xT = sb("xT", [P, 2, D])
            hx = sb("hx", [P, 2, WX])
            xT_ps = ps("xT_ps", [P, 2, 512])
            h_ps = ps("h_ps", [P, 2, 512])
            w_loaded = sem("w_loaded")
            acc_one = sem("acc_one")
            wx_ready = sem("wx_ready")
            var_ready = sem("var_ready")
            std_ready = sem("std_ready")
            dve_seq = sem("proj_seq")
            xn_ready = sem("xn_ready")
            xT_made = sem("xT_made")
            xT_copied = sem("xT_copied")
            h_made = sem("h_made")
            h_copied = sem("h_copied")
            dm_done = sem("dm_done")
            acc_set = sem("acc_set")
            table_stored = [sem(f"table_stored{b}") for b in range(2)]
            block = st.enter_context(nc.Block())

            @block.sync
            def _(sp):
                sp.dma_start(w_sb[:, :, :], gW.rearrange("(k p) n -> p k n", p=P)).then_inc(w_loaded, 16)
                sp.dma_start(attb[:, 0, :], att_src.rearrange("h c -> (h c)").partition_broadcast(P)).then_inc(w_loaded, 16)
                sp.dma_start(attb[:, 1, :], att_dst.rearrange("h c -> (h c)").partition_broadcast(P)).then_inc(w_loaded, 16)

                def store_rows(w, b, rows=P):
                    sp.wait_ge(h_copied, w + 1)
                    sp.dma_start(table[bass.ds(w * P, rows), :], hx[0:rows, b, 0:ROW]).then_inc(table_stored[b], 16)

                with sp.Fori(0, NW // 2) as i:
                    for b in range(2):
                        store_rows(2 * i + b, b)
                store_rows(NW - 1, 0, LAST)
                sp.wait_ge(table_stored[0], 16 * (NW // 2 + 1))
                sp.wait_ge(table_stored[1], 16 * (NW // 2))

            @block.gpsimd
            def _(pool):
                nc.gpsimd.memset(acc[:, :, :], 1.0).then_inc(acc_one, 1)
                pool.wait_ge(acc_one, 1)

                def start_acc(w, b):
                    pool.wait_ge(h_copied, w + 1)
                    nc.gpsimd.tensor_copy(acc[:, bass.ds(w, 1), :].rearrange("p o (h c) -> p (o h) c", h=H)[:, :, 0:HD],
                                          hx[:, b, 0:ROW].rearrange("p (h c) -> p h c", h=H)[:, :, 0:HD]).then_inc(acc_set, 1)

                with pool.Fori(0, NW // 2) as i:
                    for b in range(2):
                        start_acc(2 * i + b, b)
                start_acc(NW - 1, 0)

            @block.scalar
            def _(act):
                act.wait_ge(var_ready, 1)
                nc.scalar.activation(rstd[:, :], mv[:, :, 1], ACT.Sqrt, bias=eps_col[:, 0:1]).then_inc(std_ready, 1)

                def copy_xT(w, b):
                    act.wait_ge(xT_made, w + 1)
                    nc.scalar.activation(xT[:, b, :], xT_ps[:, b, 0:D], ACT.Copy).then_inc(xT_copied, 1)

                with act.Fori(0, NW // 2) as i:
                    for b in range(2):
                        copy_xT(2 * i + b, b)
                copy_xT(NW - 1, 0)

            @block.tensor
            def _(pe):
                def transpose(w, b):
                    pe.wait_ge(xn_ready, w + 1)
                    for k in range(KD):
                        last = nc.tensor.transpose(xT_ps[:, b, k * P:(k + 1) * P], xn_st[:, b, k * P:(k + 1) * P], ident[:, :])
                    last.then_inc(xT_made, 1)

                def product(w, b, reused=True):
                    pe.wait_ge(xT_copied, w + 1)
                    if reused:
                        pe.wait_ge(h_copied, w - 1)
                    for k in range(KD):
                        last = nc.tensor.matmul(h_ps[:, b, 0:WX], xT[:, b, k * P:(k + 1) * P], wx[:, k, :],
                                                start=(k == 0), stop=(k == KD - 1))
                    last.then_inc(h_made, 1)

                pe.wait_ge(wx_ready, 1)
                transpose(0, 0)
                transpose(1, 1)
                product(0, 0, reused=False)
                transpose(2, 0)
                product(1, 1, reused=False)
                with pe.Fori(1, NW // 2) as i:
                    for b in range(2):
                        transpose(2 * i + b + 1, 1 - b)
                        product(2 * i + b, b)
                product(NW - 1, 0)

            @block.vector
            def _(dve):
                link = chain(dve, dve_seq)
                nc.vector.memset(dm[:, :, :], 0.0)
                dve.wait_ge(w_loaded, 48)
                for v in range(2):
                    for k in range(KD):
                        last = nc.vector.tensor_tensor(prod[:, v, k, :], w_sb[:, k, :], attb[:, v, :], ALU.mult)
                link(last)
                for v in range(2):
                    last = nc.vector.tensor_reduce(attw[:, v, :, :].rearrange("p k h -> p (k h)"),
                                                   prod[:, v, :, :].rearrange("p k (h c) -> p (k h) c", h=H), X, ALU.add)
                link(last)
                for k in range(KD):
                    rows = wx[:, k, 0:ROW].rearrange("p (h c) -> p h c", h=H)
                    nc.vector.tensor_copy(rows[:, :, 0:HD], w_sb[:, k, :].rearrange("p (h c) -> p h c", h=H))
                    nc.vector.tensor_copy(rows[:, :, HD], attw[:, 0, k, :])
                    last = nc.vector.tensor_copy(wx[:, k, ROW:], attw[:, 1, k, :])
                last.then_inc(wx_ready, 1)

                for g in range(NG + 1):
                    dve.wait_ge(x_first[g], 16)
                    each_window(dve, lambda w: nc.vector.bn_stats(stat[:, bass.ds(w, 1), :].rearrange("p o c -> p (o c)"),
                                                                  node_rows[:, bass.ds(w, 1), :].rearrange("p o c -> p (o c)")),
                                g * GW, min(GW, NW - g * GW))
                link(nc.vector.memset(tick[:, :], 0.0))
                moments(link, mv[:, :, 0], mv[:, :, 1], stat, mtmp).then_inc(var_ready, 1)
                dve.wait_ge(std_ready, 1)
                link(nc.vector.reciprocal(rstd[:, :], rstd[:, :]))

                def normalise(w, b, reused=True):
                    if reused:
                        dve.wait_ge(xT_made, w - 1)
                    nc.vector.tensor_scalar(xn_st[:, b, :], node_rows[:, bass.ds(w, 1), :].rearrange("p o c -> p (o c)"),
                                            mv[:, bass.ds(w, 1), 0], rstd[:, bass.ds(w, 1)],
                                            ALU.subtract, ALU.mult).then_inc(xn_ready, 1)

                def take_h(w, b, use=None):
                    dve.wait_ge(h_made, w + 1)
                    if use is not None:
                        dve.wait_ge(table_stored[b], 16 * use)
                        dve.wait_ge(acc_set, w - 1)
                    nc.vector.tensor_copy(hx[:, b, :], h_ps[:, b, 0:WX]).then_inc(h_copied, 1)
                    dve.wait_ge(h_copied, w + 1)
                    d_row = dm[:, bass.ds(w, 1), :].rearrange("p o c -> p (o c)")
                    copied(d_row[:, 0:H], hx[:, b, ROW:])
                    nc.vector.tensor_tensor(d_row[:, H:], hx[:, b, ROW:],
                                            hx[:, b, 0:ROW].rearrange("p (h c) -> p h c", h=H)[:, :, HD], ALU.add)

                normalise(0, 0, reused=False)
                normalise(1, 1, reused=False)
                normalise(2, 0)
                take_h(0, 0)
                normalise(3, 1)
                take_h(1, 1)
                with dve.Fori(1, NW // 2 - 1) as i:
                    for b in range(2):
                        normalise(2 * i + b + 2, b)
                        take_h(2 * i + b, b, use=i)
                w = NW - 3
                normalise(w + 2, 0)
                take_h(w, 0, use=w // 2)
                take_h(w + 1, 1, use=w // 2)
                take_h(w + 2, 0, use=w // 2 + 1)
                link(nc.vector.memset(tick[:, :], 0.0))
                link(nc.vector.scalar_tensor_tensor(dm[:, :, H:], dm[:, :, H:], SLOPE, dm[:, :, H:], ALU.mult, ALU.max))

        with ExitStack() as st:
            sb, ps, sem = allot(st)
            HB = HS * H
            HT = HS * T
            D8 = 2 * H
            LINKS = 17
            NB = NH // RING
            ZROWS = 7
            ZTURNS = PLACES // P // ZROWS
            assert ZTURNS * ZROWS * P == PLACES and 1 + ZTURNS < NB
            gat = big[:, 0:RING * HT * ROW].rearrange("p (r j t h c) -> p r j t h c", r=RING, j=HS, t=T, h=H)
            gat_rows = big[:, 0:RING * HT * ROW].rearrange("p (n c) -> p n c", c=ROW)
            src_t = sb("src_t", [P, RING, HS, T], I32)
            dst_t = sb("dst_t", [P, 3, RING, HS, T], I32)
            dloc = sb("dloc", [P, RING, HS, T])
            begins = sb("begins", [P, HS, T])
            ends = sb("ends", [P, RING, HS, T])
            last_edge = sb("last_edge", [P, HS, T])
            last_col = sb("last_col", [P, 1])
            resets = sb("resets", [P, T, HS, H])
            onehot = sb("onehot", [P, RING, HS, T, P])
            onehot16 = sb("onehot16", [P, HS, T, P], BF16)
            iota16 = sb("iota16", [P, P], BF16)
            onehotT = sb("onehotT", [P, HS, T * P], BF16)
            a_s = sb("a_s", [P, RING, T, HS, H])
            resT = sb("resT", [HB, T * P])
            runmax = sb("runmax", [HB, T * P])
            seg = sb("seg", [P, HS, T, H])
            seg_r = sb("seg_r", [P, HS, T, H])
            seg16 = sb("seg16", [P, HS, T, 3, H + 1], BF16)
            absent = sb("absent", [P, HS])
            cand = sb("cand", [P, HS, H])
            cand2 = sb("cand2", [P, HS, H])
            known = sb("known", [P, HS, D8])
            cur = sb("cur", [P, HS, D8])
            best = sb("best", [P, H, HS])
            highest = sb("highest", [P, H, HS])
            old = sb("old", [P, H, HS])
            wreset = sb("wreset", [P, NS])
            reset_j = sb("reset_j", [P, H, HS])
            cur_r = sb("cur_r", [P, HS, D8])
            cur16 = sb("cur16", [P, HS, 3, D8], BF16)
            shrink_x = sb("shrink_x", [P, H, HS])
            shrink = sb("shrink", [P, RING, HS, H])
            score = sb("score", [P, HS, T, H])
            score2 = sb("score2", [P, HS, T, H])
            wgt = sb("wgt", [P, RING, HS, T, H])
            wrow = sb("wrow", [P, HS, T, H, HD + 1])
            asT_ps = ps("asT_ps", [HB, 512])
            resT_ps = ps("resT_ps", [HB, 512])
            seg_ps = ps("seg_ps", [P, 512])
            ohT_ps = ps("ohT_ps", [P, 2, 1024], BF16)
            edge_ps = ps("edge_ps", [P, 512])
            sum_ps = ps("sum_ps", [P, 2, 512])
            back_ps = seg_ps[:, 0:T * HB]
            win_ps = seg_ps[:, 128:128 + HS * (H + 1)].rearrange("p (j c) -> p j c", j=HS)

            edges_loaded = [sem(f"edges_loaded{r}") for r in range(RING)]
            rows_gathered = [sem(f"rows_gathered{r}") for r in range(RING)]
            seq = sem("attend_seq")
            marks_set = sem("marks_set")
            onehot_made = sem("onehot_made")
            a_s_staged = sem("a_s_staged")
            asT_made = sem("asT_made")
            resT_copied = sem("resT_copied")
            resets_made = sem("resets_made")
            resT_made = sem("resT_made")
            onehot_copied = sem("onehot_copied")
            ohT_made = sem("ohT_made")
            onehotT_copied = sem("onehotT_copied")
            scanned = sem("scanned")
            back_made = sem("back_made")
            seg_made = sem("seg_made")
            win_made = sem("win_made")
            cur_made = sem("cur_made")
            shrink_in = sem("shrink_in")
            shrink_made = sem("shrink_made")
            edge_made = sem("edge_made")
            score_made = sem("score_made")
            weights_made = sem("weights_made")
            rows_weighted = sem("rows_weighted")
            slot_free = sem("slot_free")
            summed = sem("step_summed")
            xs_zeroed = sem("xs_zeroed")
            merged = sem("merged")
            block = st.enter_context(nc.Block())

            @block.sync
            def _(sp):
                def load_half(n, r, reused=True):
                    k = RING * n + r
                    if reused:
                        sp.wait_ge(score_made, k - RING + 1)
                    for j in range(HS):
                        off = sp.value_load(off_i[0:1, bass.ds(HS * k + j, 1)], min_val=0, max_val=E)
                        sp.dma_start(src_t[:, r, j, :], src_pad[bass.ds(off, STEP)].rearrange("(p t) -> p t", t=T)
                                     ).then_inc(edges_loaded[r], 16)
                        for v in range(3):
                            sp.dma_start(dst_t[:, v, r, j, :], dst_pad[bass.ds(off + v, STEP)].rearrange("(p t) -> p t", t=T)
                                         ).then_inc(edges_loaded[r], 16)

                for r in range(RING):
                    load_half(0, r, reused=False)
                with sp.Fori(1, NB) as n:
                    for r in range(RING):
                        load_half(n, r)

            @block.gpsimd
            def _(pool):
                def gather_half(n, r, reused=True):
                    pool.wait_ge(edges_loaded[r], 256 * (n + 1))
                    for j in range(HS):
                        if reused:
                            pool.wait_ge(rows_weighted, HS * (RING * n + r - RING) + j + 1)
                            pool.sem_inc(slot_free, 1)
                        for t in range(T):
                            pool.indirect_dma_start(
                                gat_rows[:, (r * HS + j) * T + t, :], None, table,
                                bass.IndirectOffsetOnAxis(ap=src_t[:, r, j, t:t + 1].bitcast(U32), axis=0),
                            ).then_inc(rows_gathered[r], 16)

                for r in range(RING):
                    gather_half(0, r, reused=False)
                with pool.Fori(1, NB) as n:
                    for r in range(RING):
                        gather_half(n, r)


            def turns(eng, half):
                for r in range(RING):
                    half(r, 0, r)
                with eng.Fori(1, NB - 1) as n:
                    for r in range(RING):
                        half(RING * n + r, n, r)
                for r in range(RING):
                    half(RING * (NB - 1) + r, NB - 1, r)

            @block.scalar
            def _(act):
                def half(k, n, r):
                    started = not (isinstance(k, int) and k == 0)
                    act.wait_ge(resT_made, k + 1)
                    if started:
                        act.wait_ge(scanned, k)
                    nc.scalar.activation(resT[:, :], resT_ps[:, :], ACT.Copy).then_inc(resT_copied, 1)
                    if started:
                        act.wait_ge(edge_made, k)
                    for g in range(2):
                        act.wait_ge(ohT_made, 2 * k + g + 1)
                        nc.scalar.activation(onehotT[:, 2 * g:2 * g + 2, :].rearrange("p j c -> p (j c)"), ohT_ps[:, g, :],
                                             ACT.Copy).then_inc(onehotT_copied, 1)
                    if not isinstance(k, int) or k >= RING:
                        act.wait_ge(summed, HS * (k - RING + 1))
                    nc.scalar.activation(onehot[:, r, :, :, :].rearrange("p j t c -> p (j t c)"),
                                         onehot16[:, :, :, :].rearrange("p j t c -> p (j t c)"),
                                         ACT.Copy).then_inc(onehot_copied, 1)
                    act.wait_ge(shrink_in, k + 1)
                    nc.scalar.activation(shrink[:, r, :, :].rearrange("p j h -> p h j"), shrink_x[:, :, :], ACT.Exp).then_inc(shrink_made, 1)
                    act.wait_ge(score_made, k + 1)
                    nc.scalar.activation(wgt[:, r, :, :, :], score[:, :, :, :], ACT.Exp).then_inc(weights_made, 1)

                def zero_places(n):
                    act.dma_start(xs.rearrange("(p r) d -> p r d", p=P)[:, bass.ds(n * ZROWS, ZROWS), :],
                                  zeros[:, :].unsqueeze(1).to_broadcast([P, ZROWS, D])).then_inc(xs_zeroed, 16)

                for r in range(RING):
                    half(r, 0, r)
                with act.Fori(1, 1 + ZTURNS) as n:
                    zero_places(n - 1)
                    for r in range(RING):
                        half(RING * n + r, n, r)
                with act.Fori(1 + ZTURNS, NB) as n:
                    for r in range(RING):
                        half(RING * n + r, n, r)
                act.wait_ge(xs_zeroed, 16 * ZTURNS)

            @block.tensor
            def _(pe):
                def add_rows(s, j, rr):
                    pe.wait_ge(rows_weighted, s + 1)
                    if not isinstance(s, int) or s >= 2:
                        pe.wait_ge(merged, s - 1)
                    for t in range(T):
                        last = nc.tensor.matmul(sum_ps[:, j % 2, 0:ROW], onehot[:, rr, j, t, :],
                                                wrow[:, j, t, :, :].rearrange("p h c -> p (h c)"),
                                                start=(t == 0), stop=(t == T - 1))
                    last.then_inc(summed, 1)

                def transpose_maxima(k, r):
                    pe.wait_ge(a_s_staged, k + 1)
                    for t in range(T):
                        last = nc.tensor.transpose(asT_ps[:, t:T * P:T], a_s[:, r, t, :, :].rearrange("p j h -> p (j h)"), ident[:, :])
                    last.then_inc(asT_made, 1)
                    pe.wait_ge(resets_made, k + 1)
                    if not (isinstance(k, int) and k == 0):
                        pe.wait_ge(resT_copied, k)
                    for t in range(T):
                        last = nc.tensor.transpose(resT_ps[:, t:T * P:T], resets[:, t, :, :].rearrange("p j h -> p (j h)"),
                                                   ident[:, :])
                    last.then_inc(resT_made, 1)

                def half(k, n, r):
                    prev = not (isinstance(k, int) and k == 0)
                    rr = (r - 1) % RING
                    s = HS * k - HS
                    pe.wait_ge(onehot_made, k + 1)
                    for g in range(2):
                        for j in (2 * g, 2 * g + 1):
                            for t in range(T):
                                c = (j % 2) * T * P + t * P
                                last = nc.tensor.transpose(ohT_ps[:, g, c:c + P], onehot16[:, j, t, :], ident16[:, :])
                        last.then_inc(ohT_made, 1)
                    pe.wait_ge(asT_made, 1)
                    pe.wait_ge(scanned, k + 1)
                    for t in range(T):
                        last = nc.tensor.transpose(back_ps[:, t * HB:(t + 1) * HB], runmax[:, t:T * P:T], ident[0:HB, 0:HB])
                    last.then_inc(back_made, 1)
                    if prev:
                        pe.wait_ge(onehot_copied, k)
                        add_rows(s, 0, rr)
                    pe.wait_ge(seg_made, k + 1)
                    for j in range(HS):
                        for t in range(T):
                            for v in range(3):
                                last = nc.tensor.matmul(win_ps[:, j, :], onehot16[:, j, t, :], seg16[:, j, t, v, :],
                                                        start=(t == 0 and v == 0), stop=(t == T - 1 and v == 2))
                    last.then_inc(win_made, 1)
                    if prev:
                        add_rows(s + 1, 1, rr)
                    pe.wait_ge(cur_made, k + 1)
                    pe.wait_ge(onehotT_copied, 2 * k + 2)
                    for j in range(HS):
                        for t in range(T):
                            c = (j * T + t) * D8
                            for v in range(3):
                                last = nc.tensor.matmul(edge_ps[:, c:c + D8], onehotT[:, j, t * P:(t + 1) * P],
                                                        cur16[:, j, v, :], start=(v == 0), stop=(v == 2))
                    last.then_inc(edge_made, 1)
                    if prev:
                        add_rows(s + 2, 2, rr)
                    if not (isinstance(k, int) and k == NH - 1):
                        transpose_maxima(k + 1, (r + 1) % RING)
                    if prev:
                        add_rows(s + 3, 3, rr)

                transpose_maxima(0, 0)
                turns(pe, half)
                pe.wait_ge(onehot_copied, NH)
                for j in range(HS):
                    add_rows(HS * (NH - 1) + j, j, (NH - 1) % RING)

            @block.vector
            def _(dve):
                link = chain(dve, marks_set)
                nc.vector.memset(seg16[:, :, :, :, H], 0.0)
                nc.vector.memset(old[:, :, 0], -BIG)
                nc.vector.memset(wreset[:, 0:1], 0.0)
                nc.vector.tensor_copy(iota16[:, :], iota_row[:, :])
                link(nc.vector.tensor_scalar(last_col[:, :], iota_col[:, :], float(P - 1), None, ALU.is_equal))
                link(nc.vector.memset(last_edge[:, :, :], 0.0))
                nc.vector.tensor_copy(last_edge[:, :, T - 1], last_col[:, 0:1].to_broadcast([P, HS]))
                link(nc.vector.tensor_tensor(wreset[:, 1:], wbase[:, 1:NS], wbase[:, 0:NS - 1], ALU.not_equal))
                link(nc.vector.tensor_scalar(wreset[:, :], wreset[:, :], -BIG, None, ALU.mult))
                link(nc.vector.memset(wreset[:, 0:NS:HS], -BIG))

                def edge_marks(k, n, r, link):
                    dve.wait_ge(edges_loaded[r], 256 * (n + 1))
                    base = wbase[:, bass.ds(HS * k, HS)].unsqueeze(2).to_broadcast([P, HS, T])
                    nc.vector.tensor_tensor(dloc[:, r, :, :], dst_t[:, 1, r, :, :], base, ALU.subtract)
                    nc.vector.tensor_tensor(ends[:, r, :, :], dst_t[:, 1, r, :, :], dst_t[:, 2, r, :, :], ALU.not_equal)
                    link(nc.vector.tensor_tensor(begins[:, :, :], dst_t[:, 1, r, :, :], dst_t[:, 0, r, :, :], ALU.not_equal))
                    nc.vector.tensor_scalar(resets[:, :, :, :],
                                            begins[:, :, :].rearrange("p j t -> p t j").unsqueeze(3).to_broadcast([P, T, HS, H]),
                                            -BIG, None, ALU.mult).then_inc(resets_made, 1)
                    nc.vector.tensor_tensor(ends[:, r, :, :], ends[:, r, :, :], last_edge[:, :, :], ALU.max)
                    copied(reset_j[:, :, :], wreset[:, bass.ds(HS * k, HS)].unsqueeze(1).to_broadcast([P, H, HS]))
                    if not (isinstance(k, int) and k == 0):
                        dve.wait_ge(onehot_copied, k)
                    for j in range(HS):
                        for t in range(T):
                            last = nc.vector.tensor_scalar(onehot16[:, j, t, :], iota16[:, :], dloc[:, r, j, t:t + 1],
                                                           None, ALU.is_equal)
                    last.then_inc(onehot_made, 1)

                def stage_and_mark(k, n, r, link):
                    dve.wait_ge(rows_gathered[r], 256 * (n + 1))
                    nc.vector.tensor_copy(a_s[:, r, :, :, :].rearrange("p t j h -> p j t h"),
                                          gat[:, r, :, :, :, HD]).then_inc(a_s_staged, 1)
                    edge_marks(k, n, r, link)

                def weight_rows(s, j, rr):
                    if not isinstance(s, int) or s >= HS:
                        dve.wait_ge(summed, s - HS + 1)
                    w_e = wgt[:, rr, j, :, :]
                    nc.vector.scalar_tensor_tensor(wrow[:, j, :, :, 0:HD], w_e.unsqueeze(3).to_broadcast([P, T, H, HD]), 1.0,
                                                   gat[:, rr, j, :, :, 0:HD], ALU.min, ALU.mult)
                    nc.vector.tensor_scalar(wrow[:, j, :, :, HD], w_e, 1.0, None, ALU.min).then_inc(rows_weighted, 1)

                def merge(s, j, rr, w):
                    dve.wait_ge(summed, s + 1)
                    if not isinstance(s, int) or s >= 1:
                        dve.wait_ge(merged, s)
                    for h in range(H):
                        cols = slice(h * (HD + 1), (h + 1) * (HD + 1))
                        a = acc[:, bass.ds(w, 1), cols].rearrange("p o c -> p (o c)")
                        last = nc.vector.scalar_tensor_tensor(a, a, shrink[:, rr, j, h:h + 1], sum_ps[:, j % 2, cols],
                                                              ALU.mult, ALU.add)
                    last.then_inc(merged, 1)

                win_regs = [[dve.alloc_register(f"win{r}_{j}") for j in range(HS)] for r in range(RING)]

                def windows(r):
                    return [dve.snap(reg, min_val=0, max_val=NW) for reg in win_regs[r]]

                def half(k, n, r, link):
                    prev = not (isinstance(k, int) and k == 0)
                    rr = (r - 1) % RING
                    s = HS * k - HS
                    by_head = "p j h -> p h j"
                    dve.wait_ge(asT_made, k + 1)
                    dve.wait_ge(resT_copied, k + 1)
                    nc.vector.tensor_tensor_scan(runmax[:, :], resT[:, :], asT_ps[:, :], -BIG, ALU.add, ALU.max
                                                 ).then_inc(scanned, 1)
                    if prev:
                        dve.wait_ge(weights_made, k)
                        weight_rows(s, 0, rr)
                    dve.wait_ge(back_made, k + 1)
                    nc.vector.tensor_copy(seg16[:, :, :, 0, H], ends[:, r, :, :])
                    link(nc.vector.tensor_tensor(seg[:, :, :, :], back_ps.rearrange("p (t j h) -> p j t h", t=T, j=HS),
                                                 ends[:, r, :, :].unsqueeze(3).to_broadcast([P, HS, T, H]), ALU.mult))
                    link(nc.vector.tensor_copy(seg16[:, :, :, 0, 0:H], seg[:, :, :, :]))
                    link(nc.vector.tensor_tensor(seg_r[:, :, :, :], seg[:, :, :, :], seg16[:, :, :, 0, 0:H], ALU.subtract))
                    link(nc.vector.tensor_copy(seg16[:, :, :, 1, 0:H], seg_r[:, :, :, :]))
                    nc.vector.tensor_tensor(seg16[:, :, :, 2, 0:H], seg_r[:, :, :, :], seg16[:, :, :, 1, 0:H],
                                            ALU.subtract).then_inc(seg_made, 1)
                    dve.load(win_regs[r], win_i[0:1, bass.ds(HS * k, HS)])
                    mine = windows(r)
                    wins = windows(rr)
                    if prev:
                        weight_rows(s + 1, 1, rr)
                    for j in range(HS):
                        last = copied(known[:, j, :], dm[:, bass.ds(mine[j], 1), :].rearrange("p o c -> p (o c)"))
                    link(last)
                    nc.vector.tensor_copy(cur[:, :, 0:H], known[:, :, 0:H])
                    if prev:
                        dve.wait_ge(shrink_made, k)
                        merge(s, 0, rr, wins[0])
                    dve.wait_ge(win_made, k + 1)
                    nc.vector.tensor_scalar(absent[:, :], win_ps[:, :, H], BIG, -BIG, ALU.mult, ALU.add)
                    link(nc.vector.tensor_tensor(cand[:, :, :], win_ps[:, :, 0:H], known[:, :, 0:H], ALU.add))
                    link(nc.vector.tensor_tensor(cand2[:, :, :], cand[:, :, :],
                                                 absent[:, :].unsqueeze(2).to_broadcast([P, HS, H]), ALU.add))
                    link(nc.vector.scalar_tensor_tensor(cand[:, :, :], cand2[:, :, :], SLOPE, cand2[:, :, :], ALU.mult, ALU.max))
                    link(nc.vector.tensor_tensor(best[:, :, :], cand[:, :, :].rearrange(by_head),
                                                 known[:, :, H:].rearrange(by_head), ALU.max))
                    link(nc.vector.tensor_tensor_scan(highest[:, :, :].rearrange("p h j -> p (h j)"),
                                                      reset_j[:, :, :].rearrange("p h j -> p (h j)"),
                                                      best[:, :, :].rearrange("p h j -> p (h j)"), -BIG, ALU.add, ALU.max))

                    def keep(j):
                        return copied(dm[:, bass.ds(mine[j], 1), H:].rearrange("p o c -> p (o c)"), highest[:, :, j])

                    nc.vector.tensor_copy(cur[:, :, H:].rearrange(by_head), highest[:, :, :])
                    keep(0)
                    link(nc.vector.tensor_tensor(old[:, :, 1:], highest[:, :, 0:HS - 1], reset_j[:, :, 1:], ALU.add))
                    nc.vector.tensor_copy(cur16[:, :, 0, :], cur[:, :, :])
                    keep(1)
                    link(nc.vector.tensor_tensor(best[:, :, :], old[:, :, :], known[:, :, H:].rearrange(by_head), ALU.max))
                    nc.vector.tensor_tensor(shrink_x[:, :, :], best[:, :, :], highest[:, :, :], ALU.subtract).then_inc(shrink_in, 1)
                    keep(2)
                    link(nc.vector.tensor_tensor(cur_r[:, :, :], cur[:, :, :], cur16[:, :, 0, :], ALU.subtract))
                    nc.vector.tensor_copy(cur16[:, :, 1, :], cur_r[:, :, :])
                    link(keep(3))
                    nc.vector.tensor_tensor(cur16[:, :, 2, :], cur_r[:, :, :], cur16[:, :, 1, :], ALU.subtract).then_inc(cur_made, 1)
                    if prev:
                        weight_rows(s + 2, 2, rr)
                        merge(s + 1, 1, rr, wins[1])
                        weight_rows(s + 3, 3, rr)
                    dve.wait_ge(edge_made, k + 1)
                    edge = edge_ps[:, 0:HT * D8].rearrange("p (j t c) -> p j t c", j=HS, t=T)
                    link(nc.vector.tensor_tensor(score[:, :, :, :], edge[:, :, :, 0:H],
                                                 a_s[:, r, :, :, :].rearrange("p t j h -> p j t h"), ALU.add))
                    flat = "p j t h -> p (j t h)"
                    link(nc.vector.scalar_tensor_tensor(score2[:, :, :, :].rearrange(flat), score[:, :, :, :].rearrange(flat), SLOPE,
                                                        score[:, :, :, :].rearrange(flat), ALU.mult, ALU.max))
                    nc.vector.tensor_tensor(score[:, :, :, :], score2[:, :, :, :], edge[:, :, :, H:], ALU.subtract).then_inc(score_made, 1)
                    if not (isinstance(k, int) and k == NH - 1):
                        stage_and_mark(k + 1, n + (r + 1) // RING, (r + 1) % RING, link)
                    if prev:
                        merge(s + 2, 2, rr, wins[2])
                        merge(s + 3, 3, rr, wins[3])

                before_loop = 1 + RING * LINKS
                link = chain(dve, seq)
                stage_and_mark(0, 0, 0, link)
                for r in range(RING):
                    half(r, 0, r, link)
                assert link.count[0] == before_loop, link.count
                with dve.Fori(1, NB - 1) as n:
                    link = chain(dve, seq, base=(n - 1) * (RING * LINKS) + before_loop)
                    for r in range(RING):
                        half(RING * n + r, n, r, link)
                link = chain(dve, seq, base=before_loop + (NB - 2) * RING * LINKS)
                for r in range(RING):
                    half(RING * (NB - 1) + r, NB - 1, r, link)
                wins = windows(RING - 1)
                s, rr = HS * (NH - 1), (NH - 1) % RING
                dve.wait_ge(weights_made, NH)
                dve.wait_ge(shrink_made, NH)
                weight_rows(s, 0, rr)
                weight_rows(s + 1, 1, rr)
                for j in range(HS):
                    merge(s + j, j, rr, wins[j])
                    if j + 2 < HS:
                        weight_rows(s + j + 2, j + 2, rr)

        with ExitStack() as st:
            sb, ps, sem = allot(st)
            xn = sb("xn", [P, NW, D])
            rden = sb("rden", [P, NW, H])
            gb = sb("gb", [P, D])
            brb = sb("brb", [P, NE])
            wr = sb("wr", [P, KD, NE])
            stat = sb("stat2", [P, NW, 6])
            mv = sb("mv2", [P, 2, NW, 2])
            mtmp = sb("mtmp2", [P, 2, NW])
            rstd = sb("rstd2", [P, 2, NW])
            xt_st = sb("xt_st", [P, 2, D])
            xT = sb("xtT", [P, 2, D])
            logit = sb("logit", [P, NW, NE])
            top = sb("top", [P, 2, NW])
            number = sb("number", [P, NE])
            equal = sb("equal", [P, NW, NE])
            rest = sb("rest", [P, NW, NE])
            chosen = sb("chosen", [P, NW])
            diff = sb("diff", [P, NW])
            gate = sb("gate", [P, NW])
            gate_d = sb("gate_d", [P, NW])
            pick = [sb(f"pick{k}", [P, NW, NE]) for k in range(2)]
            real = sb("real", [P, 1])
            both = sb("both", [P, NW, NE])
            total = sb("total", [P, NW, NE])
            upto = sb("upto", [P, NW, NE])
            place = sb("place", [P, NW, NE])
            placed = sb("placed", [P, NW, NE])
            posf = sb("posf", [P, NW])
            zero = sb("zero2", [P, NW])
            need = sb("need", [P, NE])
            need_i = sb("need_i", [P, NE], I32)
            need_c = sb("need_c", [P, NE])
            slot0 = sb("slot0", [P, NE])
            owner = sb("owner", [1, SLOTS, NE])
            owner_s = sb("owner_s", [1, SLOTS])
            xT_ps = ps("xtT_ps", [P, 2, 512])
            lg_ps = ps("lg_ps", [P, 2, 512])
            rank_ps = ps("rank_ps", [P, 512])
            total_ps = ps("total_ps", [P, 512])
            x_loaded = [sem(f"x_again{g}") for g in range(NG + 1)]
            small_loaded = sem("small_loaded")
            pad_zeroed = sem("pad_zeroed2")
            seq = sem("norm_seq")
            added = sem("added")
            biased = sem("biased")
            var_ready = [sem(f"var_ready{v}") for v in range(2)]
            std_ready = [sem(f"std_ready{v}") for v in range(2)]
            xt_ready = sem("xt_ready")
            xT_made = sem("xtT_made")
            xT_copied = sem("xtT_copied")
            lg_made = sem("lg_made")
            lg_taken = sem("lg_taken")
            gate_in = sem("gate_in")
            gate_made = sem("gate_made")
            both_made = sem("both_made")
            ranked = sem("ranked")
            xn_ready = sem("xn_ready2")
            pos_ready = sem("pos_ready")
            scattered = sem("scattered")
            block = st.enter_context(nc.Block())
            acc_rows = lambda w: acc[:, bass.ds(w, 1), :].rearrange("p o (h c) -> p (o h) c", h=H)[:, :, 0:HD]
            row = lambda a, w: a[:, bass.ds(w, 1), :].rearrange("p o c -> p (o c)")
            xt_row = lambda w: acc[:, bass.ds(w, 1), 0:D].rearrange("p o c -> p (o c)")

            @block.sync
            def _(sp):
                sp.dma_start(gb[:, :], gbias.partition_broadcast(P)).then_inc(small_loaded, 16)
                sp.dma_start(brb[:, :], br.partition_broadcast(P)).then_inc(small_loaded, 16)
                sp.dma_start(wr[:, :, :], Wr.rearrange("(k p) e -> p k e", p=P)).then_inc(small_loaded, 16)
                sp.wait_ge(pad_zeroed, 1)
                load_nodes(sp, x_loaded)

            @block.gpsimd
            def _(pool):
                pool.wait_ge(small_loaded, 48)

                def add_bias(w):
                    pool.wait_ge(added, w + 1)
                    nc.gpsimd.tensor_tensor(row(node_rows, w), row(node_rows, w), gb[:, :], ALU.add).then_inc(biased, 1)

                each_window(pool, add_bias)
                pool.wait_ge(pos_ready, 1)
                for w in range(NW):
                    n = LAST if w == NW - 1 else P
                    pool.wait_ge(xn_ready, w + 1)
                    for k in range(2):
                        pool.indirect_dma_start(xs, bass.IndirectOffsetOnAxis(ap=pos[k][0:n, w:w + 1], axis=0),
                                                xn[0:n, w, :], None).then_inc(scattered, 16)
                pool.wait_ge(scattered, 16 * 2 * NW)

            @block.scalar
            def _(act):
                act.wait_ge(var_ready[0], 1)
                nc.scalar.activation(rstd[:, 0, :], mv[:, 0, :, 1], ACT.Sqrt, bias=eps_col[:, 0:1]).then_inc(std_ready[0], 1)

                def copy_xT(w, b):
                    act.wait_ge(xT_made, w + 1)
                    nc.scalar.activation(xT[:, b, :], xT_ps[:, b, 0:D], ACT.Copy).then_inc(xT_copied, 1)

                with act.Fori(0, NW // 2) as i:
                    for b in range(2):
                        copy_xT(2 * i + b, b)
                copy_xT(NW - 1, 0)
                act.wait_ge(gate_in, 1)
                nc.scalar.activation(gate[:, :], diff[:, :], ACT.Exp).then_inc(gate_made, 1)
                act.wait_ge(var_ready[1], 1)
                nc.scalar.activation(rstd[:, 1, :], mv[:, 1, :, 1], ACT.Sqrt, bias=eps_col[:, 0:1]).then_inc(std_ready[1], 1)

            @block.tensor
            def _(pe):
                def transpose(w, b):
                    pe.wait_ge(xt_ready, w + 1)
                    for k in range(KD):
                        last = nc.tensor.transpose(xT_ps[:, b, k * P:(k + 1) * P], xt_st[:, b, k * P:(k + 1) * P], ident[:, :])
                    last.then_inc(xT_made, 1)

                def product(w, b, reused=True):
                    pe.wait_ge(xT_copied, w + 1)
                    if reused:
                        pe.wait_ge(lg_taken, w - 1)
                    for k in range(KD):
                        last = nc.tensor.matmul(lg_ps[:, b, 0:NE], xT[:, b, k * P:(k + 1) * P], wr[:, k, :],
                                                start=(k == 0), stop=(k == KD - 1))
                    last.then_inc(lg_made, 1)

                pe.wait_ge(small_loaded, 48)
                transpose(0, 0)
                transpose(1, 1)
                product(0, 0, reused=False)
                transpose(2, 0)
                product(1, 1, reused=False)
                with pe.Fori(1, NW // 2) as i:
                    for b in range(2):
                        transpose(2 * i + b + 1, 1 - b)
                        product(2 * i + b, b)
                product(NW - 1, 0)
                pe.wait_ge(both_made, 1)
                flat = both[:, :, :].rearrange("p w e -> p (w e)")
                nc.tensor.matmul(rank_ps[:, 0:NW * NE], before[:, :], flat, start=True, stop=True)
                nc.tensor.matmul(total_ps[:, 0:NW * NE], ones[:, :], flat, start=True, stop=True).then_inc(ranked, 1)

            @block.vector
            def _(dve):
                link = chain(dve, seq)
                nc.vector.memset(node_rows[:, NW - 1, :], 0.0).then_inc(pad_zeroed, 1)
                nc.vector.memset(zero[:, :], 0.0)
                link(nc.vector.reciprocal(rden[:, :, :], acc[:, 0:NW, :].rearrange("p w (h c) -> p w h c", h=H)[:, :, :, HD]))
                each_window(dve, lambda w: nc.vector.tensor_tensor(
                    acc_rows(w), acc_rows(w), rden[:, bass.ds(w, 1), :].rearrange("p o h -> p (o h)").unsqueeze(2)
                    .to_broadcast([P, H, HD]), ALU.mult))
                link(nc.vector.memset(tick[:, :], 0.0))

                def add_x(w):
                    r4 = row(node_rows, w).rearrange("p (h c) -> p h c", h=H)
                    nc.vector.tensor_tensor(r4, r4, acc_rows(w), ALU.add).then_inc(added, 1)

                for g in range(NG + 1):
                    dve.wait_ge(x_loaded[g], 16)
                    each_window(dve, add_x, g * GW, min(GW, NW - g * GW))

                def row_statistics(w):
                    dve.wait_ge(biased, w + 1)
                    nc.vector.bn_stats(row(stat, w), row(node_rows, w))

                def find_moments(v):
                    link(nc.vector.memset(tick[:, :], 0.0))
                    moments(link, mv[:, v, :, 0], mv[:, v, :, 1], stat, mtmp).then_inc(var_ready[v], 1)

                def find_scale(v):
                    dve.wait_ge(std_ready[v], 1)
                    link(nc.vector.reciprocal(rstd[:, v, :], rstd[:, v, :]))

                def scaled(out_ap, in_ap, v, w):
                    return nc.vector.tensor_scalar(out_ap, in_ap, mv[:, v, bass.ds(w, 1), 0], rstd[:, v, bass.ds(w, 1)],
                                                   ALU.subtract, ALU.mult)

                each_window(dve, row_statistics)
                find_moments(0)
                find_scale(0)

                def take_xt(w, b, reused=True):
                    if reused:
                        dve.wait_ge(xT_made, w - 1)
                    scaled(xt_st[:, b, :], row(node_rows, w), 0, w).then_inc(xt_ready, 1)
                    scaled(xt_row(w), row(node_rows, w), 0, w)

                def take_logits(w, b):
                    dve.wait_ge(xt_ready, w + (1 if isinstance(w, int) and w == NW - 1 else 2))
                    nc.vector.bn_stats(row(stat, w), xt_row(w))
                    dve.wait_ge(lg_made, w + 1)
                    nc.vector.tensor_tensor(row(logit, w), lg_ps[:, b, 0:NE], brb[:, :], ALU.add).then_inc(lg_taken, 1)

                dve.wait_ge(small_loaded, 48)
                take_xt(0, 0, reused=False)
                take_xt(1, 1, reused=False)
                with dve.Fori(1, NW // 2) as i:
                    for b in range(2):
                        take_xt(2 * i + b, b)
                        take_logits(2 * i + b - 2, b)
                take_xt(NW - 1, 0)
                take_logits(NW - 3, 0)
                take_logits(NW - 2, 1)
                link(nc.vector.memset(tick[:, :], 0.0))
                take_logits(NW - 1, 0)
                find_moments(1)

                of_rows = lambda a: a.unsqueeze(2).to_broadcast([P, NW, NE])
                nc.vector.tensor_scalar(real[:, :], iota_col[:, :], float(LAST), None, ALU.is_lt)
                link(nc.vector.tensor_scalar(number[:, :], iota_row[:, 0:NE], -float(NE), None, ALU.add))
                numbers = number[:, :].unsqueeze(1).to_broadcast([P, NW, NE])
                left = logit
                for k in range(2):
                    link(nc.vector.tensor_reduce(top[:, k, :], left[:, :, :], X, ALU.max))
                    link(nc.vector.tensor_tensor(equal[:, :, :], left[:, :, :], of_rows(top[:, k, :]), ALU.is_equal))
                    link(nc.vector.tensor_tensor(equal[:, :, :], equal[:, :, :], numbers, ALU.mult))
                    link(nc.vector.tensor_reduce(chosen[:, :], equal[:, :, :], X, ALU.min))
                    link(nc.vector.tensor_tensor(pick[k][:, :, :], numbers, of_rows(chosen[:, :]), ALU.is_equal))
                    if k == 0:
                        link(nc.vector.scalar_tensor_tensor(rest[:, :, :], pick[0][:, :, :], -BIG, logit[:, :, :], ALU.mult, ALU.add))
                        left = rest
                nc.vector.tensor_tensor(diff[:, :], top[:, 1, :], top[:, 0, :], ALU.subtract).then_inc(gate_in, 1)
                for k in range(2):
                    last = nc.vector.tensor_scalar(pick[k][:, NW - 1, :], pick[k][:, NW - 1, :], real[:, 0:1], None, ALU.mult)
                link(last)
                nc.vector.tensor_tensor(both[:, :, :], pick[0][:, :, :], pick[1][:, :, :], ALU.add).then_inc(both_made, 1)
                dve.wait_ge(gate_made, 1)
                link(nc.vector.tensor_scalar(gate_d[:, :], gate[:, :], 1.0, None, ALU.add))
                link(nc.vector.reciprocal(wt[0][:, :], gate_d[:, :]))
                nc.vector.tensor_tensor(wt[1][:, :], gate[:, :], wt[0][:, :], ALU.mult)
                dve.wait_ge(ranked, 1)
                link(nc.vector.tensor_copy(total[:, :, :].rearrange("p w e -> p (w e)"), total_ps[:, 0:NW * NE]))
                for e in range(NE):
                    last = nc.vector.tensor_tensor_scan(upto[:, :, e], total[:, :, e], zero[:, :], 0.0, ALU.add, ALU.add)
                link(last)
                link(nc.vector.tensor_scalar(need_i[:, :], upto[:, NW - 1, :], float(TOK - 1), None, ALU.add))
                link(nc.vector.tensor_scalar(need_i[:, :], need_i[:, :], TOK.bit_length() - 1, None, ALU.arith_shift_right))
                link(nc.vector.tensor_copy(need[:, :], need_i[:, :]))
                link(nc.vector.tensor_tensor_scan(need_c[:, :], need[:, :], zero[:, 0:NE], 0.0, ALU.add, ALU.add))
                link(nc.vector.tensor_tensor(slot0[:, :], need_c[:, :], need[:, :], ALU.subtract))
                link(nc.vector.tensor_tensor(owner[:, :, :], iota_row[0:1, 0:SLOTS].unsqueeze(2).to_broadcast([1, SLOTS, NE]),
                                             slot0[0:1, :].unsqueeze(1).to_broadcast([1, SLOTS, NE]), ALU.is_ge))
                link(nc.vector.tensor_reduce(owner_s[:, :], owner[:, :, :], X, ALU.add))
                nc.vector.tensor_scalar(slot_e[:, :], owner_s[:, :], -1.0, None, ALU.add)
                link(nc.vector.tensor_tensor(place[:, :, :], upto[:, :, :], total[:, :, :], ALU.subtract))
                link(nc.vector.tensor_tensor(place[:, :, :], place[:, :, :],
                                             rank_ps[:, 0:NW * NE].rearrange("p (w e) -> p w e", e=NE), ALU.add))
                link(nc.vector.tensor_scalar(slot0[:, :], slot0[:, :], float(TOK), None, ALU.mult))
                link(nc.vector.tensor_tensor(place[:, :, :], place[:, :, :],
                                             slot0[:, :].unsqueeze(1).to_broadcast([P, NW, NE]), ALU.add))
                for k in range(2):
                    link(nc.vector.tensor_tensor(placed[:, :, :], place[:, :, :], pick[k][:, :, :], ALU.mult))
                    link(nc.vector.tensor_reduce(posf[:, :], placed[:, :, :], X, ALU.add))
                    link(nc.vector.tensor_copy(pos[k][:, :], posf[:, :]))
                nc.vector.memset(tick[:, :], 0.0).then_inc(pos_ready, 1)

                find_scale(1)
                each_window(dve, lambda w: scaled(row(xn, w), xt_row(w), 1, w).then_inc(xn_ready, 1))

        until_experts.close()
        with ExitStack() as st:
            sb, ps, sem = allot(st)
            NT = TOK // P
            NPRM = FC + 2 * KD
            FR = mybir.dt.float32r
            w1_raw = sb("w1_raw", [P, KD, FH])
            w2_raw = sb("w2_raw", [P, FC, D])
            w1_top = sb("w1_top", [P, 2, KD, FH], FR)
            w1_rest = sb("w1_rest", [P, 2, KD, FH], FR)
            w2_top = sb("w2_top", [P, 2, FC, D], FR)
            w2_rest = sb("w2_rest", [P, 2, FC, D], FR)
            prm_sb = sb("prm_sb", [P, 2, NPRM])
            b2_sb = sb("b2_sb", [P, 2, D])
            xin = sb("xin", [P, 2, NT, D])
            xe = sb("xe", [P, KD, TOK])
            xe_top = sb("xe_top", [P, KD, TOK], FR)
            xe_rest = sb("xe_rest", [P, KD, TOK], FR)
            hid = sb("hid", [P, 2, 2, TOK])
            hid_top = sb("hid_top", [P, 2, FC, TOK], FR)
            hid_rest = sb("hid_rest", [P, 2, FC, TOK], FR)
            yo = sb("yo", [P, 2, NT, D])
            xT_ps = ps("xeT_ps", [P, 2, 512])
            hid_ps = ps("hid_ps", [P, 4, 512])
            y_ps = ps("y_ps", [P, 2, 512])
            x_loaded = [sem(f"slot_x_loaded{b}") for b in range(2)]
            w1_loaded = [sem(f"w1_loaded{b}") for b in range(2)]
            w2_loaded = [sem(f"w2_loaded{b}") for b in range(2)]
            stored = [sem(f"y_stored{b}") for b in range(2)]
            w1_split = [sem(f"w1_split{b}") for b in range(2)]
            w2_cut = [sem(f"w2_cut{b}") for b in range(2)]
            w2_split = [sem(f"w2_split{b}") for b in range(2)]
            xT_made = sem("xeT_made")
            xe_raw = sem("xe_raw")
            xe_ready = sem("xe_ready")
            hid_made = sem("hid_made")
            gelu_done = sem("gelu_done")
            hid_cut = sem("hid_cut")
            hid_split = sem("hid_split")
            y_made = sem("y_made")
            y_taken = sem("y_taken")
            sp_waited = sem("sp_waited")
            pool_waited = sem("pool_waited")
            block = st.enter_context(nc.Block())
            HALF = FC // 2

            def slots(eng, slot):
                for b in range(2):
                    slot(b, 0, b, True)
                with eng.Fori(1, SLOTS // 2) as i:
                    for b in range(2):
                        slot(2 * i + b, i, b, False)

            def experts_of(eng, q, new):
                return [eng.value_load(slot_e[0:1, bass.ds(n, 1)], min_val=0, max_val=NE - 1)
                        for n in ([q] if new else [q, q - 2])]

            def on_new_expert(eng, experts, fresh, same):
                if len(experts) == 1:
                    fresh()
                    return
                with eng.If(experts[0] != experts[1]):
                    fresh()
                with eng.If(experts[0] == experts[1]):
                    same()

            def cut_top(top, raw):
                return nc.vector.tensor_copy(top, raw)

            def cut_rest(eng, rest, raw, top):
                return eng.tensor_tensor(rest, raw, top.bitcast(F32), ALU.subtract)

            @block.sync
            def _(sp):
                def slot(q, i, b, new):
                    experts = experts_of(sp, q, new)
                    mine = experts[0]
                    if not new:
                        sp.wait_ge(xT_made, q - 1)
                    sp.dma_start(xin[:, b, :, :], xs[bass.ds(q * TOK, TOK), :].rearrange("(t p) d -> p t d", p=P)).then_inc(x_loaded[b], 16)
                    if not new:
                        sp.wait_ge(y_taken, q - 1)
                    sp.dma_start(prm_sb[:, b, :], prm[bass.ds(mine, 1)].rearrange("o p c -> p (o c)")).then_inc(x_loaded[b], 16)
                    sp.dma_start(b2_sb[:, b, :], b2[bass.ds(mine, 1)].rearrange("o d -> (o d)").partition_broadcast(P)).then_inc(x_loaded[b], 16)

                    if not (isinstance(q, int) and q == 0):
                        sp.wait_ge(w1_split[1 - b], 2 * (i + b))
                        sp.wait_ge(w2_split[1 - b], i + b)
                        sp.sem_inc(sp_waited, 1)

                    def load_expert():
                        one = lambda a: a[bass.ds(mine, 1)]
                        sp.dma_start(w1_raw[:, :, :], one(W1).rearrange("o (k p) f -> p (o k) f", p=P)).then_inc(w1_loaded[b], 16)
                        sp.dma_start(w2_raw[:, :, :], one(W2).rearrange("o (c p) d -> p (o c) d", p=P)).then_inc(w2_loaded[b], 16)

                    def keep_expert():
                        sp.sem_inc(w1_loaded[b], 16)
                        sp.sem_inc(w2_loaded[b], 16)

                    on_new_expert(sp, experts, load_expert, keep_expert)

                slots(sp, slot)

            @block.gpsimd
            def _(pool):
                def split_w2(q, i, b, new):
                    experts = experts_of(pool, q, new)
                    pool.wait_ge(w2_cut[b], i + 1)
                    pool.sem_inc(pool_waited, 1)

                    def fresh():
                        cut_rest(nc.gpsimd, w2_rest[:, b, :, :], w2_raw[:, :, :], w2_top[:, b, :, :]).then_inc(w2_split[b], 1)

                    on_new_expert(pool, experts, fresh, lambda: pool.sem_inc(w2_split[b], 1))

                def store_y(q, b):
                    pool.wait_ge(y_taken, q + 1)
                    pool.dma_start(ys[bass.ds(q * TOK, TOK), :].rearrange("(t p) d -> p t d", p=P), yo[:, b, :, :]).then_inc(stored[b], 16)

                split_w2(0, 0, 0, True)
                split_w2(1, 0, 1, True)
                store_y(0, 0)
                with pool.Fori(1, SLOTS // 2) as i:
                    split_w2(2 * i, i, 0, False)
                    store_y(2 * i - 1, 1)
                    split_w2(2 * i + 1, i, 1, False)
                    store_y(2 * i, 0)
                store_y(SLOTS - 1, 1)
                for b in range(2):
                    pool.wait_ge(stored[b], 16 * (SLOTS // 2))

            @block.scalar
            def _(act):
                def slot(q, i, b, new):
                    for c in range(FC):
                        if c % 2 == 0:
                            act.wait_ge(hid_made, HALF * q + c // 2 + 1)
                            if not (isinstance(q, int) and q == 0 and c < 4):
                                act.wait_ge(hid_split, HALF * q + c // 2 - 1)
                        nc.scalar.activation(hid[:, (c // 2) % 2, c % 2, :], hid_ps[:, c // 2, (c % 2) * TOK:(c % 2 + 1) * TOK], ACT.Gelu,
                                             bias=prm_sb[:, b, c:c + 1]).then_inc(gelu_done, 1)

                slots(act, slot)

            @block.tensor
            def _(pe):
                def product(out_ap, a, b, first, last):
                    (a_top, a_rest), (b_top, b_rest) = a, b
                    nc.tensor.matmul(out_ap, a_top, b_top, start=first, stop=False)
                    nc.tensor.matmul(out_ap, a_rest, b_top, start=False, stop=False)
                    return nc.tensor.matmul(out_ap, a_top, b_rest, start=False, stop=last)

                def transpose(q, i, b):
                    pe.wait_ge(x_loaded[b], 48 * (i + 1))
                    for t in range(NT):
                        for k in range(KD):
                            last = nc.tensor.transpose(xT_ps[:, b, k * TOK + t * P:k * TOK + (t + 1) * P],
                                                       xin[:, b, t, k * P:(k + 1) * P], ident[:, :])
                    last.then_inc(xT_made, 1)

                def slot(q, i, b, new, following=True):
                    pe.wait_ge(xe_ready, q + 1)
                    pe.wait_ge(w1_split[b], 2 * i + 2)
                    for c in range(FC):
                        if c % 2 == 0 and not (isinstance(q, int) and q == 0):
                            pe.wait_ge(gelu_done, FC * q - FC + c + 2)
                        for k in range(KD):
                            chunk = slice(c * P, (c + 1) * P)
                            last = product(hid_ps[:, c // 2, (c % 2) * TOK:(c % 2 + 1) * TOK],
                                           (w1_top[:, b, k, chunk], w1_rest[:, b, k, chunk]),
                                           (xe_top[:, k, :], xe_rest[:, k, :]), k == 0, k == KD - 1)
                        if c % 2:
                            last.then_inc(hid_made, 1)
                    if following:
                        transpose(q + 1, i + b, 1 - b)
                    pe.wait_ge(w2_split[b], i + 1)
                    if not new:
                        pe.wait_ge(y_taken, q - 1)
                    for t in range(NT):
                        for c in range(FC):
                            if t == 0 and c % 2 == 0:
                                pe.wait_ge(hid_split, HALF * q + c // 2 + 1)
                            toks = slice(t * P, (t + 1) * P)
                            last = product(y_ps[:, b, t * D:(t + 1) * D],
                                           (hid_top[:, b, c, toks], hid_rest[:, b, c, toks]),
                                           (w2_top[:, b, c, :], w2_rest[:, b, c, :]), c == 0, c == FC - 1)
                    last.then_inc(y_made, 1)

                transpose(0, 0, 0)
                slot(0, 0, 0, True)
                slot(1, 0, 1, True)
                with pe.Fori(1, SLOTS // 2 - 1) as i:
                    for b in range(2):
                        slot(2 * i + b, i, b, False)
                i = SLOTS // 2 - 1
                slot(2 * i, i, 0, False)
                slot(2 * i + 1, i, 1, False, following=False)

            @block.vector
            def _(dve):
                def take_x(q, b):
                    dve.wait_ge(xT_made, q + 1)
                    for k in range(KD):
                        last = nc.vector.tensor_scalar(xe[:, k, :], xT_ps[:, b, k * TOK:(k + 1) * TOK],
                                                       prm_sb[:, b, FC + k:FC + k + 1], prm_sb[:, b, FC + KD + k:FC + KD + k + 1],
                                                       ALU.mult, ALU.add)
                    last.then_inc(xe_raw, 1)
                    dve.wait_ge(xe_raw, 2 * q + 1)
                    cut_top(xe_top[:, :, :], xe[:, :, :]).then_inc(xe_raw, 1)
                    dve.wait_ge(xe_raw, 2 * q + 2)
                    cut_rest(nc.vector, xe_rest[:, :, :], xe[:, :, :], xe_top[:, :, :]).then_inc(xe_ready, 1)

                def split_weights(q, i, b, new):
                    def fresh():
                        dve.wait_ge(w1_loaded[b], 16 * (i + 1))
                        cut_top(w1_top[:, b, :, :], w1_raw[:, :, :]).then_inc(w1_split[b], 1)
                        dve.wait_ge(w1_split[b], 2 * i + 1)
                        cut_rest(nc.vector, w1_rest[:, b, :, :], w1_raw[:, :, :], w1_top[:, b, :, :]).then_inc(w1_split[b], 1)
                        dve.wait_ge(w2_loaded[b], 16 * (i + 1))
                        cut_top(w2_top[:, b, :, :], w2_raw[:, :, :]).then_inc(w2_cut[b], 1)

                    def same():
                        dve.wait_ge(w1_loaded[b], 16 * (i + 1))
                        dve.sem_inc(w1_split[b], 2)
                        dve.wait_ge(w2_loaded[b], 16 * (i + 1))
                        dve.sem_inc(w2_cut[b], 1)

                    on_new_expert(dve, experts_of(dve, q, new), fresh, same)

                def split_hidden(q, b):
                    for g in range(HALF):
                        n = HALF * q + g + 1
                        dve.wait_ge(gelu_done, 2 * n)
                        pair = slice(2 * g, 2 * g + 2)
                        raw = hid[:, g % 2, :, :]
                        cut_top(hid_top[:, b, pair, :], raw).then_inc(hid_cut, 1)
                        dve.wait_ge(hid_cut, n)
                        cut_rest(nc.vector, hid_rest[:, b, pair, :], raw, hid_top[:, b, pair, :]).then_inc(hid_split, 1)

                def take_y(q, i, b, new):
                    dve.wait_ge(y_made, q + 1)
                    if not new:
                        dve.wait_ge(stored[b], 16 * i)
                    nc.vector.tensor_tensor(yo[:, b, :, :], y_ps[:, b, :].rearrange("p (t d) -> p t d", t=NT),
                                            b2_sb[:, b, :].unsqueeze(1).to_broadcast([P, NT, D]), ALU.add).then_inc(y_taken, 1)

                def slot(q, i, b, new, following=True, early=False):
                    split_hidden(q, b)
                    if following:
                        take_x(q + 1, 1 - b)
                        if not early:
                            split_weights(q + 1, i + b, 1 - b, False)
                    take_y(q, i, b, new)

                split_weights(0, 0, 0, True)
                take_x(0, 0)
                split_weights(1, 0, 1, True)
                slot(0, 0, 0, True, early=True)
                slot(1, 0, 1, True)
                with dve.Fori(1, SLOTS // 2 - 1) as i:
                    for b in range(2):
                        slot(2 * i + b, i, b, False)
                i = SLOTS // 2 - 1
                slot(2 * i, i, 0, False)
                slot(2 * i + 1, i, 1, False, following=False)

        with ExitStack() as st:
            sb, ps, sem = allot(st)
            CR = 4
            y_g = sb("y_g", [P, CR, 2, D])
            gathered = [sem(f"gathered{r}") for r in range(CR)]
            first_added = sem("first_added")
            done = sem("done")
            stored = sem("out_stored")
            block = st.enter_context(nc.Block())
            rows = lambda w: LAST if w == NW - 1 else P

            @block.gpsimd
            def _(pool):
                for w in range(NW):
                    if w >= CR:
                        pool.wait_ge(done, w - CR + 1)
                    for k in range(2):
                        pool.indirect_dma_start(y_g[0:rows(w), w % CR, k, :], None, ys,
                                                bass.IndirectOffsetOnAxis(ap=pos[k][0:rows(w), w:w + 1], axis=0)
                                                ).then_inc(gathered[w % CR], 16)

            @block.vector
            def _(dve):
                def add(w):
                    n = rows(w)
                    dve.wait_ge(gathered[w % CR], 32 * (w // CR + 1))
                    x1 = node_rows[0:n, w, :]
                    nc.vector.scalar_tensor_tensor(x1, y_g[0:n, w % CR, 0, :], wt[0][0:n, w:w + 1], x1,
                                                   ALU.mult, ALU.add).then_inc(first_added, 1)
                    dve.wait_ge(first_added, w + 1)
                    nc.vector.scalar_tensor_tensor(x1, y_g[0:n, w % CR, 1, :], wt[1][0:n, w:w + 1], x1,
                                                   ALU.mult, ALU.add).then_inc(done, 1)

                for w in range(NW):
                    add(w)

            @block.sync
            def _(sp):
                for g in range(NG):
                    sp.wait_ge(done, (g + 1) * GW)
                    sp.dma_start(out[g * GW * P:(g + 1) * GW * P, :].rearrange("(w p) d -> p w d", p=P),
                                 node_rows[:, g * GW:(g + 1) * GW, :]).then_inc(stored, 16)
                sp.wait_ge(done, NW)
                sp.dma_start(out[(NW - 1) * P:N, :], node_rows[0:LAST, NW - 1, :]).then_inc(stored, 16)
                sp.wait_ge(stored, 16 * (NG + 1))


_INS = ['x', 'src', 'dst', 'L0_gnn_W', 'L0_gnn_att_src', 'L0_gnn_att_dst', 'L0_gnn_bias', 'L0_ffn_Wr', 'L0_ffn_br',
        'L0_ffn_ln_g', 'L0_ffn_ln_b', 'L0_ffn_W1', 'L0_ffn_b1', 'L0_ffn_W2', 'L0_ffn_b2']


def kernel(**inputs):
    import numpy as _np
    import concourse.bacc as _bacc
    from concourse import mybir as _mybir
    from concourse.bass_utils import run_bass_kernel_spmd as _run

    nc = _bacc.Bacc("TRN2", target_bir_lowering=False, num_devices=1)
    arrays, args = {}, []
    for name in _INS:
        a = _np.ascontiguousarray(inputs[name])
        arrays[f"in_{name}"] = a
        args.append(nc.dram_tensor(f"in_{name}", a.shape, _mybir.dt.from_np(a.dtype), kind="ExternalInput").ap())
    out = nc.dram_tensor("out_x", inputs["x"].shape, _mybir.dt.float32, kind="ExternalOutput").ap()
    gat_moe(nc, *args, out)
    r = _run(nc, [arrays], core_ids=[0])
    return r.results[0]["out_x"]
```

```python
from contextlib import ExitStack

import concourse.bass as bass
from concourse import mybir

F32 = mybir.dt.float32
I32 = mybir.dt.int32
U32 = mybir.dt.uint32
BF16 = mybir.dt.bfloat16
ALU = mybir.AluOpType
ACT = mybir.ActivationFunctionType
X = mybir.AxisListType.X

P = 128
EPS = 1e-5
SLOPE = 0.2
BIG = 1e30
T = 4
STEP = T * P
HS = 4
RING = 3
TOK = 256


def gat_moe(nc, x, src, dst, gW, att_src, att_dst, gbias, Wr, br, ln_g, ln_b, W1, b1, W2, b2, out):
    N, D = x.shape
    E = src.shape[0]
    H, HD = att_src.shape
    NE = Wr.shape[1]
    FH = W1.shape[2]
    KD = D // P
    FC = FH // P
    NW = -(-N // P)
    LAST = N - (NW - 1) * P
    ROW = H * (HD + 1)
    TROW = ROW + H
    steps_bound = (E + NW * (STEP - 1)) // STEP
    NH = -(-steps_bound // HS)
    NS = NH * HS
    PAIRS = 2 * N
    SLOTS = (PAIRS + NE * (TOK - 1)) // TOK
    PLACES = SLOTS * TOK
    NCNT = NW + 1
    PAIRED = NW // 2
    GW = 6
    NG = (NW - 1) // GW
    assert NG * GW == NW - 1
    EP, EC = 125, E // 125
    assert EP * EC == E and D == KD * P and NS <= 2 * P and SLOTS % 2 == 0 and NW % 4 == 1 and NW % 7 == 0

    dst_pad = nc.dram_tensor("dst_pad", [1 + E + 2 * STEP], I32, kind="Internal").ap()
    src_pad = nc.dram_tensor("src_pad", [E + 2 * STEP], I32, kind="Internal").ap()
    table = nc.dram_tensor("table", [N, TROW], F32, kind="Internal").ap()
    x1_dram = nc.dram_tensor("x1_dram", [N, D], F32, kind="Internal").ap()
    xs = nc.dram_tensor("xs", [PLACES, D], F32, kind="Internal").ap()
    ys = nc.dram_tensor("ys", [PLACES, D], F32, kind="Internal").ap()
    prm = nc.dram_tensor("prm", [NE, P, FC + 2 * KD], F32, kind="Internal").ap()

    ctx = ExitStack()
    with ctx:
        def allot(stack):
            def sb(name, shape, dt=F32):
                return stack.enter_context(nc.sbuf_tensor(name, shape, dt))

            def ps(name, shape, dt=F32):
                return stack.enter_context(nc.psum_tensor(name, shape, dt))

            def sem(name):
                return stack.enter_context(nc.semaphore(name))

            return sb, ps, sem

        sb, _, _ = allot(ctx)
        ident = sb("ident", [P, P])
        ident16 = sb("ident16", [P, P], BF16)
        ones = sb("ones", [P, P])
        iota_row = sb("iota_row", [P, P])
        iota_col = sb("iota_col", [P, 1])
        before = sb("before", [P, P])
        wbase = sb("wbase", [P, 2 * P])
        win_i = sb("win_i", [1, 2 * P], I32)
        off_i = sb("off_i", [1, 2 * P], I32)
        edge_cnt = sb("edge_cnt", [P, NCNT])
        big = sb("big", [P, max(NW * D, RING * HS * T * TROW)])
        slot_e = sb("slot_e", [1, SLOTS], I32)
        pos = [sb(f"pos{k}", [P, NW], U32) for k in range(2)]
        wt = [sb(f"wt{k}", [P, NW]) for k in range(2)]
        eps_col = sb("eps_col", [P, 1])
        tick = sb("tick", [P, 1])

        _, _, lasting = allot(ctx)
        x_first = [lasting(f"x_first{g}") for g in range(NG + 1)]
        edges_loaded = [lasting(f"edges_loaded{r}") for r in range(RING)]
        until_experts = ctx.enter_context(ExitStack())
        sb, _, _ = allot(until_experts)
        zeros = sb("zeros", [P, D])
        src_t = sb("src_t", [P, RING, HS, T], I32)
        dst_t = sb("dst_t", [P, 3, RING, HS, T], I32)
        dm = sb("dm", [P, NW + 1, 2 * H])
        acc = sb("acc", [P, NW + 1, ROW])

        node_rows = big[:, 0:NW * D].rearrange("p (w d) -> p w d", d=D)

        def chain(eng, s, base=0):
            count = [0]

            def link(ins):
                count[0] += 1
                ins.then_inc(s, 1)
                eng.wait_ge(s, base + count[0])

            link.count = count
            return link

        def moments(link, mean, var, stats, tmp):
            nc.vector.tensor_tensor(mean, stats[:, :, 1], stats[:, :, 4], ALU.add)
            nc.vector.tensor_tensor(tmp[:, 0, :], stats[:, :, 1], stats[:, :, 4], ALU.subtract)
            link(nc.vector.tensor_tensor(var, stats[:, :, 2], stats[:, :, 5], ALU.add))
            link(nc.vector.tensor_scalar(mean, mean, 0.5, None, ALU.mult))
            link(nc.vector.scalar_tensor_tensor(tmp[:, 1, :], tmp[:, 0, :], 0.25, tmp[:, 0, :], ALU.mult, ALU.mult))
            return nc.vector.scalar_tensor_tensor(var, var, 1.0 / D, tmp[:, 1, :], ALU.mult, ALU.add)

        def copied(out_ap, in_ap):
            return nc.vector.tensor_scalar(out_ap, in_ap, 1.0, None, ALU.mult)

        def each_window(eng, body, start=0, count=NW):
            turn = next(u for u in (7, 3, 2, 1) if count % u == 0)
            if count == turn:
                for u in range(turn):
                    body(start + u)
                return
            with eng.Fori(0, count // turn) as i:
                for u in range(turn):
                    body(turn * i + u + start)

        def load_half(sp, n, r):
            for j in range(HS):
                off = sp.value_load(off_i[0:1, bass.ds(HS * (RING * n + r) + j, 1)], min_val=0, max_val=E)
                sp.dma_start(src_t[:, r, j, :], src_pad[bass.ds(off, STEP)].rearrange("(p t) -> p t", t=T)
                             ).then_inc(edges_loaded[r], 16)
                for v in range(3):
                    sp.dma_start(dst_t[:, v, r, j, :], dst_pad[bass.ds(off + v, STEP)].rearrange("(p t) -> p t", t=T)
                                 ).then_inc(edges_loaded[r], 16)

        def load_nodes(sp, loaded):
            for g in range(NG):
                sp.dma_start(node_rows[:, g * GW:(g + 1) * GW, :],
                             x[g * GW * P:(g + 1) * GW * P, :].rearrange("(w p) d -> p w d", p=P)).then_inc(loaded[g], 16)
            sp.dma_start(node_rows[0:LAST, NW - 1, :], x[(NW - 1) * P:N, :]).then_inc(loaded[NG], 16)

        with ExitStack() as st:
            sb, ps, sem = allot(st)
            pad = sb("pad", [1, 2 * STEP], I32)
            zpad = sb("zpad", [1, 2 * STEP], I32)
            dst_i = sb("dst_i", [P, EC], I32)
            win_of = sb("win_of", [P, EC], I32)
            win_f = sb("win_f", [P, EC], BF16)
            junk = sb("junk", [P, 7, EC], BF16)
            bound = sb("bound", [P, NCNT])
            pt = sb("pt", [P, NE, FC + 2 * KD])
            consts_made = sem("consts_made")
            pad_zeroed = sem("pad_zeroed")
            tiles_set = sem("tiles_set")
            dst_set = sem("dst_set")
            dst_loaded = sem("dst_loaded")
            ident_made = sem("ident_made")
            counted = sem("counted")
            prm_loaded = sem("prm_loaded")
            stores = sem("stores")
            loads = sem("loads")
            block = st.enter_context(nc.Block())

            @block.gpsimd
            def _(pool):
                nc.gpsimd.iota(iota_row[:, :], [[1, P]], base=0, channel_multiplier=0,
                               allow_small_or_imprecise_dtypes=True)
                nc.gpsimd.iota(iota_col[:, :], [[0, 1]], base=0, channel_multiplier=1,
                               allow_small_or_imprecise_dtypes=True)
                nc.gpsimd.iota(bound[:, :], [[1, NCNT]], base=0, channel_multiplier=0,
                               allow_small_or_imprecise_dtypes=True)
                nc.gpsimd.memset(ident[:, :], 0.0)
                nc.gpsimd.memset(ones[:, :], 1.0).then_inc(consts_made, 1)
                pool.wait_ge(consts_made, 1)
                nc.gpsimd.affine_select(out=ident[:, :], in_=ident[:, :], compare_op=ALU.not_equal, fill=1.0,
                                        base=0, pattern=[[-1, P]], channel_multiplier=1).then_inc(ident_made, 1)
                nc.gpsimd.affine_select(out=before[:, :], in_=ones[:, :], compare_op=ALU.is_gt, fill=0.0,
                                        base=0, pattern=[[1, P]], channel_multiplier=-1).then_inc(ident_made, 1)

            @block.vector
            def _(dve):
                link = chain(dve, counted)
                nc.vector.memset(dst_i[:, :], N + P)
                nc.vector.memset(pad[:, :], 2 * N).then_inc(dst_set, 1)
                nc.vector.memset(zpad[:, :], 0)
                nc.vector.memset(node_rows[:, NW - 1, :], 0.0).then_inc(pad_zeroed, 1)
                nc.vector.memset(zeros[:, :], 0.0)
                nc.vector.memset(eps_col[:, :], EPS)
                nc.vector.memset(edge_cnt[:, :], 0.0).then_inc(tiles_set, 1)
                dve.wait_ge(ident_made, 1)
                nc.vector.tensor_copy(ident16[:, :], ident[:, :])
                dve.wait_ge(dst_loaded, 16)
                link(nc.vector.tensor_scalar(win_of[:, :], dst_i[:, :], P.bit_length() - 1, None, ALU.arith_shift_right))
                link(nc.vector.tensor_copy(win_f[:, :], win_of[:, :]))

                with dve.Fori(0, NW // 7) as i:
                    for u in range(7):
                        w = 7 * i + u + 1
                        last = nc.vector.tensor_scalar(junk[:, u, :], win_f[:, :], bound[:, bass.ds(w, 1)], 0.0, ALU.is_lt,
                                                       ALU.add, accum_out=edge_cnt[:, bass.ds(w, 1)])
                    last.then_inc(counted, 1)
                    dve.wait_ge(counted, i + 3)

            @block.sync
            def _(sp):
                sp.wait_ge(dst_set, 1)
                sp.dma_start(dst_i[0:EP, :], dst.rearrange("(p c) -> p c", p=EP)).then_inc(dst_loaded, 16)
                sp.dma_start(dst_pad[1:1 + E].rearrange("(a b) -> a b", a=EP), dst.rearrange("(a b) -> a b", a=EP)).then_inc(stores, 16)
                sp.dma_start(src_pad[0:E].rearrange("(a b) -> a b", a=EP), src.rearrange("(a b) -> a b", a=EP)).then_inc(stores, 16)
                sp.wait_ge(tiles_set, 1)
                sp.dma_start(dst_pad[0:1].rearrange("(a b) -> a b", a=1), pad[:, 0:1]).then_inc(stores, 16)
                sp.dma_start(dst_pad[1 + E:].rearrange("(a b) -> a b", a=1), pad[:, :]).then_inc(stores, 16)
                sp.dma_start(src_pad[E:].rearrange("(a b) -> a b", a=1), zpad[:, :]).then_inc(stores, 16)
                sp.wait_ge(pad_zeroed, 1)
                load_nodes(sp, x_first)
                sp.wait_ge(stores, 16 * 5)

            @block.scalar
            def _(act):
                for e in range(NE):
                    act.dma_start(pt[:, e, 0:FC], b1[e].rearrange("(c p) -> p c", p=P),
                                  allow_slow_non_contiguous=True).then_inc(prm_loaded, 16)
                    act.dma_start(pt[:, e, FC:FC + KD], ln_g[e].rearrange("(k p) -> p k", p=P),
                                  allow_slow_non_contiguous=True).then_inc(prm_loaded, 16)
                    act.dma_start(pt[:, e, FC + KD:], ln_b[e].rearrange("(k p) -> p k", p=P),
                                  allow_slow_non_contiguous=True).then_inc(prm_loaded, 16)
                act.wait_ge(prm_loaded, 16 * 3 * NE)
                act.dma_start(prm.rearrange("e p c -> p e c"), pt[:, :, :]).then_inc(loads, 16)
                act.wait_ge(loads, 16)

        with ExitStack() as st:
            sb, ps, sem = allot(st)
            start_ps = ps("start_ps", [P, NCNT])
            row_ps = ps("row_ps", [P, 4, P])
            start = sb("start", [P, NCNT])
            first = sb("first", [P, NCNT])
            cnt = sb("cnt", [P, NW])
            cnt_i = sb("cnt_i", [P, NW], I32)
            zero = sb("zero", [P, NW])
            q = sb("q", [P, NCNT])
            dq = sb("dq", [P, NCNT])
            passed = sb("passed", [P, 2, NCNT])
            part = sb("part", [P, 2, NCNT])
            stepno = sb("stepno", [P, 2])
            val = sb("val", [P, 4])
            spread = sb("spread", [P, 4, P])
            summed = sem("summed")
            spread_done = sem("spread_done")
            rows_done = sem("rows_done")
            dve_seq = sem("sched_seq")
            block = st.enter_context(nc.Block())

            @block.tensor
            def _(pe):
                nc.tensor.matmul(start_ps[:, :], ones[:, :], edge_cnt[:, :], start=True, stop=True).then_inc(summed, 1)
                pe.wait_ge(spread_done, 1)
                for v in range(4):
                    last = nc.tensor.matmul(row_ps[:, v, :], spread[:, v, :], ident[:, :], start=True, stop=True)
                last.then_inc(rows_done, 1)

            @block.vector
            def _(dve):
                link = chain(dve, dve_seq)
                nc.vector.memset(zero[:, :], 0.0)
                nc.vector.memset(first[:, :], 0.0)
                nc.vector.memset(dq[:, :], 0.0)
                nc.vector.tensor_copy(stepno[:, 0:1], iota_col[:, :])
                link(nc.vector.tensor_scalar(stepno[:, 1:2], iota_col[:, :], float(P), None, ALU.add))
                dve.wait_ge(summed, 1)
                link(nc.vector.tensor_copy(start[:, :], start_ps[:, :]))
                link(nc.vector.tensor_tensor(cnt[:, :], start[:, 1:], start[:, 0:NW], ALU.subtract))
                link(nc.vector.tensor_scalar(cnt_i[:, :], cnt[:, :], float(STEP - 1), None, ALU.add))
                link(nc.vector.tensor_scalar(cnt_i[:, :], cnt_i[:, :], STEP.bit_length() - 1, None, ALU.arith_shift_right))
                link(nc.vector.tensor_copy(cnt[:, :], cnt_i[:, :]))
                link(nc.vector.tensor_tensor_scan(first[:, 1:], cnt[:, :], zero[:, :], 0.0, ALU.add, ALU.add))
                link(nc.vector.scalar_tensor_tensor(q[:, :], first[:, :], -float(STEP), start[:, :], ALU.mult, ALU.add))
                link(nc.vector.tensor_tensor(dq[:, 1:], q[:, 1:], q[:, 0:NW], ALU.subtract))
                for j in range(2):
                    last = nc.vector.tensor_scalar(passed[:, j, :], first[:, :], stepno[:, j:j + 1], None, ALU.is_le)
                link(last)
                for j in range(2):
                    last = nc.vector.tensor_tensor(part[:, j, :], passed[:, j, :], dq[:, :], ALU.mult)
                link(last)
                nc.vector.tensor_reduce(val[:, 0:2], passed[:, :, :], X, ALU.add)
                link(nc.vector.tensor_reduce(val[:, 2:4], part[:, :, :], X, ALU.add))
                link(nc.vector.scalar_tensor_tensor(val[:, 2:4], stepno[:, :], float(STEP), val[:, 2:4], ALU.mult, ALU.add))
                nc.vector.tensor_scalar(val[:, 0:2], val[:, 0:2], -1.0, None, ALU.add)
                link(nc.vector.tensor_scalar(val[:, 2:4], val[:, 2:4], float(E), None, ALU.min))
                for v in range(4):
                    last = nc.vector.tensor_scalar(spread[:, v, :], ones[:, :], val[:, v:v + 1], None, ALU.mult)
                last.then_inc(spread_done, 1)
                dve.wait_ge(rows_done, 1)
                nc.vector.tensor_scalar(wbase[:, :], row_ps[:, 0:2, :].rearrange("p a b -> p (a b)"), float(P), None, ALU.mult)
                nc.vector.tensor_copy(win_i[:, :], row_ps[0:1, 0:2, :].rearrange("p a b -> p (a b)"))
                nc.vector.tensor_copy(off_i[:, :], row_ps[0:1, 2:4, :].rearrange("p a b -> p (a b)"))

        with ExitStack() as st:
            sb, ps, sem = allot(st)
            WX = D + 2 * H
            wx = sb("wx", [P, KD, WX])
            w_sb = sb("w_sb", [P, KD, D])
            attb = sb("attb", [P, 2, D])
            prod = sb("prod", [P, 2, KD, D])
            attw = sb("attw", [P, 2, KD, H])
            stat = sb("stat", [P, NW, 6])
            mv = sb("mv", [P, NW, 2])
            rstd = sb("rstd", [P, NW])
            mtmp = sb("mtmp", [P, 2, NW])
            xn_st = sb("xn_st", [P, 2, 2, D])
            xT = sb("xT", [P, 2, 2 * D])
            hx = sb("hx", [P, 2, 2, TROW + H])
            xT_ps = ps("xT_ps", [P, 2, 512])
            h_ps = ps("h_ps", [P, 4, 512])
            w_loaded = sem("w_loaded")
            acc_one = sem("acc_one")
            wx_ready = sem("wx_ready")
            var_ready = sem("var_ready")
            std_ready = sem("std_ready")
            dve_seq = sem("proj_seq")
            xn_ready = sem("xn_ready")
            xT_made = sem("xT_made")
            xT_copied = sem("xT_copied")
            h_made = sem("h_made")
            h_copied = sem("h_copied")
            dm_done = sem("dm_done")
            acc_set = sem("acc_set")
            table_stored = [sem(f"table_stored{b}") for b in range(2)]
            block = st.enter_context(nc.Block())

            @block.sync
            def _(sp):
                sp.dma_start(w_sb[:, :, :], gW.rearrange("(k p) n -> p k n", p=P)).then_inc(w_loaded, 16)
                sp.dma_start(attb[:, 0, :], att_src.rearrange("h c -> (h c)").partition_broadcast(P)).then_inc(w_loaded, 16)
                sp.dma_start(attb[:, 1, :], att_dst.rearrange("h c -> (h c)").partition_broadcast(P)).then_inc(w_loaded, 16)

                def store_rows(m, b, n=2, rows=P):
                    sp.wait_ge(h_copied, m + 1)
                    sp.dma_start(table[bass.ds(m * 2 * P, n * rows), :].rearrange("(u p) c -> p u c", p=rows),
                                 hx[0:rows, b, 0:n, 0:TROW]).then_inc(table_stored[b], 16)

                for r in range(RING):
                    load_half(sp, 0, r)
                with sp.Fori(0, PAIRED // 2) as i:
                    for b in range(2):
                        store_rows(2 * i + b, b)
                store_rows(PAIRED, 0, 1, LAST)
                sp.wait_ge(table_stored[0], 16 * (PAIRED // 2 + 1))
                sp.wait_ge(table_stored[1], 16 * (PAIRED // 2))

            @block.gpsimd
            def _(pool):
                nc.gpsimd.memset(acc[:, :, :], 1.0).then_inc(acc_one, 1)
                pool.wait_ge(acc_one, 1)

                def start_acc(m, b, n=2):
                    pool.wait_ge(h_copied, m + 1)
                    for u in range(n):
                        last = nc.gpsimd.tensor_copy(acc[:, bass.ds(2 * m + u, 1), :].rearrange("p o (h c) -> p (o h) c", h=H)[:, :, 0:HD],
                                                     hx[:, b, u, 0:ROW].rearrange("p (h c) -> p h c", h=H)[:, :, 0:HD])
                    last.then_inc(acc_set, 1)

                with pool.Fori(0, PAIRED // 2) as i:
                    for b in range(2):
                        start_acc(2 * i + b, b)
                start_acc(PAIRED, 0, 1)

            @block.scalar
            def _(act):
                act.wait_ge(var_ready, 1)
                nc.scalar.activation(rstd[:, :], mv[:, :, 1], ACT.Sqrt, bias=eps_col[:, 0:1]).then_inc(std_ready, 1)

                def copy_xT(m, b, n=2):
                    act.wait_ge(xT_made, m + 1)
                    nc.scalar.activation(xT[:, b, 0:n * D], xT_ps[:, b, 0:n * D], ACT.Copy).then_inc(xT_copied, 1)

                with act.Fori(0, PAIRED // 2) as i:
                    for b in range(2):
                        copy_xT(2 * i + b, b)
                copy_xT(PAIRED, 0, 1)

            @block.tensor
            def _(pe):
                def transpose(m, b, n=2):
                    pe.wait_ge(xn_ready, m + 1)
                    for u in range(n):
                        for k in range(KD):
                            c = (u * KD + k) * P
                            last = nc.tensor.transpose(xT_ps[:, b, c:c + P], xn_st[:, b, u, k * P:(k + 1) * P], ident[:, :])
                    last.then_inc(xT_made, 1)

                def product(m, b, n=2, reused=True):
                    pe.wait_ge(xT_copied, m + 1)
                    if reused:
                        pe.wait_ge(h_copied, m - 1)
                    for u in range(n):
                        for k in range(KD):
                            c = (u * KD + k) * P
                            last = nc.tensor.matmul(h_ps[:, 2 * b + u, 0:WX], xT[:, b, c:c + P], wx[:, k, :],
                                                    start=(k == 0), stop=(k == KD - 1))
                    last.then_inc(h_made, 1)

                pe.wait_ge(wx_ready, 1)
                transpose(0, 0)
                transpose(1, 1)
                product(0, 0, reused=False)
                transpose(2, 0)
                product(1, 1, reused=False)
                with pe.Fori(1, PAIRED // 2 - 1) as i:
                    for b in range(2):
                        transpose(2 * i + b + 1, 1 - b)
                        product(2 * i + b, b)
                transpose(PAIRED - 1, 1)
                product(PAIRED - 2, 0)
                transpose(PAIRED, 0, 1)
                product(PAIRED - 1, 1)
                product(PAIRED, 0, 1)

            @block.vector
            def _(dve):
                link = chain(dve, dve_seq)
                nc.vector.memset(dm[:, :, :], 0.0)
                nc.vector.memset(hx[:, :, :, :], 1.0)
                dve.wait_ge(w_loaded, 48)
                for v in range(2):
                    for k in range(KD):
                        last = nc.vector.tensor_tensor(prod[:, v, k, :], w_sb[:, k, :], attb[:, v, :], ALU.mult)
                link(last)
                for v in range(2):
                    last = nc.vector.tensor_reduce(attw[:, v, :, :].rearrange("p k h -> p (k h)"),
                                                   prod[:, v, :, :].rearrange("p k (h c) -> p (k h) c", h=H), X, ALU.add)
                link(last)
                for k in range(KD):
                    nc.vector.tensor_copy(wx[:, k, 0:D], w_sb[:, k, :])
                    nc.vector.tensor_copy(wx[:, k, D:D + H], attw[:, 0, k, :])
                    last = nc.vector.tensor_copy(wx[:, k, D + H:], attw[:, 1, k, :])
                last.then_inc(wx_ready, 1)

                for g in range(NG + 1):
                    dve.wait_ge(x_first[g], 16)
                    each_window(dve, lambda w: nc.vector.bn_stats(stat[:, bass.ds(w, 1), :].rearrange("p o c -> p (o c)"),
                                                                  node_rows[:, bass.ds(w, 1), :].rearrange("p o c -> p (o c)")),
                                g * GW, min(GW, NW - g * GW))
                link(nc.vector.memset(tick[:, :], 0.0))
                moments(link, mv[:, :, 0], mv[:, :, 1], stat, mtmp).then_inc(var_ready, 1)
                dve.wait_ge(std_ready, 1)
                link(nc.vector.reciprocal(rstd[:, :], rstd[:, :]))

                def normalise(m, b, n=2, reused=True):
                    if reused:
                        dve.wait_ge(xT_made, m - 1)
                    for u in range(n):
                        w = 2 * m + u
                        last = nc.vector.tensor_scalar(xn_st[:, b, u, :], node_rows[:, bass.ds(w, 1), :].rearrange("p o c -> p (o c)"),
                                                       mv[:, bass.ds(w, 1), 0], rstd[:, bass.ds(w, 1)], ALU.subtract, ALU.mult)
                    last.then_inc(xn_ready, 1)

                def take_h(m, b, n=2, use=None):
                    dve.wait_ge(h_made, m + 1)
                    if use is not None:
                        dve.wait_ge(table_stored[b], 16 * use)
                        dve.wait_ge(acc_set, m - 1)
                    nc.vector.tensor_copy(hx[:, b, 0:n, 0:ROW].rearrange("p u (h c) -> p u h c", h=H)[:, :, :, 0:HD],
                                          h_ps[:, 2 * b:2 * b + n, 0:D].rearrange("p u (h c) -> p u h c", h=H))
                    nc.vector.tensor_copy(hx[:, b, 0:n, ROW:], h_ps[:, 2 * b:2 * b + n, D:WX]).then_inc(h_copied, 1)
                    dve.wait_ge(h_copied, m + 1)
                    rows = dm[:, bass.ds(2 * m, n), :]
                    copied(rows[:, :, 0:H], hx[:, b, 0:n, TROW:])
                    nc.vector.tensor_tensor(rows[:, :, H:], hx[:, b, 0:n, TROW:], hx[:, b, 0:n, ROW:TROW], ALU.add)

                normalise(0, 0, reused=False)
                normalise(1, 1, reused=False)
                normalise(2, 0)
                take_h(0, 0)
                normalise(3, 1)
                take_h(1, 1)
                with dve.Fori(1, PAIRED // 2 - 1) as i:
                    for b in range(2):
                        normalise(2 * i + b + 2, b)
                        take_h(2 * i + b, b, use=i)
                i = PAIRED // 2 - 1
                normalise(PAIRED, 0, 1)
                take_h(PAIRED - 2, 0, use=i)
                take_h(PAIRED - 1, 1, use=i)
                take_h(PAIRED, 0, 1, use=i + 1)
                link(nc.vector.memset(tick[:, :], 0.0))
                link(nc.vector.scalar_tensor_tensor(dm[:, :, H:], dm[:, :, H:], SLOPE, dm[:, :, H:], ALU.mult, ALU.max))

        with ExitStack() as st:
            sb, ps, sem = allot(st)
            HB = HS * H
            HT = HS * T
            D8 = 2 * H
            LINKS = 17
            NB = -(-NH // RING)
            LEFT = NH - RING * (NB - 1)
            ZROWS = 7
            ZTURNS = PLACES // P // ZROWS
            assert ZTURNS * ZROWS * P == PLACES and 1 + ZTURNS < NB - 1
            gat_rows = big[:, 0:RING * HT * TROW].rearrange("p (n c) -> p n c", c=TROW)
            gat = big[:, 0:RING * HT * TROW].rearrange("p (r j t c) -> p r j t c", r=RING, j=HS, t=T)
            dloc = sb("dloc", [P, RING, HS, T], BF16)
            begins = sb("begins", [P, HS, T])
            ends = sb("ends", [P, RING, HS, T])
            last_edge = sb("last_edge", [P, HS, T])
            last_col = sb("last_col", [P, 1])
            resets = sb("resets", [P, T, HS, H])
            onehot = sb("onehot", [P, RING, HS, T, P])
            onehot16 = sb("onehot16", [P, HS, T, P], BF16)
            iota16 = sb("iota16", [P, P], BF16)
            onehotT = sb("onehotT", [P, HS, T * P], BF16)
            a_s = sb("a_s", [P, RING, T, HS, H])
            resT = sb("resT", [HB, T * P])
            runmax = sb("runmax", [HB, T * P])
            seg = sb("seg", [P, HS, T, H])
            seg_r = sb("seg_r", [P, HS, T, H])
            seg16 = sb("seg16", [P, HS, T, 3, H + 1], BF16)
            absent = sb("absent", [P, HS])
            cand = sb("cand", [P, HS, H])
            cand2 = sb("cand2", [P, HS, H])
            known = sb("known", [P, HS, D8])
            cur = sb("cur", [P, HS, D8])
            best = sb("best", [P, H, HS])
            highest = sb("highest", [P, H, HS])
            old = sb("old", [P, H, HS])
            wreset = sb("wreset", [P, NS])
            reset_j = sb("reset_j", [P, H, HS])
            cur_r = sb("cur_r", [P, HS, D8])
            cur16 = sb("cur16", [P, HS, 3, D8], BF16)
            shrink_x = sb("shrink_x", [P, H, HS])
            shrink = sb("shrink", [P, RING, HS, H])
            score = sb("score", [P, HS, T, H])
            score2 = sb("score2", [P, HS, T, H])
            wgt = sb("wgt", [P, RING, HS, T, H])
            wrow = sb("wrow", [P, HS, T, H, HD + 1])
            asT_ps = ps("asT_ps", [HB, 512])
            resT_ps = ps("resT_ps", [HB, 512])
            seg_ps = ps("seg_ps", [P, 512])
            ohT_ps = ps("ohT_ps", [P, 2, 1024], BF16)
            edge_ps = ps("edge_ps", [P, 512])
            sum_ps = ps("sum_ps", [P, 2, 512])
            back_ps = seg_ps[:, 0:T * HB]
            win_ps = seg_ps[:, 128:128 + HS * (H + 1)].rearrange("p (j c) -> p j c", j=HS)

            rows_gathered = [sem(f"rows_gathered{r}") for r in range(RING)]
            seq = sem("attend_seq")
            marks_set = sem("marks_set")
            onehot_made = sem("onehot_made")
            a_s_staged = sem("a_s_staged")
            asT_made = sem("asT_made")
            resT_copied = sem("resT_copied")
            resets_made = sem("resets_made")
            resT_made = sem("resT_made")
            onehot_copied = sem("onehot_copied")
            ohT_made = sem("ohT_made")
            onehotT_copied = sem("onehotT_copied")
            scanned = sem("scanned")
            back_made = sem("back_made")
            seg_made = sem("seg_made")
            win_made = sem("win_made")
            cur_made = sem("cur_made")
            shrink_in = sem("shrink_in")
            shrink_made = sem("shrink_made")
            edge_made = sem("edge_made")
            score_made = sem("score_made")
            weights_made = sem("weights_made")
            rows_weighted = sem("rows_weighted")
            slot_free = sem("slot_free")
            summed = sem("step_summed")
            xs_zeroed = sem("xs_zeroed")
            merged = sem("merged")
            block = st.enter_context(nc.Block())

            @block.sync
            def _(sp):
                def next_half(n, r):
                    sp.wait_ge(score_made, RING * (n - 1) + r + 1)
                    load_half(sp, n, r)

                with sp.Fori(1, NB - 1) as n:
                    for r in range(RING):
                        next_half(n, r)
                for r in range(LEFT):
                    next_half(NB - 1, r)

            @block.gpsimd
            def _(pool):
                def gather_half(n, r, reused=True):
                    pool.wait_ge(edges_loaded[r], 256 * (n + 1))
                    for j in range(HS):
                        if reused:
                            pool.wait_ge(rows_weighted, HS * (RING * n + r - RING) + j + 1)
                            pool.sem_inc(slot_free, 1)
                        for t in range(T):
                            pool.indirect_dma_start(
                                gat_rows[:, (r * HS + j) * T + t, :], None, table,
                                bass.IndirectOffsetOnAxis(ap=src_t[:, r, j, t:t + 1].bitcast(U32), axis=0),
                            ).then_inc(rows_gathered[r], 16)

                for r in range(RING):
                    gather_half(0, r, reused=False)
                with pool.Fori(1, NB - 1) as n:
                    for r in range(RING):
                        gather_half(n, r)
                for r in range(LEFT):
                    gather_half(NB - 1, r)


            def turns(eng, half):
                for r in range(RING):
                    half(r, 0, r)
                with eng.Fori(1, NB - 1) as n:
                    for r in range(RING):
                        half(RING * n + r, n, r)
                for r in range(LEFT):
                    half(RING * (NB - 1) + r, NB - 1, r)

            @block.scalar
            def _(act):
                def half(k, n, r):
                    started = not (isinstance(k, int) and k == 0)
                    act.wait_ge(resT_made, k + 1)
                    if started:
                        act.wait_ge(scanned, k)
                    nc.scalar.activation(resT[:, :], resT_ps[:, :], ACT.Copy).then_inc(resT_copied, 1)
                    if started:
                        act.wait_ge(edge_made, k)
                    for g in range(2):
                        act.wait_ge(ohT_made, 2 * k + g + 1)
                        nc.scalar.activation(onehotT[:, 2 * g:2 * g + 2, :].rearrange("p j c -> p (j c)"), ohT_ps[:, g, :],
                                             ACT.Copy).then_inc(onehotT_copied, 1)
                    if not isinstance(k, int) or k >= RING:
                        act.wait_ge(summed, HS * (k - RING + 1))
                    nc.scalar.activation(onehot[:, r, :, :, :].rearrange("p j t c -> p (j t c)"),
                                         onehot16[:, :, :, :].rearrange("p j t c -> p (j t c)"),
                                         ACT.Copy).then_inc(onehot_copied, 1)
                    act.wait_ge(shrink_in, k + 1)
                    nc.scalar.activation(shrink[:, r, :, :].rearrange("p j h -> p h j"), shrink_x[:, :, :], ACT.Exp).then_inc(shrink_made, 1)
                    act.wait_ge(score_made, k + 1)
                    nc.scalar.activation(wgt[:, r, :, :, :], score[:, :, :, :], ACT.Exp).then_inc(weights_made, 1)

                def zero_places(n):
                    act.dma_start(xs.rearrange("(p r) d -> p r d", p=P)[:, bass.ds(n * ZROWS, ZROWS), :],
                                  zeros[:, :].unsqueeze(1).to_broadcast([P, ZROWS, D])).then_inc(xs_zeroed, 16)

                for r in range(RING):
                    half(r, 0, r)
                with act.Fori(1, 1 + ZTURNS) as n:
                    zero_places(n - 1)
                    for r in range(RING):
                        half(RING * n + r, n, r)
                with act.Fori(1 + ZTURNS, NB - 1) as n:
                    for r in range(RING):
                        half(RING * n + r, n, r)
                for r in range(LEFT):
                    half(RING * (NB - 1) + r, NB - 1, r)
                act.wait_ge(xs_zeroed, 16 * ZTURNS)

            @block.tensor
            def _(pe):
                def add_rows(s, j, rr):
                    pe.wait_ge(rows_weighted, s + 1)
                    if not isinstance(s, int) or s >= 2:
                        pe.wait_ge(merged, s - 1)
                    for t in range(T):
                        last = nc.tensor.matmul(sum_ps[:, j % 2, 0:ROW], onehot[:, rr, j, t, :],
                                                wrow[:, j, t, :, :].rearrange("p h c -> p (h c)"),
                                                start=(t == 0), stop=(t == T - 1))
                    last.then_inc(summed, 1)

                def transpose_maxima(k, r):
                    pe.wait_ge(a_s_staged, k + 1)
                    for t in range(T):
                        last = nc.tensor.transpose(asT_ps[:, t:T * P:T], a_s[:, r, t, :, :].rearrange("p j h -> p (j h)"), ident[:, :])
                    last.then_inc(asT_made, 1)
                    pe.wait_ge(resets_made, k + 1)
                    if not (isinstance(k, int) and k == 0):
                        pe.wait_ge(resT_copied, k)
                    for t in range(T):
                        last = nc.tensor.transpose(resT_ps[:, t:T * P:T], resets[:, t, :, :].rearrange("p j h -> p (j h)"),
                                                   ident[:, :])
                    last.then_inc(resT_made, 1)

                def half(k, n, r):
                    prev = not (isinstance(k, int) and k == 0)
                    rr = (r - 1) % RING
                    s = HS * k - HS
                    pe.wait_ge(onehot_made, k + 1)
                    for g in range(2):
                        for j in (2 * g, 2 * g + 1):
                            for t in range(T):
                                c = (j % 2) * T * P + t * P
                                last = nc.tensor.transpose(ohT_ps[:, g, c:c + P], onehot16[:, j, t, :], ident16[:, :])
                        last.then_inc(ohT_made, 1)
                    pe.wait_ge(asT_made, 1)
                    pe.wait_ge(scanned, k + 1)
                    for t in range(T):
                        last = nc.tensor.transpose(back_ps[:, t * HB:(t + 1) * HB], runmax[:, t:T * P:T], ident[0:HB, 0:HB])
                    last.then_inc(back_made, 1)
                    if prev:
                        pe.wait_ge(onehot_copied, k)
                        add_rows(s, 0, rr)
                    pe.wait_ge(seg_made, k + 1)
                    for j in range(HS):
                        for t in range(T):
                            for v in range(3):
                                last = nc.tensor.matmul(win_ps[:, j, :], onehot16[:, j, t, :], seg16[:, j, t, v, :],
                                                        start=(t == 0 and v == 0), stop=(t == T - 1 and v == 2))
                    last.then_inc(win_made, 1)
                    if prev:
                        add_rows(s + 1, 1, rr)
                    pe.wait_ge(cur_made, k + 1)
                    pe.wait_ge(onehotT_copied, 2 * k + 2)
                    for j in range(HS):
                        for t in range(T):
                            c = (j * T + t) * D8
                            for v in range(3):
                                last = nc.tensor.matmul(edge_ps[:, c:c + D8], onehotT[:, j, t * P:(t + 1) * P],
                                                        cur16[:, j, v, :], start=(v == 0), stop=(v == 2))
                    last.then_inc(edge_made, 1)
                    if prev:
                        add_rows(s + 2, 2, rr)
                    if not (isinstance(k, int) and k == NH - 1):
                        transpose_maxima(k + 1, (r + 1) % RING)
                    if prev:
                        add_rows(s + 3, 3, rr)

                transpose_maxima(0, 0)
                turns(pe, half)
                pe.wait_ge(onehot_copied, NH)
                for j in range(HS):
                    add_rows(HS * (NH - 1) + j, j, (NH - 1) % RING)

            @block.vector
            def _(dve):
                link = chain(dve, marks_set)
                nc.vector.memset(seg16[:, :, :, :, H], 0.0)
                nc.vector.memset(old[:, :, 0], -BIG)
                nc.vector.memset(wreset[:, 0:1], 0.0)
                nc.vector.tensor_copy(iota16[:, :], iota_row[:, :])
                link(nc.vector.tensor_scalar(last_col[:, :], iota_col[:, :], float(P - 1), None, ALU.is_equal))
                link(nc.vector.memset(last_edge[:, :, :], 0.0))
                nc.vector.tensor_copy(last_edge[:, :, T - 1], last_col[:, 0:1].to_broadcast([P, HS]))
                link(nc.vector.tensor_tensor(wreset[:, 1:], wbase[:, 1:NS], wbase[:, 0:NS - 1], ALU.not_equal))
                link(nc.vector.tensor_scalar(wreset[:, :], wreset[:, :], -BIG, None, ALU.mult))
                link(nc.vector.memset(wreset[:, 0:NS:HS], -BIG))

                def edge_marks(k, n, r, link):
                    dve.wait_ge(edges_loaded[r], 256 * (n + 1))
                    base = wbase[:, bass.ds(HS * k, HS)].unsqueeze(2).to_broadcast([P, HS, T])
                    nc.vector.tensor_tensor(dloc[:, r, :, :], dst_t[:, 1, r, :, :], base, ALU.subtract)
                    nc.vector.tensor_tensor(ends[:, r, :, :], dst_t[:, 1, r, :, :], dst_t[:, 2, r, :, :], ALU.not_equal)
                    link(nc.vector.tensor_tensor(begins[:, :, :], dst_t[:, 1, r, :, :], dst_t[:, 0, r, :, :], ALU.not_equal))
                    nc.vector.tensor_scalar(resets[:, :, :, :],
                                            begins[:, :, :].rearrange("p j t -> p t j").unsqueeze(3).to_broadcast([P, T, HS, H]),
                                            -BIG, None, ALU.mult).then_inc(resets_made, 1)
                    nc.vector.tensor_tensor(ends[:, r, :, :], ends[:, r, :, :], last_edge[:, :, :], ALU.max)
                    copied(reset_j[:, :, :], wreset[:, bass.ds(HS * k, HS)].unsqueeze(1).to_broadcast([P, H, HS]))
                    if not (isinstance(k, int) and k == 0):
                        dve.wait_ge(onehot_copied, k)
                    nc.vector.tensor_tensor(onehot16[:, :, :, :].rearrange("p j t c -> p (j t) c"),
                                            iota16[:, :].unsqueeze(1).to_broadcast([P, HT, P]),
                                            dloc[:, r, :, :].rearrange("p j t -> p (j t)").unsqueeze(2).to_broadcast([P, HT, P]),
                                            ALU.is_equal).then_inc(onehot_made, 1)

                def stage_and_mark(k, n, r, link):
                    dve.wait_ge(rows_gathered[r], 256 * (n + 1))
                    nc.vector.tensor_copy(a_s[:, r, :, :, :].rearrange("p t j h -> p j t h"),
                                          gat[:, r, :, :, ROW:]).then_inc(a_s_staged, 1)
                    edge_marks(k, n, r, link)

                def weight_rows(s, j, rr):
                    if not isinstance(s, int) or s >= HS:
                        dve.wait_ge(summed, s - HS + 1)
                    w_e = wgt[:, rr, j, :, :]
                    nc.vector.scalar_tensor_tensor(wrow[:, j, :, :, :], w_e.unsqueeze(3).to_broadcast([P, T, H, HD + 1]), 1.0,
                                                   gat[:, rr, j, :, 0:ROW].rearrange("p t (h c) -> p t h c", h=H),
                                                   ALU.min, ALU.mult).then_inc(rows_weighted, 1)

                def merge(s, j, rr, w):
                    dve.wait_ge(summed, s + 1)
                    if not isinstance(s, int) or s >= 1:
                        dve.wait_ge(merged, s)
                    for h in range(H):
                        cols = slice(h * (HD + 1), (h + 1) * (HD + 1))
                        a = acc[:, bass.ds(w, 1), cols].rearrange("p o c -> p (o c)")
                        last = nc.vector.scalar_tensor_tensor(a, a, shrink[:, rr, j, h:h + 1], sum_ps[:, j % 2, cols],
                                                              ALU.mult, ALU.add)
                    last.then_inc(merged, 1)

                win_regs = [[dve.alloc_register(f"win{r}_{j}") for j in range(HS)] for r in range(RING)]

                def windows(r):
                    return [dve.snap(reg, min_val=0, max_val=NW) for reg in win_regs[r]]

                def half(k, n, r, link):
                    prev = not (isinstance(k, int) and k == 0)
                    rr = (r - 1) % RING
                    s = HS * k - HS
                    by_head = "p j h -> p h j"
                    dve.wait_ge(asT_made, k + 1)
                    dve.wait_ge(resT_copied, k + 1)
                    nc.vector.tensor_tensor_scan(runmax[:, :], resT[:, :], asT_ps[:, :], -BIG, ALU.add, ALU.max
                                                 ).then_inc(scanned, 1)
                    if prev:
                        dve.wait_ge(weights_made, k)
                        weight_rows(s, 0, rr)
                    dve.wait_ge(back_made, k + 1)
                    nc.vector.tensor_copy(seg16[:, :, :, 0, H], ends[:, r, :, :])
                    link(nc.vector.tensor_tensor(seg[:, :, :, :], back_ps.rearrange("p (t j h) -> p j t h", t=T, j=HS),
                                                 ends[:, r, :, :].unsqueeze(3).to_broadcast([P, HS, T, H]), ALU.mult))
                    link(nc.vector.tensor_copy(seg16[:, :, :, 0, 0:H], seg[:, :, :, :]))
                    link(nc.vector.tensor_tensor(seg_r[:, :, :, :], seg[:, :, :, :], seg16[:, :, :, 0, 0:H], ALU.subtract))
                    link(nc.vector.tensor_copy(seg16[:, :, :, 1, 0:H], seg_r[:, :, :, :]))
                    nc.vector.tensor_tensor(seg16[:, :, :, 2, 0:H], seg_r[:, :, :, :], seg16[:, :, :, 1, 0:H],
                                            ALU.subtract).then_inc(seg_made, 1)
                    dve.load(win_regs[r], win_i[0:1, bass.ds(HS * k, HS)])
                    mine = windows(r)
                    wins = windows(rr)
                    if prev:
                        weight_rows(s + 1, 1, rr)
                    for j in range(HS):
                        last = copied(known[:, j, :], dm[:, bass.ds(mine[j], 1), :].rearrange("p o c -> p (o c)"))
                    link(last)
                    nc.vector.tensor_copy(cur[:, :, 0:H], known[:, :, 0:H])
                    if prev:
                        dve.wait_ge(shrink_made, k)
                        merge(s, 0, rr, wins[0])
                    dve.wait_ge(win_made, k + 1)
                    nc.vector.tensor_scalar(absent[:, :], win_ps[:, :, H], BIG, -BIG, ALU.mult, ALU.add)
                    link(nc.vector.tensor_tensor(cand[:, :, :], win_ps[:, :, 0:H], known[:, :, 0:H], ALU.add))
                    link(nc.vector.tensor_tensor(cand2[:, :, :], cand[:, :, :],
                                                 absent[:, :].unsqueeze(2).to_broadcast([P, HS, H]), ALU.add))
                    link(nc.vector.scalar_tensor_tensor(cand[:, :, :], cand2[:, :, :], SLOPE, cand2[:, :, :], ALU.mult, ALU.max))
                    link(nc.vector.tensor_tensor(best[:, :, :], cand[:, :, :].rearrange(by_head),
                                                 known[:, :, H:].rearrange(by_head), ALU.max))
                    link(nc.vector.tensor_tensor_scan(highest[:, :, :].rearrange("p h j -> p (h j)"),
                                                      reset_j[:, :, :].rearrange("p h j -> p (h j)"),
                                                      best[:, :, :].rearrange("p h j -> p (h j)"), -BIG, ALU.add, ALU.max))

                    def keep(j):
                        return copied(dm[:, bass.ds(mine[j], 1), H:].rearrange("p o c -> p (o c)"), highest[:, :, j])

                    nc.vector.tensor_copy(cur[:, :, H:].rearrange(by_head), highest[:, :, :])
                    keep(0)
                    link(nc.vector.tensor_tensor(old[:, :, 1:], highest[:, :, 0:HS - 1], reset_j[:, :, 1:], ALU.add))
                    nc.vector.tensor_copy(cur16[:, :, 0, :], cur[:, :, :])
                    keep(1)
                    link(nc.vector.tensor_tensor(best[:, :, :], old[:, :, :], known[:, :, H:].rearrange(by_head), ALU.max))
                    nc.vector.tensor_tensor(shrink_x[:, :, :], best[:, :, :], highest[:, :, :], ALU.subtract).then_inc(shrink_in, 1)
                    keep(2)
                    link(nc.vector.tensor_tensor(cur_r[:, :, :], cur[:, :, :], cur16[:, :, 0, :], ALU.subtract))
                    nc.vector.tensor_copy(cur16[:, :, 1, :], cur_r[:, :, :])
                    link(keep(3))
                    nc.vector.tensor_tensor(cur16[:, :, 2, :], cur_r[:, :, :], cur16[:, :, 1, :], ALU.subtract).then_inc(cur_made, 1)
                    if prev:
                        weight_rows(s + 2, 2, rr)
                        merge(s + 1, 1, rr, wins[1])
                        weight_rows(s + 3, 3, rr)
                    dve.wait_ge(edge_made, k + 1)
                    edge = edge_ps[:, 0:HT * D8].rearrange("p (j t c) -> p j t c", j=HS, t=T)
                    link(nc.vector.tensor_tensor(score[:, :, :, :], edge[:, :, :, 0:H],
                                                 a_s[:, r, :, :, :].rearrange("p t j h -> p j t h"), ALU.add))
                    flat = "p j t h -> p (j t h)"
                    link(nc.vector.scalar_tensor_tensor(score2[:, :, :, :].rearrange(flat), score[:, :, :, :].rearrange(flat), SLOPE,
                                                        score[:, :, :, :].rearrange(flat), ALU.mult, ALU.max))
                    nc.vector.tensor_tensor(score[:, :, :, :], score2[:, :, :, :], edge[:, :, :, H:], ALU.subtract).then_inc(score_made, 1)
                    if not (isinstance(k, int) and k == NH - 1):
                        stage_and_mark(k + 1, n + (r + 1) // RING, (r + 1) % RING, link)
                    if prev:
                        merge(s + 2, 2, rr, wins[2])
                        merge(s + 3, 3, rr, wins[3])

                before_loop = 1 + RING * LINKS
                link = chain(dve, seq)
                stage_and_mark(0, 0, 0, link)
                for r in range(RING):
                    half(r, 0, r, link)
                assert link.count[0] == before_loop, link.count
                with dve.Fori(1, NB - 1) as n:
                    link = chain(dve, seq, base=(n - 1) * (RING * LINKS) + before_loop)
                    for r in range(RING):
                        half(RING * n + r, n, r, link)
                link = chain(dve, seq, base=before_loop + (NB - 2) * RING * LINKS)
                for r in range(LEFT):
                    half(RING * (NB - 1) + r, NB - 1, r, link)
                wins = windows((NH - 1) % RING)
                s, rr = HS * (NH - 1), (NH - 1) % RING
                dve.wait_ge(weights_made, NH)
                dve.wait_ge(shrink_made, NH)
                weight_rows(s, 0, rr)
                weight_rows(s + 1, 1, rr)
                for j in range(HS):
                    merge(s + j, j, rr, wins[j])
                    if j + 2 < HS:
                        weight_rows(s + j + 2, j + 2, rr)

        with ExitStack() as st:
            sb, ps, sem = allot(st)
            xn = sb("xn", [P, NW, D])
            rden = sb("rden", [P, NW, H])
            gb = sb("gb", [P, D])
            brb = sb("brb", [P, NE])
            wr = sb("wr", [P, KD, NE])
            stat = sb("stat2", [P, NW, 6])
            mv = sb("mv2", [P, 2, NW, 2])
            mtmp = sb("mtmp2", [P, 2, NW])
            rstd = sb("rstd2", [P, 2, NW])
            xt_st = sb("xt_st", [P, 2, 2, D])
            xT = sb("xtT", [P, 2, 2 * D])
            logit = sb("logit", [P, NW, NE])
            top = sb("top", [P, 2, NW])
            number = sb("number", [P, NE])
            equal = sb("equal", [P, NW, NE])
            rest = sb("rest", [P, NW, NE])
            chosen = sb("chosen", [P, NW])
            diff = sb("diff", [P, NW])
            gate = sb("gate", [P, NW])
            gate_d = sb("gate_d", [P, NW])
            pick = [sb(f"pick{k}", [P, NW, NE]) for k in range(2)]
            real = sb("real", [P, 1])
            both = sb("both", [P, NW, NE])
            total = sb("total", [P, NW, NE])
            upto = sb("upto", [P, NW, NE])
            place = sb("place", [P, NW, NE])
            placed = sb("placed", [P, NW, NE])
            posf = sb("posf", [P, NW])
            zero = sb("zero2", [P, NW])
            need = sb("need", [P, NE])
            need_i = sb("need_i", [P, NE], I32)
            need_c = sb("need_c", [P, NE])
            slot0 = sb("slot0", [P, NE])
            owner = sb("owner", [1, SLOTS, NE])
            owner_s = sb("owner_s", [1, SLOTS])
            xT_ps = ps("xtT_ps", [P, 2, 512])
            lg_ps = ps("lg_ps", [P, 2, 512])
            rank_ps = ps("rank_ps", [P, 512])
            total_ps = ps("total_ps", [P, 512])
            x_loaded = [sem(f"x_again{g}") for g in range(NG + 1)]
            small_loaded = sem("small_loaded")
            pad_zeroed = sem("pad_zeroed2")
            seq = sem("norm_seq")
            added = sem("added")
            biased = sem("biased")
            var_ready = [sem(f"var_ready{v}") for v in range(2)]
            std_ready = [sem(f"std_ready{v}") for v in range(2)]
            xt_ready = sem("xt_ready")
            xT_made = sem("xtT_made")
            xT_copied = sem("xtT_copied")
            lg_made = sem("lg_made")
            lg_taken = sem("lg_taken")
            gate_in = sem("gate_in")
            gate_made = sem("gate_made")
            both_made = sem("both_made")
            ranked = sem("ranked")
            xn_ready = sem("xn_ready2")
            pos_ready = sem("pos_ready")
            scattered = sem("scattered")
            block = st.enter_context(nc.Block())
            acc_rows = lambda w: acc[:, bass.ds(w, 1), :].rearrange("p o (h c) -> p (o h) c", h=H)[:, :, 0:HD]
            row = lambda a, w: a[:, bass.ds(w, 1), :].rearrange("p o c -> p (o c)")
            xt_row = lambda w: acc[:, bass.ds(w, 1), 0:D].rearrange("p o c -> p (o c)")

            @block.sync
            def _(sp):
                sp.dma_start(gb[:, :], gbias.partition_broadcast(P)).then_inc(small_loaded, 16)
                sp.dma_start(brb[:, :], br.partition_broadcast(P)).then_inc(small_loaded, 16)
                sp.dma_start(wr[:, :, :], Wr.rearrange("(k p) e -> p k e", p=P)).then_inc(small_loaded, 16)
                sp.wait_ge(pad_zeroed, 1)
                load_nodes(sp, x_loaded)

            @block.gpsimd
            def _(pool):
                pool.wait_ge(small_loaded, 48)

                def add_bias(w):
                    pool.wait_ge(added, w + 1)
                    nc.gpsimd.tensor_tensor(row(node_rows, w), row(node_rows, w), gb[:, :], ALU.add).then_inc(biased, 1)

                each_window(pool, add_bias)
                pool.wait_ge(pos_ready, 1)
                for w in range(NW):
                    n = LAST if w == NW - 1 else P
                    pool.wait_ge(xn_ready, w + 1)
                    for k in range(2):
                        pool.indirect_dma_start(xs, bass.IndirectOffsetOnAxis(ap=pos[k][0:n, w:w + 1], axis=0),
                                                xn[0:n, w, :], None).then_inc(scattered, 16)
                pool.wait_ge(scattered, 16 * 2 * NW)

            @block.scalar
            def _(act):
                act.wait_ge(var_ready[0], 1)
                nc.scalar.activation(rstd[:, 0, :], mv[:, 0, :, 1], ACT.Sqrt, bias=eps_col[:, 0:1]).then_inc(std_ready[0], 1)

                def copy_xT(m, b, n=2):
                    act.wait_ge(xT_made, m + 1)
                    nc.scalar.activation(xT[:, b, 0:n * D], xT_ps[:, b, 0:n * D], ACT.Copy).then_inc(xT_copied, 1)

                with act.Fori(0, PAIRED // 2) as i:
                    for b in range(2):
                        copy_xT(2 * i + b, b)
                copy_xT(PAIRED, 0, 1)
                act.wait_ge(gate_in, 1)
                nc.scalar.activation(gate[:, :], diff[:, :], ACT.Exp).then_inc(gate_made, 1)
                act.wait_ge(var_ready[1], 1)
                nc.scalar.activation(rstd[:, 1, :], mv[:, 1, :, 1], ACT.Sqrt, bias=eps_col[:, 0:1]).then_inc(std_ready[1], 1)

            @block.tensor
            def _(pe):
                def transpose(m, b, n=2):
                    pe.wait_ge(xt_ready, m + 1)
                    for u in range(n):
                        for k in range(KD):
                            c = (u * KD + k) * P
                            last = nc.tensor.transpose(xT_ps[:, b, c:c + P], xt_st[:, b, u, k * P:(k + 1) * P], ident[:, :])
                    last.then_inc(xT_made, 1)

                def product(m, b, n=2, reused=True):
                    pe.wait_ge(xT_copied, m + 1)
                    if reused:
                        pe.wait_ge(lg_taken, m - 1)
                    for u in range(n):
                        for k in range(KD):
                            c = (u * KD + k) * P
                            last = nc.tensor.matmul(lg_ps[:, b, u * NE:(u + 1) * NE], xT[:, b, c:c + P], wr[:, k, :],
                                                    start=(k == 0), stop=(k == KD - 1))
                    last.then_inc(lg_made, 1)

                pe.wait_ge(small_loaded, 48)
                transpose(0, 0)
                transpose(1, 1)
                product(0, 0, reused=False)
                transpose(2, 0)
                product(1, 1, reused=False)
                with pe.Fori(1, PAIRED // 2 - 1) as i:
                    for b in range(2):
                        transpose(2 * i + b + 1, 1 - b)
                        product(2 * i + b, b)
                transpose(PAIRED - 1, 1)
                product(PAIRED - 2, 0)
                transpose(PAIRED, 0, 1)
                product(PAIRED - 1, 1)
                product(PAIRED, 0, 1)
                pe.wait_ge(both_made, 1)
                flat = both[:, :, :].rearrange("p w e -> p (w e)")
                nc.tensor.matmul(rank_ps[:, 0:NW * NE], before[:, :], flat, start=True, stop=True)
                nc.tensor.matmul(total_ps[:, 0:NW * NE], ones[:, :], flat, start=True, stop=True).then_inc(ranked, 1)

            @block.vector
            def _(dve):
                link = chain(dve, seq)
                nc.vector.memset(node_rows[:, NW - 1, :], 0.0).then_inc(pad_zeroed, 1)
                nc.vector.memset(zero[:, :], 0.0)
                link(nc.vector.reciprocal(rden[:, :, :], acc[:, 0:NW, :].rearrange("p w (h c) -> p w h c", h=H)[:, :, :, HD]))
                each_window(dve, lambda w: nc.vector.tensor_tensor(
                    acc_rows(w), acc_rows(w), rden[:, bass.ds(w, 1), :].rearrange("p o h -> p (o h)").unsqueeze(2)
                    .to_broadcast([P, H, HD]), ALU.mult))
                link(nc.vector.memset(tick[:, :], 0.0))

                def add_x(w):
                    r4 = row(node_rows, w).rearrange("p (h c) -> p h c", h=H)
                    nc.vector.tensor_tensor(r4, r4, acc_rows(w), ALU.add).then_inc(added, 1)

                for g in range(NG + 1):
                    dve.wait_ge(x_loaded[g], 16)
                    each_window(dve, add_x, g * GW, min(GW, NW - g * GW))

                def row_statistics(w):
                    dve.wait_ge(biased, w + 1)
                    nc.vector.bn_stats(row(stat, w), row(node_rows, w))

                def find_moments(v):
                    link(nc.vector.memset(tick[:, :], 0.0))
                    moments(link, mv[:, v, :, 0], mv[:, v, :, 1], stat, mtmp).then_inc(var_ready[v], 1)

                def find_scale(v):
                    dve.wait_ge(std_ready[v], 1)
                    link(nc.vector.reciprocal(rstd[:, v, :], rstd[:, v, :]))

                def scaled(out_ap, in_ap, v, w):
                    return nc.vector.tensor_scalar(out_ap, in_ap, mv[:, v, bass.ds(w, 1), 0], rstd[:, v, bass.ds(w, 1)],
                                                   ALU.subtract, ALU.mult)

                each_window(dve, row_statistics)
                find_moments(0)
                find_scale(0)

                def take_xt(m, b, n=2, reused=True):
                    if reused:
                        dve.wait_ge(xT_made, m - 1)
                    for u in range(n):
                        last = scaled(xt_st[:, b, u, :], row(node_rows, 2 * m + u), 0, 2 * m + u)
                    last.then_inc(xt_ready, 1)
                    for u in range(n):
                        scaled(xt_row(2 * m + u), row(node_rows, 2 * m + u), 0, 2 * m + u)

                def take_logits(m, b, n=2, after=2):
                    dve.wait_ge(xt_ready, m + after)
                    for u in range(n):
                        nc.vector.bn_stats(row(stat, 2 * m + u), xt_row(2 * m + u))
                    dve.wait_ge(lg_made, m + 1)
                    nc.vector.tensor_tensor(logit[:, bass.ds(2 * m, n), :], lg_ps[:, b, 0:n * NE].rearrange("p (u e) -> p u e", u=n),
                                            brb[:, :].unsqueeze(1).to_broadcast([P, n, NE]), ALU.add).then_inc(lg_taken, 1)

                dve.wait_ge(small_loaded, 48)
                take_xt(0, 0, reused=False)
                take_xt(1, 1, reused=False)
                with dve.Fori(1, PAIRED // 2) as i:
                    for b in range(2):
                        take_xt(2 * i + b, b)
                        take_logits(2 * i + b - 2, b)
                take_xt(PAIRED, 0, 1)
                take_logits(PAIRED - 2, 0)
                take_logits(PAIRED - 1, 1)
                link(nc.vector.memset(tick[:, :], 0.0))
                take_logits(PAIRED, 0, 1, after=1)
                find_moments(1)

                of_rows = lambda a: a.unsqueeze(2).to_broadcast([P, NW, NE])
                nc.vector.tensor_scalar(real[:, :], iota_col[:, :], float(LAST), None, ALU.is_lt)
                link(nc.vector.tensor_scalar(number[:, :], iota_row[:, 0:NE], -float(NE), None, ALU.add))
                numbers = number[:, :].unsqueeze(1).to_broadcast([P, NW, NE])
                left = logit
                for k in range(2):
                    link(nc.vector.tensor_reduce(top[:, k, :], left[:, :, :], X, ALU.max))
                    link(nc.vector.tensor_tensor(equal[:, :, :], left[:, :, :], of_rows(top[:, k, :]), ALU.is_equal))
                    link(nc.vector.tensor_tensor(equal[:, :, :], equal[:, :, :], numbers, ALU.mult))
                    link(nc.vector.tensor_reduce(chosen[:, :], equal[:, :, :], X, ALU.min))
                    link(nc.vector.tensor_tensor(pick[k][:, :, :], numbers, of_rows(chosen[:, :]), ALU.is_equal))
                    if k == 0:
                        link(nc.vector.scalar_tensor_tensor(rest[:, :, :], pick[0][:, :, :], -BIG, logit[:, :, :], ALU.mult, ALU.add))
                        left = rest
                nc.vector.tensor_tensor(diff[:, :], top[:, 1, :], top[:, 0, :], ALU.subtract).then_inc(gate_in, 1)
                for k in range(2):
                    last = nc.vector.tensor_scalar(pick[k][:, NW - 1, :], pick[k][:, NW - 1, :], real[:, 0:1], None, ALU.mult)
                link(last)
                nc.vector.tensor_tensor(both[:, :, :], pick[0][:, :, :], pick[1][:, :, :], ALU.add).then_inc(both_made, 1)
                dve.wait_ge(gate_made, 1)
                link(nc.vector.tensor_scalar(gate_d[:, :], gate[:, :], 1.0, None, ALU.add))
                link(nc.vector.reciprocal(wt[0][:, :], gate_d[:, :]))
                nc.vector.tensor_tensor(wt[1][:, :], gate[:, :], wt[0][:, :], ALU.mult)
                dve.wait_ge(ranked, 1)
                link(nc.vector.tensor_copy(total[:, :, :].rearrange("p w e -> p (w e)"), total_ps[:, 0:NW * NE]))
                for e in range(NE):
                    last = nc.vector.tensor_tensor_scan(upto[:, :, e], total[:, :, e], zero[:, :], 0.0, ALU.add, ALU.add)
                link(last)
                link(nc.vector.tensor_scalar(need_i[:, :], upto[:, NW - 1, :], float(TOK - 1), None, ALU.add))
                link(nc.vector.tensor_scalar(need_i[:, :], need_i[:, :], TOK.bit_length() - 1, None, ALU.arith_shift_right))
                link(nc.vector.tensor_copy(need[:, :], need_i[:, :]))
                link(nc.vector.tensor_tensor_scan(need_c[:, :], need[:, :], zero[:, 0:NE], 0.0, ALU.add, ALU.add))
                link(nc.vector.tensor_tensor(slot0[:, :], need_c[:, :], need[:, :], ALU.subtract))
                link(nc.vector.tensor_tensor(owner[:, :, :], iota_row[0:1, 0:SLOTS].unsqueeze(2).to_broadcast([1, SLOTS, NE]),
                                             slot0[0:1, :].unsqueeze(1).to_broadcast([1, SLOTS, NE]), ALU.is_ge))
                link(nc.vector.tensor_reduce(owner_s[:, :], owner[:, :, :], X, ALU.add))
                nc.vector.tensor_scalar(slot_e[:, :], owner_s[:, :], -1.0, None, ALU.add)
                link(nc.vector.tensor_tensor(place[:, :, :], upto[:, :, :], total[:, :, :], ALU.subtract))
                link(nc.vector.tensor_tensor(place[:, :, :], place[:, :, :],
                                             rank_ps[:, 0:NW * NE].rearrange("p (w e) -> p w e", e=NE), ALU.add))
                link(nc.vector.tensor_scalar(slot0[:, :], slot0[:, :], float(TOK), None, ALU.mult))
                link(nc.vector.tensor_tensor(place[:, :, :], place[:, :, :],
                                             slot0[:, :].unsqueeze(1).to_broadcast([P, NW, NE]), ALU.add))
                for k in range(2):
                    link(nc.vector.tensor_tensor(placed[:, :, :], place[:, :, :], pick[k][:, :, :], ALU.mult))
                    link(nc.vector.tensor_reduce(posf[:, :], placed[:, :, :], X, ALU.add))
                    link(nc.vector.tensor_copy(pos[k][:, :], posf[:, :]))
                nc.vector.memset(tick[:, :], 0.0).then_inc(pos_ready, 1)

                find_scale(1)
                each_window(dve, lambda w: scaled(row(xn, w), xt_row(w), 1, w).then_inc(xn_ready, 1))

        until_experts.close()
        with ExitStack() as st:
            sb, ps, sem = allot(st)
            NT = TOK // P
            NPRM = FC + 2 * KD
            FR = mybir.dt.float32r
            w1_raw = sb("w1_raw", [P, KD, FH])
            w2_raw = sb("w2_raw", [P, FC, D])
            w1_top = sb("w1_top", [P, 2, KD, FH], FR)
            w1_rest = sb("w1_rest", [P, 2, KD, FH], FR)
            w2_top = sb("w2_top", [P, 2, FC, D], FR)
            w2_rest = sb("w2_rest", [P, 2, FC, D], FR)
            prm_sb = sb("prm_sb", [P, 2, NPRM])
            b2_sb = sb("b2_sb", [P, 2, D])
            xin = sb("xin", [P, 2, NT, D])
            xe = sb("xe", [P, KD, TOK])
            xe_top = sb("xe_top", [P, KD, TOK], FR)
            xe_rest = sb("xe_rest", [P, KD, TOK], FR)
            hid = sb("hid", [P, 2, 2, TOK])
            hid_top = sb("hid_top", [P, 2, FC, TOK], FR)
            hid_rest = sb("hid_rest", [P, 2, FC, TOK], FR)
            yo = sb("yo", [P, 2, NT, D])
            xT_ps = ps("xeT_ps", [P, 2, 512])
            hid_ps = ps("hid_ps", [P, 4, 512])
            y_ps = ps("y_ps", [P, 2, 512])
            x_loaded = [sem(f"slot_x_loaded{b}") for b in range(2)]
            w1_loaded = [sem(f"w1_loaded{b}") for b in range(2)]
            w2_loaded = [sem(f"w2_loaded{b}") for b in range(2)]
            stored = [sem(f"y_stored{b}") for b in range(2)]
            w1_split = [sem(f"w1_split{b}") for b in range(2)]
            w2_cut = [sem(f"w2_cut{b}") for b in range(2)]
            w2_split = [sem(f"w2_split{b}") for b in range(2)]
            xT_made = sem("xeT_made")
            xe_raw = sem("xe_raw")
            xe_ready = sem("xe_ready")
            hid_made = sem("hid_made")
            gelu_done = sem("gelu_done")
            hid_cut = sem("hid_cut")
            hid_split = sem("hid_split")
            y_made = sem("y_made")
            y_taken = sem("y_taken")
            sp_waited = sem("sp_waited")
            pool_waited = sem("pool_waited")
            block = st.enter_context(nc.Block())
            HALF = FC // 2

            def slots(eng, slot):
                for b in range(2):
                    slot(b, 0, b, True)
                with eng.Fori(1, SLOTS // 2) as i:
                    for b in range(2):
                        slot(2 * i + b, i, b, False)

            def experts_of(eng, q, new):
                return [eng.value_load(slot_e[0:1, bass.ds(n, 1)], min_val=0, max_val=NE - 1)
                        for n in ([q] if new else [q, q - 2])]

            def on_new_expert(eng, experts, fresh, same):
                if len(experts) == 1:
                    fresh()
                    return
                with eng.If(experts[0] != experts[1]):
                    fresh()
                with eng.If(experts[0] == experts[1]):
                    same()

            def cut_top(top, raw):
                return nc.vector.tensor_copy(top, raw)

            def cut_rest(eng, rest, raw, top):
                return eng.tensor_tensor(rest, raw, top.bitcast(F32), ALU.subtract)

            @block.sync
            def _(sp):
                def slot(q, i, b, new):
                    experts = experts_of(sp, q, new)
                    mine = experts[0]
                    if not new:
                        sp.wait_ge(xT_made, q - 1)
                    sp.dma_start(xin[:, b, :, :], xs[bass.ds(q * TOK, TOK), :].rearrange("(t p) d -> p t d", p=P)).then_inc(x_loaded[b], 16)
                    if not new:
                        sp.wait_ge(y_taken, q - 1)
                    sp.dma_start(prm_sb[:, b, :], prm[bass.ds(mine, 1)].rearrange("o p c -> p (o c)")).then_inc(x_loaded[b], 16)
                    sp.dma_start(b2_sb[:, b, :], b2[bass.ds(mine, 1)].rearrange("o d -> (o d)").partition_broadcast(P)).then_inc(x_loaded[b], 16)

                    if not (isinstance(q, int) and q == 0):
                        sp.wait_ge(w1_split[1 - b], 2 * (i + b))
                        sp.wait_ge(w2_split[1 - b], i + b)
                        sp.sem_inc(sp_waited, 1)

                    def load_expert():
                        one = lambda a: a[bass.ds(mine, 1)]
                        sp.dma_start(w1_raw[:, :, :], one(W1).rearrange("o (k p) f -> p (o k) f", p=P)).then_inc(w1_loaded[b], 16)
                        sp.dma_start(w2_raw[:, :, :], one(W2).rearrange("o (c p) d -> p (o c) d", p=P)).then_inc(w2_loaded[b], 16)

                    def keep_expert():
                        sp.sem_inc(w1_loaded[b], 16)
                        sp.sem_inc(w2_loaded[b], 16)

                    on_new_expert(sp, experts, load_expert, keep_expert)

                slots(sp, slot)

            @block.gpsimd
            def _(pool):
                def split_w2(q, i, b, new):
                    experts = experts_of(pool, q, new)
                    pool.wait_ge(w2_cut[b], i + 1)
                    pool.sem_inc(pool_waited, 1)

                    def fresh():
                        cut_rest(nc.gpsimd, w2_rest[:, b, :, :], w2_raw[:, :, :], w2_top[:, b, :, :]).then_inc(w2_split[b], 1)

                    on_new_expert(pool, experts, fresh, lambda: pool.sem_inc(w2_split[b], 1))

                def store_y(q, b):
                    pool.wait_ge(y_taken, q + 1)
                    pool.dma_start(ys[bass.ds(q * TOK, TOK), :].rearrange("(t p) d -> p t d", p=P), yo[:, b, :, :]).then_inc(stored[b], 16)

                split_w2(0, 0, 0, True)
                split_w2(1, 0, 1, True)
                store_y(0, 0)
                with pool.Fori(1, SLOTS // 2) as i:
                    split_w2(2 * i, i, 0, False)
                    store_y(2 * i - 1, 1)
                    split_w2(2 * i + 1, i, 1, False)
                    store_y(2 * i, 0)
                store_y(SLOTS - 1, 1)
                for b in range(2):
                    pool.wait_ge(stored[b], 16 * (SLOTS // 2))

            @block.scalar
            def _(act):
                def slot(q, i, b, new):
                    for c in range(FC):
                        if c % 2 == 0:
                            act.wait_ge(hid_made, HALF * q + c // 2 + 1)
                            if not (isinstance(q, int) and q == 0 and c < 4):
                                act.wait_ge(hid_split, HALF * q + c // 2 - 1)
                        nc.scalar.activation(hid[:, (c // 2) % 2, c % 2, :], hid_ps[:, c // 2, (c % 2) * TOK:(c % 2 + 1) * TOK], ACT.Gelu,
                                             bias=prm_sb[:, b, c:c + 1]).then_inc(gelu_done, 1)

                slots(act, slot)

            @block.tensor
            def _(pe):
                def product(out_ap, a, b, first, last):
                    (a_top, a_rest), (b_top, b_rest) = a, b
                    nc.tensor.matmul(out_ap, a_top, b_top, start=first, stop=False)
                    nc.tensor.matmul(out_ap, a_rest, b_top, start=False, stop=False)
                    return nc.tensor.matmul(out_ap, a_top, b_rest, start=False, stop=last)

                def transpose(q, i, b):
                    pe.wait_ge(x_loaded[b], 48 * (i + 1))
                    for t in range(NT):
                        for k in range(KD):
                            last = nc.tensor.transpose(xT_ps[:, b, k * TOK + t * P:k * TOK + (t + 1) * P],
                                                       xin[:, b, t, k * P:(k + 1) * P], ident[:, :])
                    last.then_inc(xT_made, 1)

                def slot(q, i, b, new, following=True):
                    pe.wait_ge(xe_ready, q + 1)
                    pe.wait_ge(w1_split[b], 2 * i + 2)
                    for c in range(FC):
                        if c % 2 == 0 and not (isinstance(q, int) and q == 0):
                            pe.wait_ge(gelu_done, FC * q - FC + c + 2)
                        for k in range(KD):
                            chunk = slice(c * P, (c + 1) * P)
                            last = product(hid_ps[:, c // 2, (c % 2) * TOK:(c % 2 + 1) * TOK],
                                           (w1_top[:, b, k, chunk], w1_rest[:, b, k, chunk]),
                                           (xe_top[:, k, :], xe_rest[:, k, :]), k == 0, k == KD - 1)
                        if c % 2:
                            last.then_inc(hid_made, 1)
                    if following:
                        transpose(q + 1, i + b, 1 - b)
                    pe.wait_ge(w2_split[b], i + 1)
                    if not new:
                        pe.wait_ge(y_taken, q - 1)
                    for t in range(NT):
                        for c in range(FC):
                            if t == 0 and c % 2 == 0:
                                pe.wait_ge(hid_split, HALF * q + c // 2 + 1)
                            toks = slice(t * P, (t + 1) * P)
                            last = product(y_ps[:, b, t * D:(t + 1) * D],
                                           (hid_top[:, b, c, toks], hid_rest[:, b, c, toks]),
                                           (w2_top[:, b, c, :], w2_rest[:, b, c, :]), c == 0, c == FC - 1)
                    last.then_inc(y_made, 1)

                transpose(0, 0, 0)
                slot(0, 0, 0, True)
                slot(1, 0, 1, True)
                with pe.Fori(1, SLOTS // 2 - 1) as i:
                    for b in range(2):
                        slot(2 * i + b, i, b, False)
                i = SLOTS // 2 - 1
                slot(2 * i, i, 0, False)
                slot(2 * i + 1, i, 1, False, following=False)

            @block.vector
            def _(dve):
                def take_x(q, b):
                    dve.wait_ge(xT_made, q + 1)
                    for k in range(KD):
                        last = nc.vector.tensor_scalar(xe[:, k, :], xT_ps[:, b, k * TOK:(k + 1) * TOK],
                                                       prm_sb[:, b, FC + k:FC + k + 1], prm_sb[:, b, FC + KD + k:FC + KD + k + 1],
                                                       ALU.mult, ALU.add)
                    last.then_inc(xe_raw, 1)
                    dve.wait_ge(xe_raw, 2 * q + 1)
                    cut_top(xe_top[:, :, :], xe[:, :, :]).then_inc(xe_raw, 1)
                    dve.wait_ge(xe_raw, 2 * q + 2)
                    cut_rest(nc.vector, xe_rest[:, :, :], xe[:, :, :], xe_top[:, :, :]).then_inc(xe_ready, 1)

                def split_weights(q, i, b, new):
                    def fresh():
                        dve.wait_ge(w1_loaded[b], 16 * (i + 1))
                        cut_top(w1_top[:, b, :, :], w1_raw[:, :, :]).then_inc(w1_split[b], 1)
                        dve.wait_ge(w1_split[b], 2 * i + 1)
                        cut_rest(nc.vector, w1_rest[:, b, :, :], w1_raw[:, :, :], w1_top[:, b, :, :]).then_inc(w1_split[b], 1)
                        dve.wait_ge(w2_loaded[b], 16 * (i + 1))
                        cut_top(w2_top[:, b, :, :], w2_raw[:, :, :]).then_inc(w2_cut[b], 1)

                    def same():
                        dve.wait_ge(w1_loaded[b], 16 * (i + 1))
                        dve.sem_inc(w1_split[b], 2)
                        dve.wait_ge(w2_loaded[b], 16 * (i + 1))
                        dve.sem_inc(w2_cut[b], 1)

                    on_new_expert(dve, experts_of(dve, q, new), fresh, same)

                def split_hidden(q, b):
                    for g in range(HALF):
                        n = HALF * q + g + 1
                        dve.wait_ge(gelu_done, 2 * n)
                        pair = slice(2 * g, 2 * g + 2)
                        raw = hid[:, g % 2, :, :]
                        cut_top(hid_top[:, b, pair, :], raw).then_inc(hid_cut, 1)
                        dve.wait_ge(hid_cut, n)
                        cut_rest(nc.vector, hid_rest[:, b, pair, :], raw, hid_top[:, b, pair, :]).then_inc(hid_split, 1)

                def take_y(q, i, b, new):
                    dve.wait_ge(y_made, q + 1)
                    if not new:
                        dve.wait_ge(stored[b], 16 * i)
                    nc.vector.tensor_tensor(yo[:, b, :, :], y_ps[:, b, :].rearrange("p (t d) -> p t d", t=NT),
                                            b2_sb[:, b, :].unsqueeze(1).to_broadcast([P, NT, D]), ALU.add).then_inc(y_taken, 1)

                def slot(q, i, b, new, following=True, early=False):
                    split_hidden(q, b)
                    if following:
                        take_x(q + 1, 1 - b)
                        if not early:
                            split_weights(q + 1, i + b, 1 - b, False)
                    take_y(q, i, b, new)

                split_weights(0, 0, 0, True)
                take_x(0, 0)
                split_weights(1, 0, 1, True)
                slot(0, 0, 0, True, early=True)
                slot(1, 0, 1, True)
                with dve.Fori(1, SLOTS // 2 - 1) as i:
                    for b in range(2):
                        slot(2 * i + b, i, b, False)
                i = SLOTS // 2 - 1
                slot(2 * i, i, 0, False)
                slot(2 * i + 1, i, 1, False, following=False)

        with ExitStack() as st:
            sb, ps, sem = allot(st)
            CR = 4
            y_g = sb("y_g", [P, CR, 2, D])
            gathered = [sem(f"gathered{r}") for r in range(CR)]
            first_added = sem("first_added")
            done = sem("done")
            stored = sem("out_stored")
            block = st.enter_context(nc.Block())
            rows = lambda w: LAST if w == NW - 1 else P

            @block.gpsimd
            def _(pool):
                for w in range(NW):
                    if w >= CR:
                        pool.wait_ge(done, w - CR + 1)
                    for k in range(2):
                        pool.indirect_dma_start(y_g[0:rows(w), w % CR, k, :], None, ys,
                                                bass.IndirectOffsetOnAxis(ap=pos[k][0:rows(w), w:w + 1], axis=0)
                                                ).then_inc(gathered[w % CR], 16)

            @block.vector
            def _(dve):
                def add(w):
                    n = rows(w)
                    dve.wait_ge(gathered[w % CR], 32 * (w // CR + 1))
                    x1 = node_rows[0:n, w, :]
                    nc.vector.scalar_tensor_tensor(x1, y_g[0:n, w % CR, 0, :], wt[0][0:n, w:w + 1], x1,
                                                   ALU.mult, ALU.add).then_inc(first_added, 1)
                    dve.wait_ge(first_added, w + 1)
                    nc.vector.scalar_tensor_tensor(x1, y_g[0:n, w % CR, 1, :], wt[1][0:n, w:w + 1], x1,
                                                   ALU.mult, ALU.add).then_inc(done, 1)

                for w in range(NW):
                    add(w)

            @block.sync
            def _(sp):
                for g in range(NG):
                    sp.wait_ge(done, (g + 1) * GW)
                    sp.dma_start(out[g * GW * P:(g + 1) * GW * P, :].rearrange("(w p) d -> p w d", p=P),
                                 node_rows[:, g * GW:(g + 1) * GW, :]).then_inc(stored, 16)
                sp.wait_ge(done, NW)
                sp.dma_start(out[(NW - 1) * P:N, :], node_rows[0:LAST, NW - 1, :]).then_inc(stored, 16)
                sp.wait_ge(stored, 16 * (NG + 1))


_INS = ['x', 'src', 'dst', 'L0_gnn_W', 'L0_gnn_att_src', 'L0_gnn_att_dst', 'L0_gnn_bias', 'L0_ffn_Wr', 'L0_ffn_br',
        'L0_ffn_ln_g', 'L0_ffn_ln_b', 'L0_ffn_W1', 'L0_ffn_b1', 'L0_ffn_W2', 'L0_ffn_b2']


def kernel(**inputs):
    import numpy as _np
    import concourse.bacc as _bacc
    from concourse import mybir as _mybir
    from concourse.bass_utils import run_bass_kernel_spmd as _run

    nc = _bacc.Bacc("TRN2", target_bir_lowering=False, num_devices=1)
    arrays, args = {}, []
    for name in _INS:
        a = _np.ascontiguousarray(inputs[name])
        arrays[f"in_{name}"] = a
        args.append(nc.dram_tensor(f"in_{name}", a.shape, _mybir.dt.from_np(a.dtype), kind="ExternalInput").ap())
    out = nc.dram_tensor("out_x", inputs["x"].shape, _mybir.dt.float32, kind="ExternalOutput").ap()
    gat_moe(nc, *args, out)
    r = _run(nc, [arrays], core_ids=[0])
    return r.results[0]["out_x"]
```
